# Optimizing a Trainium2 kernel written in Bass

```python
import numpy as np
import jax
import jax.numpy as jnp

def _softmax(x, axis=-1):
    return jax.nn.softmax(x, axis=axis)

def _gelu(x):
    return jax.nn.gelu(x, approximate=True)

def _silu(x):
    return jax.nn.silu(x)

def _sigmoid(x):
    return jax.nn.sigmoid(x)

def _layernorm(x, axis=-1, eps=1e-05):
    m = jnp.mean(x, axis=axis, keepdims=True)
    v = jnp.var(x, axis=axis, keepdims=True)
    return (x - m) / jnp.sqrt(v + eps)

def _scatter_add(tgt, idx, src, axis=0):
    return tgt.at[idx].add(src)

def _segment_sum(src, seg, n):
    return jax.ops.segment_sum(src, seg, n)
kernel_name = 'mk_gnn_preln_d4_gnn_r64_3f06eb'

def setup_inputs(seed: int=0):
    np.random.seed(seed)
    _w = jnp.asarray

    def _rec_inputs():
        import jax
        import jax.numpy as jnp
        _gk = jax.random.key(seed)
        x = -0.000202 + 1 * jax.random.normal(jax.random.fold_in(_gk, 1), (100000, 64), jnp.float32)
        src = jax.random.randint(jax.random.fold_in(_gk, 2), (50000,), 0, 100000, jnp.int32)
        dst = jax.random.randint(jax.random.fold_in(_gk, 3), (50000,), 0, 100000, jnp.int32)
        _o = jnp.argsort(dst, stable=True)
        src = src[_o]
        dst = dst[_o]
        return (x, src, dst)
    x, src, dst = _rec_inputs()

    def _L0_gnn_setup():
        import jax, jax.numpy as jnp
        import numpy as np
        N_NODES = 100000
        N_EDGES = 25000
        IN_C, HID_C, OUT_C = (64, 64, 64)

        def _glorot(k, shape):
            lim = np.sqrt(6.0 / (shape[0] + shape[1]))
            return jax.random.uniform(k, shape, jnp.float32, -lim, lim)

        def gcn_conv(x, edge_index, W, b, num_nodes):
            loop = jnp.arange(num_nodes, dtype=edge_index.dtype)
            row = jnp.concatenate([edge_index[0], loop])
            col = jnp.concatenate([edge_index[1], loop])
            deg = jnp.zeros((num_nodes,), x.dtype).at[col].add(jnp.float32(1.0))
            dinv = jnp.where(deg > 0, jax.lax.rsqrt(deg), 0.0)
            norm = dinv[row] * dinv[col]
            h = x @ W.T
            msg = norm[:, None] * h[row]
            out = jax.ops.segment_sum(msg, col, num_segments=num_nodes)
            return out + b
        key = jax.random.key(seed)
        ks = jax.random.split(key, 6)
        x = jax.random.normal(ks[0], (N_NODES, IN_C), jnp.float32)
        edge_index = jax.random.randint(ks[1], (2, N_EDGES), 0, N_NODES, jnp.int32)
        W1 = _glorot(ks[2], (HID_C, IN_C))
        b1 = jnp.zeros((HID_C,), jnp.float32)
        W2 = _glorot(ks[3], (OUT_C, HID_C))
        b2 = jnp.zeros((OUT_C,), jnp.float32)
        Wg = _glorot(ks[4], (OUT_C, OUT_C + IN_C))
        bg = jnp.zeros((OUT_C,), jnp.float32)
        return {'x': x, 'edge_index': edge_index, 'W1': W1, 'b1': b1, 'W2': W2, 'b2': b2, 'Wg': Wg, 'bg': bg}
    _L0_gnn_all = _L0_gnn_setup()
    _L0_gnn_in = {k: v for k, v in _L0_gnn_all.items() if k in ('W1', 'b1', 'W2', 'b2', 'Wg', 'bg')}
    del _L0_gnn_all

    def _L1_gnn_setup():
        import jax, jax.numpy as jnp
        import numpy as np
        N_NODES = 100000
        N_EDGES = 50000
        D = 64

        def _gcn_conv(x, W, b, src, dst, n):
            deg = jax.ops.segment_sum(jnp.ones_like(src, dtype=x.dtype), dst, num_segments=n)
            dinv = jnp.where(deg > 0, jax.lax.rsqrt(deg), 0.0)
            norm = dinv[src] * dinv[dst]
            h = x @ W
            agg = jax.ops.segment_sum(h[src] * norm[:, None], dst, num_segments=n)
            return agg + b
        key = jax.random.key(seed)
        k1, k2, k3, k4 = jax.random.split(key, 4)
        x = jax.random.normal(k1, (N_NODES, D), dtype=jnp.float32)
        edge_index = jax.random.randint(k2, (2, N_EDGES), 0, N_NODES, dtype=jnp.int64)
        scale = 1.0 / np.sqrt(D)
        W1 = jax.random.normal(k3, (D, D), dtype=jnp.float32) * scale
        W2 = jax.random.normal(k4, (D, D), dtype=jnp.float32) * scale
        b1 = jnp.zeros((D,), dtype=jnp.float32)
        b2 = jnp.zeros((D,), dtype=jnp.float32)
        return {'x': x, 'edge_index': edge_index, 'W1': W1, 'b1': b1, 'W2': W2, 'b2': b2}
    _L1_gnn_all = _L1_gnn_setup()
    _L1_gnn_in = {k: v for k, v in _L1_gnn_all.items() if k in ('W1', 'b1', 'W2', 'b2')}
    del _L1_gnn_all

    def _L2_gnn_setup():
        import jax, jax.numpy as jnp
        import numpy as np
        N_NODES = 100000
        N_EDGES = 12500
        D = 64
        H = 4
        key = jax.random.key(seed)
        k1, k2, k3, k4, k5 = jax.random.split(key, 5)
        xavier = float(np.sqrt(2.0 / (D + D)))
        all_embeddings = jax.random.normal(k1, (N_NODES, D), dtype=jnp.float32)
        Wq = jax.random.normal(k2, (D, D), dtype=jnp.float32) * xavier
        Wk = jax.random.normal(k3, (D, D), dtype=jnp.float32) * xavier
        Wv = jax.random.normal(k4, (D, D), dtype=jnp.float32) * xavier
        edge_index = jax.random.randint(k5, (2, N_EDGES), 0, N_NODES, dtype=jnp.int32)
        return {'all_embeddings': all_embeddings, 'Wq': Wq, 'Wk': Wk, 'Wv': Wv, 'edge_index': edge_index}
    _L2_gnn_all = _L2_gnn_setup()
    _L2_gnn_in = {k: v for k, v in _L2_gnn_all.items() if k in ('Wq', 'Wk', 'Wv')}
    del _L2_gnn_all

    def _L3_gnn_setup():
        import jax, jax.numpy as jnp
        import numpy as np
        N = 100000
        E = 12500
        D = 64
        NUM_ROUNDS = 4
        EPS = 1e-05
        key = jax.random.key(seed)
        k0, k1, k2 = jax.random.split(key, 3)
        x = jax.random.normal(k0, (N, D), dtype=jnp.float32)
        edge_index = jax.random.randint(k1, (2, E), 0, N, dtype=jnp.int32)
        W = jax.random.normal(k2, (D, D), dtype=jnp.float32) * (1.0 / np.sqrt(D))
        b = jnp.zeros((D,), dtype=jnp.float32)
        gamma = jnp.ones((D,), dtype=jnp.float32)
        beta = jnp.zeros((D,), dtype=jnp.float32)
        return {'x': x, 'edge_index': edge_index, 'W': W, 'b': b, 'gamma': gamma, 'beta': beta, 'num_rounds': NUM_ROUNDS}
    _L3_gnn_all = _L3_gnn_setup()
    _L3_gnn_in = {k: v for k, v in _L3_gnn_all.items() if k in ('W', 'b', 'gamma', 'beta')}
    del _L3_gnn_all
    return {'x': x, 'src': src, 'dst': dst, 'L0_gnn_W1': _L0_gnn_in['W1'], 'L0_gnn_b1': _L0_gnn_in['b1'], 'L0_gnn_W2': _L0_gnn_in['W2'], 'L0_gnn_b2': _L0_gnn_in['b2'], 'L0_gnn_Wg': _L0_gnn_in['Wg'], 'L0_gnn_bg': _L0_gnn_in['bg'], 'L1_gnn_W1': _L1_gnn_in['W1'], 'L1_gnn_b1': _L1_gnn_in['b1'], 'L1_gnn_W2': _L1_gnn_in['W2'], 'L1_gnn_b2': _L1_gnn_in['b2'], 'L2_gnn_Wq': _L2_gnn_in['Wq'], 'L2_gnn_Wk': _L2_gnn_in['Wk'], 'L2_gnn_Wv': _L2_gnn_in['Wv'], 'L3_gnn_W': _L3_gnn_in['W'], 'L3_gnn_b': _L3_gnn_in['b'], 'L3_gnn_gamma': _L3_gnn_in['gamma'], 'L3_gnn_beta': _L3_gnn_in['beta']}

def reference(x, src, dst, L0_gnn_W1, L0_gnn_b1, L0_gnn_W2, L0_gnn_b2, L0_gnn_Wg, L0_gnn_bg, L1_gnn_W1, L1_gnn_b1, L1_gnn_W2, L1_gnn_b2, L2_gnn_Wq, L2_gnn_Wk, L2_gnn_Wv, L3_gnn_W, L3_gnn_b, L3_gnn_gamma, L3_gnn_beta):
    import jax
    import jax.numpy as jnp

    def _L0_gnn_ref(x, W1, b1, W2, b2, Wg, bg, edge_index):
        import jax, jax.numpy as jnp
        import numpy as np
        N_NODES = 100000
        N_EDGES = 25000
        IN_C, HID_C, OUT_C = (64, 64, 64)

        def _glorot(k, shape):
            lim = np.sqrt(6.0 / (shape[0] + shape[1]))
            return jax.random.uniform(k, shape, jnp.float32, -lim, lim)

        def gcn_conv(x, edge_index, W, b, num_nodes):
            loop = jnp.arange(num_nodes, dtype=edge_index.dtype)
            row = jnp.concatenate([edge_index[0], loop])
            col = jnp.concatenate([edge_index[1], loop])
            deg = jnp.zeros((num_nodes,), x.dtype).at[col].add(jnp.float32(1.0))
            dinv = jnp.where(deg > 0, jax.lax.rsqrt(deg), 0.0)
            norm = dinv[row] * dinv[col]
            h = x @ W.T
            msg = norm[:, None] * h[row]
            out = jax.ops.segment_sum(msg, col, num_segments=num_nodes)
            return out + b
        n = x.shape[0]
        h = jax.nn.relu(gcn_conv(x, edge_index, W1, b1, n))
        h = jax.nn.relu(gcn_conv(h, edge_index, W2, b2, n))
        h = h + x
        gate = jax.nn.sigmoid(jnp.concatenate([h, x], axis=1) @ Wg.T + bg)
        return h * gate

    def _L1_gnn_ref(x, edge_index, W1, b1, W2, b2):
        import jax, jax.numpy as jnp
        import numpy as np
        N_NODES = 100000
        N_EDGES = 50000
        D = 64

        def _gcn_conv(x, W, b, src, dst, n):
            deg = jax.ops.segment_sum(jnp.ones_like(src, dtype=x.dtype), dst, num_segments=n)
            dinv = jnp.where(deg > 0, jax.lax.rsqrt(deg), 0.0)
            norm = dinv[src] * dinv[dst]
            h = x @ W
            agg = jax.ops.segment_sum(h[src] * norm[:, None], dst, num_segments=n)
            return agg + b
        n = x.shape[0]
        loops = jnp.arange(n, dtype=edge_index.dtype)
        src = jnp.concatenate([edge_index[0], loops])
        dst = jnp.concatenate([edge_index[1], loops])
        h = jax.nn.relu(_gcn_conv(x, W1, b1, src, dst, n))
        out = jax.nn.relu(_gcn_conv(h, W2, b2, src, dst, n))
        return out

    def _L2_gnn_ref(all_embeddings, Wq, Wk, Wv, edge_index):
        import jax, jax.numpy as jnp
        import numpy as np
        N_NODES = 100000
        N_EDGES = 12500
        D = 64
        H = 4
        rows, cols = (edge_index[0], edge_index[1])
        n_nodes = all_embeddings.shape[0]
        e = rows.shape[0]
        dh = D // H
        row_emb = all_embeddings[rows]
        col_emb = all_embeddings[cols]
        q = (row_emb @ Wq).reshape(e, H, dh)
        k = (col_emb @ Wk).reshape(e, H, dh)
        v = (col_emb @ Wv).reshape(e, H, dh)
        att = jnp.einsum('ehd,ehd->eh', q, k)
        att = jnp.clip(att, -10.0, 10.0)
        exp_att = jnp.exp(att)
        att_norm = jax.ops.segment_sum(exp_att, rows, num_segments=n_nodes)
        att = exp_att / (att_norm[rows] + 1e-08)
        out_e = (att[:, :, None] * v).reshape(e, D)
        out = jax.ops.segment_sum(out_e, rows, num_segments=n_nodes)
        return out

    def _L3_gnn_ref(x, edge_index, W, b, gamma, beta, num_rounds):
        import jax, jax.numpy as jnp
        import numpy as np
        N = 100000
        E = 12500
        D = 64
        NUM_ROUNDS = 4
        EPS = 1e-05
        n = x.shape[0]
        loops = jnp.arange(n, dtype=edge_index.dtype)
        src = jnp.concatenate([edge_index[0], loops])
        dst = jnp.concatenate([edge_index[1], loops])
        deg = jax.ops.segment_sum(jnp.ones_like(dst, dtype=x.dtype), dst, num_segments=n)
        dis = jnp.where(deg > 0, jax.lax.rsqrt(deg), 0.0)
        norm = dis[src] * dis[dst]
        for _ in range(num_rounds):
            h = x @ W
            msgs = h[src] * norm[:, None]
            agg = jax.ops.segment_sum(msgs, dst, num_segments=n) + b
            mu = agg.mean(axis=-1, keepdims=True)
            var = agg.var(axis=-1, keepdims=True)
            x = (agg - mu) * jax.lax.rsqrt(var + EPS) * gamma + beta
        return x
    edge_index = jnp.stack([src, dst])
    h = jnp.maximum(_layernorm(x, axis=-1), 0.0)
    x = x + _L0_gnn_ref(h, L0_gnn_W1, L0_gnn_b1, L0_gnn_W2, L0_gnn_b2, L0_gnn_Wg, L0_gnn_bg, edge_index)
    h = jnp.maximum(_layernorm(x, axis=-1), 0.0)
    x = x + _L1_gnn_ref(h, edge_index, L1_gnn_W1, L1_gnn_b1, L1_gnn_W2, L1_gnn_b2)
    h = jnp.maximum(_layernorm(x, axis=-1), 0.0)
    x = x + _L2_gnn_ref(h, L2_gnn_Wq, L2_gnn_Wk, L2_gnn_Wv, edge_index)
    h = jnp.maximum(_layernorm(x, axis=-1), 0.0)
    x = x + _L3_gnn_ref(h, edge_index, L3_gnn_W, L3_gnn_b, L3_gnn_gamma, L3_gnn_beta, 4)
    return x

_drawn_inputs = setup_inputs


def setup_inputs(seed=0):
    import zlib

    import numpy as np

    out = dict(_drawn_inputs(seed))
    spreads = {'L0_gnn_b1': (0.0, 0.436),
     'L0_gnn_b2': (0.0, 0.299),
     'L0_gnn_bg': (0.0, 0.515),
     'L1_gnn_b1': (0.0, 0.293),
     'L1_gnn_b2': (0.0, 0.1),
     'L3_gnn_b': (0.0, 0.1),
     'L3_gnn_gamma': (1.0, 0.2),
     'L3_gnn_beta': (0.0, 0.1)}
    factors = {}
    for name, (base, spread) in spreads.items():
        noise = np.random.default_rng([zlib.crc32(name.encode()), seed]).standard_normal(out[name].shape)
        drawn = base * np.exp(spread * noise) if base else spread * noise
        out[name] = jnp.asarray(drawn.astype(out[name].dtype))
    for name, factor in factors.items():
        out[name] = (out[name] * factor).astype(out[name].dtype)
    return out
```

```python
from contextlib import ExitStack

import concourse.bass as bass
from concourse import mybir

ALU = mybir.AluOpType
ACT = mybir.ActivationFunctionType
AX_X = mybir.AxisListType.X
F32 = mybir.dt.float32
BF16 = mybir.dt.bfloat16
I32 = mybir.dt.int32

P = 128
D = 64
HEADS = 4
DH = D // HEADS
GB = 8
N_NODES = 100000
N_EDGES = 50000
NG = -(-N_NODES // (P * GB))
NG += NG % 2
NROW = NG * P * GB
NBLK = NG * GB
U = 4
NT = -(-N_EDGES // P)
NT += -NT % U
NIT = NT // U
PAD_KEY = 1 << 20
PAY = D + HEADS
W2 = GB * D
HB = GB // 2

(FIRST, CONV_A, CONV_GATE, CONV_B, CONV_RES, ATT_RES, ROUND_A, ROUND_B, ROUND_C, LAST) = range(10)
CONVS = (CONV_A, CONV_GATE, CONV_B, CONV_RES, ROUND_A, ROUND_B, ROUND_C, LAST)
ROUNDS = (ROUND_A, ROUND_B, ROUND_C, LAST)
READS_X = (FIRST, CONV_GATE, CONV_RES, ATT_RES, LAST)
WRITES_X = (CONV_GATE, CONV_RES, ATT_RES)
LN_RELU = (FIRST, CONV_GATE, CONV_RES, ATT_RES)
LINKS = {FIRST: 6, CONV_A: 2, CONV_GATE: 16, CONV_B: 2, CONV_RES: 9, ATT_RES: 9, ROUND_A: 10, ROUND_B: 10, ROUND_C: 10, LAST: 10}


def gnn_kernel(nc, x, src, dst, dst_row, src_row, wt, bias, out):
    with ExitStack() as ctx:
        def sb(name, shape, dt=F32):
            return ctx.enter_context(nc.sbuf_tensor(name, shape, dt))

        def ps(name, shape, dt=F32):
            return ctx.enter_context(nc.psum_tensor(name, shape, dt))

        def sem(name):
            return ctx.enter_context(nc.semaphore(name))

        table = [nc.dram_tensor(f"table{k}", [NROW, D], F32).ap() for k in range(10)]
        total = [nc.dram_tensor(f"total{k}", [NROW + P, D], F32).ap() for k in range(10)]
        payload = nc.dram_tensor("payload", [NROW + P, PAY], F32).ap()
        xres = [nc.dram_tensor(f"xres{k}", [NROW, D], F32).ap() for k in range(3)]

        key = {"src": sb("src_key", [P, NT], I32), "dst": sb("dst_key", [P, NT], I32)}
        keyf = {k: sb(f"{k}_keyf", [P, NT]) for k in key}
        row = {k: sb(f"{k}_row", [P, NT], I32) for k in key}
        rowm = {k: sb(f"{k}_rowm", [P, NT]) for k in key}
        bits = sb("bits", [P, 2, NT], I32)
        lo = sb("lo", [P, NT])
        hi = sb("hi", [P, NT])
        spare = sb("spare", [P, 1])
        iota_b = sb("iota_b", [P, NBLK])
        ident = sb("ident", [P, P])
        lower = sb("lower", [P, P])
        onehot_lo = sb("onehot_lo", [P, U, P], BF16)
        onehot_hi = sb("onehot_hi", [P, U, NBLK], BF16)
        root = sb("root", [P, NBLK])
        dinv = sb("dinv", [P, NBLK])
        wsb = sb("wsb", [P, 4, P])
        wround = sb("wround", [P, P])
        wgate = sb("wgate", [P, D])
        wqkv = sb("wqkv", [P, 3 * D])
        bsb = sb("bsb", [P, 8, D])
        zeros = sb("zeros", [P, GB * PAY])

        own = sb("own", [P, 2, W2])
        xt = sb("xt", [P, 2, W2])
        t0 = sb("t0", [P, 2, W2])
        pay_in = sb("pay_in", [P, 2, GB * PAY])
        aT = sb("aT", [P, 2, W2])
        z = sb("z", [P, 2, W2])
        sq = sb("sq", [P, 2, W2])
        xc = sb("xc", [P, 2, W2])
        cat = sb("cat", [P, 2, GB, 2, D])
        catT = sb("catT", [P, 2, GB, P])
        gate = sb("gate", [P, 2, W2])
        xnew = sb("xnew", [P, 2, W2])
        tnew = sb("tnew", [P, 2, W2])
        mean = sb("mean", [P, 2, GB])
        var = sb("var", [P, 2, GB])
        std = sb("std", [P, 2, GB])
        rstd = sb("rstd", [P, 2, GB])
        rden = sb("rden", [P, 2, GB, HEADS])

        idx_g = sb("idx_g", [P, U, 2], I32)
        idx_s = sb("idx_s", [P, U], I32)
        krow = sb("krow", [P, U, P], I32)
        eq = sb("eq", [P, U, P])
        junk = sb("junk", [P, P])
        cnt = sb("cnt", [P, U])
        pos = sb("pos", [P, U])
        msg = sb("msg", [P, U, 2 * D])
        msgT = sb("msgT", [P, U, P])
        qs = sb("qs", [P, U, D])
        qk = sb("qk", [P, U, D])
        att = sb("att", [P, U, HEADS])
        attc = sb("attc", [P, U, HEADS])
        pay = sb("pay", [P, U, PAY])
        summed = sb("summed", [P, U, PAY])

        pA = [ps(f"pA{u}", [P, 512]) for u in range(2)]
        pB = [ps(f"pB{u}", [P, 512]) for u in range(2)]
        pC = [ps(f"pC{u}", [P, 512]) for u in range(2)]
        pD = [ps(f"pD{u}", [P, 512]) for u in range(2)]

        NAMES = ("go const_in iota mask prep oh_ready oh_used deg_done root_done norm_done zero_ready zero_out "
                 "chain dchain sq_ready std_ready "
                 "trans_done aT_ready y_ready y_used cat_ready catT_psum catT_ready g_ready gate_ready "
                 "t_ready x_ready idx_ready "
                 "eq_ready sum_done sum_used echain "
                 "hT_done hT_ready qkv_done q_ready att_ready exp_ready pay_ready").split()
        s = {n: sem(n) for n in NAMES}
        loaded = [sem(f"loaded{u}") for u in range(2)]
        stored_t = [sem(f"stored_t{u}") for u in range(2)]
        stored_x = [sem(f"stored_x{u}") for u in range(2)]
        krow_in = [sem(f"krow_in{q}") for q in range(U)]
        gathered = [sem(f"gathered{q}") for q in range(U)]
        scattered = [sem(f"scattered{q}") for q in range(U)]
        block = ctx.enter_context(nc.Block())

        def grp(tab, g, w=D):
            return tab[0:NROW, :].rearrange("(g p s) d -> g p (s d)", p=P, s=GB)[bass.ds(g, 1) if not isinstance(g, int) else slice(g, g + 1)].rearrange("g p c -> p (g c)")

        def col(t, g):
            return t[:, bass.ds(g * GB, GB)].unsqueeze(2).to_broadcast([P, GB, D])

        def b3(ap):
            return ap.rearrange("p (s d) -> p s d", s=GB)

        def spread(ap):
            return ap.unsqueeze(2).to_broadcast([P, GB, D])

        def vec(k):
            return bsb[:, k, :].unsqueeze(1).to_broadcast([P, GB, D])

        def before(k, kinds):
            return NG * sum(1 for j in range(k) if j in kinds)

        def n_loads(k):
            return (k in CONVS) + (k in READS_X) + (k == CONV_GATE) + (k == ATT_RES)

        def loads_before(k):
            return 16 * (NG // 2) * sum(n_loads(j) for j in range(k))

        def n_tstores(k):
            return 1 if k in (LAST, CONV_RES) else 2

        def tstores_before(k):
            return 16 * (NG // 2) * sum(n_tstores(j) for j in range(k))

        def xstores_before(k):
            return 16 * (NG // 2) * sum(1 for j in range(k) if j in WRITES_X)

        ZG = NG
        SCATTERS = 16 * NIT

        def links_before(k):
            return sum(NG * LINKS[j] for j in range(k))

        BIAS = {CONV_A: 0, CONV_GATE: 1, CONV_B: 2, CONV_RES: 3, ROUND_A: 4, ROUND_B: 4, ROUND_C: 4, LAST: 4}
        B_GATE, B_GAMMA, B_BETA = 5, 6, 7

        @block.sync
        def _(sp):
            n = 0
            for t, a in ((key["src"], src), (key["dst"], dst)):
                sp.dma_start(t[:], a).then_inc(s["const_in"], 16)
            sp.wait_ge(s["zero_ready"], 1)
            for k in range(4):
                for h in range(2):
                    sp.dma_start(wsb[h * D:(h + 1) * D, k, h * D:(h + 1) * D], wt[k * D:(k + 1) * D, :]).then_inc(s["const_in"], 16)
            for h in range(2):
                sp.dma_start(wround[h * D:(h + 1) * D, h * D:(h + 1) * D], wt[4 * D:5 * D, :]).then_inc(s["const_in"], 16)
            sp.dma_start(wgate[:], wt[5 * D:7 * D, :]).then_inc(s["const_in"], 16)
            sp.dma_start(wqkv[0:D, 0:D], wt[7 * D:8 * D, :]).then_inc(s["const_in"], 16)
            sp.dma_start(wqkv[D:P, D:2 * D], wt[8 * D:9 * D, :]).then_inc(s["const_in"], 16)
            sp.dma_start(wqkv[D:P, 2 * D:3 * D], wt[9 * D:10 * D, :]).then_inc(s["const_in"], 16)
            sp.dma_start(bsb[:].rearrange("p k d -> p (k d)"), bias.rearrange("k d -> (k d)").partition_broadcast(P)).then_inc(s["const_in"], 16)
            for k in range(10):
                sp.dma_start(total[k][NROW:NROW + P, :], zeros[:, 0:D]).then_inc(s["zero_out"], 16)
            sp.dma_start(payload[NROW:NROW + P, :], zeros[:, 0:PAY]).then_inc(s["zero_out"], 16)
            with sp.Fori(0, NG) as g:
                sp.dma_start(grp(payload, g), zeros[:]).then_inc(s["zero_out"], 16)

            def load(k, g, u, base):
                if k in CONVS:
                    sp.wait_ge(s["trans_done"], before(k, CONVS) + base * 2 + u + 1)
                    sp.dma_start(own[:, u, :], grp(total[k - 1], g)).then_inc(loaded[u], 16)
                if k in READS_X or k == CONV_GATE or k == ATT_RES:
                    sp.wait_ge(s["t_ready"], NG * k + base * 2 + u + 1)
                if k in READS_X:
                    a = x if k in (FIRST, CONV_GATE) else xres[WRITES_X.index(k) - 1 if k != LAST else 2]
                    sp.dma_start(xt[:, u, :], grp(a, g)).then_inc(loaded[u], 16)
                if k == CONV_GATE:
                    sp.dma_start(t0[:, u, :], grp(table[FIRST], g)).then_inc(loaded[u], 16)
                if k == ATT_RES:
                    sp.dma_start(pay_in[:, u, :], grp(payload, g)).then_inc(loaded[u], 16)

            def store(k, g, u, base):
                if k in WRITES_X:
                    sp.wait_ge(s["x_ready"], before(k, WRITES_X) + base * 2 + u + 1)
                    sp.dma_start(grp(xres[WRITES_X.index(k)], g), xnew[:, u, :]).then_inc(stored_x[u], 16)
                sp.wait_ge(s["t_ready"], NG * k + base * 2 + u + 3)
                if k == LAST:
                    sp.dma_start(grp(out, g), tnew[:, u, :]).then_inc(stored_t[u], 16)
                else:
                    sp.dma_start(grp(table[k], g), tnew[:, u, :]).then_inc(stored_t[u], 16)
                    if n_tstores(k) == 2:
                        sp.dma_start(grp(total[k], g), tnew[:, u, :]).then_inc(stored_t[u], 16)

            def edge_rows(k, t, a):
                rows = src_row if k == CONV_RES else dst_row
                for q in range(U):
                    sp.wait_ge(s["idx_ready"], NT * a + t * U + q + 1)
                    sp.dma_start(krow[:, q, :], rows[bass.ds(t * U + q, 1), :].rearrange("a e -> (a e)").partition_broadcast(P)).then_inc(krow_in[q], 16)

            for k in range(10):
                load(k, 0, 0, 0)
                load(k, 1, 1, 0)
                with sp.Fori(1, NG // 2) as h:
                    for u in range(2):
                        load(k, h * 2 + u, u, h)
                        store(k, h * 2 + (u - 2), u, h - 1)
                for u in range(2):
                    store(k, NG - 2 + u, u, NG // 2 - 1)
                if k != LAST:
                    with sp.Fori(0, NIT) as t:
                        edge_rows(k, t, k)
                    if k == CONV_RES:
                        sp.wait_ge(s["zero_out"], 16 * (11 + NG))
                    for q in range(U):
                        sp.wait_ge(scattered[q], SCATTERS * (k + 1))
                    if k in WRITES_X:
                        for u in range(2):
                            sp.wait_ge(stored_x[u], xstores_before(k + 1))
            for u in range(2):
                sp.wait_ge(stored_t[u], tstores_before(10))

        @block.gpsimd
        def _(pool):
            nc.gpsimd.iota(bits[:, 0, :].rearrange("p c -> p c")[:, 0:1], [[0, 1]], base=NROW, channel_multiplier=1).then_inc(s["iota"], 1)
            nc.gpsimd.iota(iota_b[:], [[1, NBLK]], base=0, channel_multiplier=0, allow_small_or_imprecise_dtypes=True).then_inc(s["iota"], 1)
            nc.gpsimd.memset(ident[:], 0.0).then_inc(s["mask"], 1)
            nc.gpsimd.memset(lower[:], 1.0).then_inc(s["mask"], 1)
            pool.wait_ge(s["mask"], 2)
            nc.gpsimd.affine_select(out=ident[:], in_=ident[:], compare_op=ALU.not_equal, fill=1.0, base=0,
                                    pattern=[[-1, P]], channel_multiplier=1).then_inc(s["mask"], 1)
            nc.gpsimd.affine_select(out=lower[:], in_=lower[:], compare_op=ALU.is_gt, fill=0.0, base=0,
                                    pattern=[[-1, P]], channel_multiplier=1).then_inc(s["mask"], 1)

            def gather(k, a, n, q, t):
                pool.wait_ge(s["idx_ready"], NT * a + U * t + q + 1 + U)
                pool.wait_ge(s["sum_done"], NT * a + U * t + q + 1)
                pool.sem_inc(s["go"], 1)
                if k == CONV_RES:
                    pool.indirect_dma_start(msg[:, q, 0:D], None, table[k], bass.IndirectOffsetOnAxis(ap=idx_g[:, q, 0:1], axis=0)).then_inc(gathered[q], 16)
                    pool.indirect_dma_start(msg[:, q, D:2 * D], None, table[k], bass.IndirectOffsetOnAxis(ap=idx_g[:, q, 1:2], axis=0)).then_inc(gathered[q], 16)
                else:
                    pool.indirect_dma_start(msg[:, q, 0:D], None, table[k], bass.IndirectOffsetOnAxis(ap=idx_g[:, q, 0:1], axis=0)).then_inc(gathered[q], 16)

            def scatter(k, a, q, t):
                pool.wait_ge(s["sum_used"], NT * a + U * t + q + 1 + U)
                if q:
                    pool.wait_ge(scattered[q - 1], SCATTERS * a + 16 * t + 16)
                else:
                    pool.wait_ge(scattered[U - 1], SCATTERS * a + 16 * t)
                w = PAY if k == CONV_RES else D
                pool.sem_inc(s["go"], 1)
                pool.indirect_dma_start(payload if k == CONV_RES else total[k], bass.IndirectOffsetOnAxis(ap=idx_s[:, q:q + 1], axis=0),
                                        summed[:, q, 0:w], None, compute_op=ALU.add).then_inc(scattered[q], 16)

            AHEAD = 2
            pool.wait_ge(s["zero_out"], 16 * (11 + NG))
            for k in range(9):
                for u in range(2):
                    pool.wait_ge(stored_t[u], tstores_before(k + 1))
                for q in range(AHEAD):
                    gather(k, k, q, q, 0)
                with pool.Fori(0, NIT - 1) as t:
                    for q in range(U):
                        gather(k, k, None, (q + AHEAD) % U, t + (q + AHEAD) // U)
                        scatter(k, k, q, t)
                for q in range(U):
                    if q + AHEAD < U:
                        gather(k, k, None, q + AHEAD, NIT - 1)
                    scatter(k, k, q, NIT - 1)

        @block.scalar
        def _(act):
            act.wait_ge(s["deg_done"], 1)
            nc.scalar.activation(root[:, 0:NBLK // 2], pA[0][:, 0:NBLK // 2], ACT.Sqrt, bias=1.0).then_inc(s["root_done"], 1)
            nc.scalar.activation(root[:, NBLK // 2:NBLK], pA[1][:, 0:NBLK // 2], ACT.Sqrt, bias=1.0).then_inc(s["root_done"], 1)

            def step(k, h, u):
                n = h * 2 + u
                if k in CONVS:
                    c = before(k, CONVS)
                    act.wait_ge(s["trans_done"], c + n + 3)
                    act.wait_ge(s["y_ready"], c + n - 1 + 2)
                    nc.scalar.copy(aT[:, u, :], pA[u][:]).then_inc(s["aT_ready"], 1)
                if k == CONV_GATE:
                    act.wait_ge(s["catT_psum"], n + 1)
                    act.wait_ge(s["g_ready"], n + 1)
                    nc.scalar.copy(catT[:, u, 0:HB, :].rearrange("p a b -> p (a b)"), pC[0][:]).then_inc(s["catT_ready"], 1)
                    nc.scalar.copy(catT[:, u, HB:GB, :].rearrange("p a b -> p (a b)"), pC[1][:]).then_inc(s["catT_ready"], 1)
                    act.wait_ge(s["gate_ready"], n * 2 + 1)
                    nc.scalar.activation(gate[:, u, :], gate[:, u, :], ACT.Sigmoid).then_inc(s["gate_ready"], 1)
                if k in LN_RELU or k in ROUNDS:
                    c = before(k, LN_RELU + ROUNDS)
                    act.wait_ge(s["sq_ready"], 2 * (c + n) + 1)
                    nc.scalar.activation(sq[:, u, :], xc[:, u, :], ACT.Square).then_inc(s["std_ready"], 1)
                    act.wait_ge(s["sq_ready"], 2 * (c + n) + 2)
                    nc.scalar.activation(std[:, u, :], var[:, u, :], ACT.Sqrt).then_inc(s["std_ready"], 1)

            def edge(k, a, t):
                for q in range(U):
                    n = NT * a + U * t + q
                    if k == CONV_RES:
                        m = U * t + q
                        act.wait_ge(s["hT_done"], m + 1)
                        act.wait_ge(s["qkv_done"], m + 1)
                        nc.scalar.copy(msgT[:, q, :], pB[q % 2][:, 0:P]).then_inc(s["hT_ready"], 1)
                        act.wait_ge(s["qkv_done"], m + 1 + U)
                        nc.scalar.copy(qs[:, q, :], pC[q % 2][:, 0:D]).then_inc(s["q_ready"], 1)
                        act.wait_ge(s["att_ready"], m + 1)
                        nc.scalar.activation(pay[:, q, D:PAY], attc[:, q, :], ACT.Exp).then_inc(s["exp_ready"], 1)
                    act.wait_ge(s["sum_done"], n + 1 + U)
                    act.wait_ge(scattered[q], SCATTERS * a + 16 * t)
                    w = PAY if k == CONV_RES else D
                    nc.scalar.copy(summed[:, q, 0:w], pA[q % 2][:, 0:w]).then_inc(s["sum_used"], 1)

            act.sem_inc(s["sum_used"], U)
            for k in range(10):
                with act.Fori(0, NG // 2) as h:
                    for u in range(2):
                        step(k, h, u)
                if k != LAST:
                    with act.Fori(0, NIT) as t:
                        edge(k, k, t)

        @block.vector
        def _(dve):
            links = [0]

            def link(ins, name="dchain"):
                links[0] += 1
                ins.then_inc(s[name], 1)
                dve.wait_ge(s[name], links[0])

            nc.vector.memset(zeros[:], 0.0)
            nc.vector.memset(wqkv[:], 0.0)
            nc.vector.memset(wround[:], 0.0)
            nc.vector.memset(wsb[:], 0.0).then_inc(s["zero_ready"], 1)
            dve.wait_ge(s["iota"], 2)
            link(nc.vector.tensor_copy(spare[:], bits[:, 0, 0:1]))
            dve.wait_ge(s["const_in"], 16 * 17)
            for k in ("src", "dst"):
                link(nc.vector.tensor_copy(keyf[k][:], key[k][:]))
                link(nc.vector.tensor_scalar(row[k][:], key[k][:], 10, 10, ALU.logical_shift_right, ALU.logical_shift_left))
                link(nc.vector.tensor_scalar(bits[:, 0, :], key[k][:], P - 1, 3, ALU.bitwise_and, ALU.logical_shift_left))
                link(nc.vector.tensor_tensor(row[k][:], row[k][:], bits[:, 0, :], ALU.bitwise_or))
                link(nc.vector.tensor_scalar(bits[:, 0, :], key[k][:], 7, GB - 1, ALU.logical_shift_right, ALU.bitwise_and))
                link(nc.vector.tensor_tensor(row[k][:], row[k][:], bits[:, 0, :], ALU.bitwise_or))
                link(nc.vector.tensor_scalar(row[k][:], row[k][:], NROW - 1, None, ALU.min))
                link(nc.vector.tensor_scalar(rowm[k][:], row[k][:], spare[:, 0:1], None, ALU.subtract))
            link(nc.vector.tensor_scalar(bits[:, 0, :], key["dst"][:], P - 1, None, ALU.bitwise_and))
            link(nc.vector.tensor_scalar(bits[:, 1, :], key["dst"][:], 7, None, ALU.logical_shift_right))
            link(nc.vector.tensor_copy(lo[:], bits[:, 0, :]))
            link(nc.vector.tensor_copy(hi[:], bits[:, 1, :]))

            def onehots(t):
                for q in range(U):
                    n = t * U + q
                    dve.wait_ge(s["oh_used"], n + 1)
                    nc.vector.tensor_scalar(onehot_lo[:, q, :], iota_b[:, 0:P], lo[:, bass.ds(n, 1)], None, ALU.is_equal).then_inc(s["oh_ready"], 1)
                    nc.vector.tensor_scalar(onehot_hi[:, q, :], iota_b[:], hi[:, bass.ds(n, 1)], None, ALU.is_equal).then_inc(s["oh_ready"], 1)
            with dve.Fori(0, NIT) as t:
                onehots(t)
            dve.wait_ge(s["root_done"], 2)
            nc.vector.reciprocal(dinv[:], root[:]).then_inc(s["norm_done"], 1)
            dve.wait_ge(s["norm_done"], 1)

            def step(k, h, u):
                base = links_before(k) + (h * 2 + u) * LINKS[k]
                n = h * 2 + u
                g = n
                made = [0]

                def link(ins):
                    made[0] += 1
                    ins.then_inc(s["chain"], 1)
                    dve.wait_ge(s["chain"], base + made[0])

                dve.wait_ge(loaded[u], loads_before(k) + 16 * n_loads(k) * (h + 1))
                zt, xct = b3(z[:, u, :]), b3(xc[:, u, :])
                x_in = b3(xt[:, u, :])
                if k in CONVS:
                    dve.wait_ge(s["y_ready"], before(k, CONVS) + n + 1 + 2)
                    ins = nc.vector.tensor_tensor(zt, b3(pB[u][:]), col(dinv, g), ALU.mult)
                    link(ins)
                    ins = nc.vector.tensor_tensor(zt, zt, vec(BIAS[k]), ALU.add)
                    link(ins)
                ln_in = None
                def out_free():
                    dve.wait_ge(stored_t[u], tstores_before(k) + 16 * n_tstores(k) * h)

                def x_free():
                    dve.wait_ge(stored_x[u], xstores_before(k) + 16 * h)

                if k in (CONV_A, CONV_B):
                    out_free()
                    nc.vector.scalar_tensor_tensor(b3(tnew[:, u, :]), zt, 0.0, col(dinv, g), ALU.max, ALU.mult).then_inc(s["t_ready"], 1)
                if k == CONV_GATE:
                    h0 = cat[:, u, :, 1, :]
                    hh = cat[:, u, :, 0, :]
                    link(nc.vector.tensor_tensor(h0, b3(t0[:, u, :]), col(root, g), ALU.mult))
                    nc.vector.scalar_tensor_tensor(hh, zt, 0.0, h0, ALU.max, ALU.add).then_inc(s["cat_ready"], 1)
                    dve.wait_ge(s["g_ready"], n + 1 + 1)
                    nc.vector.tensor_tensor(b3(gate[:, u, :]), b3(pD[u][:]), vec(B_GATE), ALU.add).then_inc(s["gate_ready"], 1)
                    dve.wait_ge(s["gate_ready"], n * 2 + 2)
                    link(nc.vector.tensor_tensor(zt, hh, b3(gate[:, u, :]), ALU.mult))
                    x_free()
                    ins = nc.vector.tensor_tensor(b3(xnew[:, u, :]), zt, x_in, ALU.add)
                if k == CONV_RES:
                    x_free()
                    ins = nc.vector.scalar_tensor_tensor(b3(xnew[:, u, :]), zt, 0.0, x_in, ALU.max, ALU.add)
                if k == ATT_RES:
                    pin = pay_in[:, u, :].rearrange("p (s c) -> p s c", s=GB)
                    link(nc.vector.tensor_scalar(rden[:, u, :, :], pin[:, :, D:PAY], 1e-8, None, ALU.add))
                    link(nc.vector.reciprocal(rden[:, u, :, :], rden[:, u, :, :]))
                    for hd in range(HEADS):
                        ins = nc.vector.tensor_tensor(zt[:, :, hd * DH:(hd + 1) * DH], pin[:, :, hd * DH:(hd + 1) * DH],
                                                      rden[:, u, :, hd:hd + 1].to_broadcast([P, GB, DH]), ALU.mult)
                    link(ins)
                    x_free()
                    ins = nc.vector.tensor_tensor(b3(xnew[:, u, :]), zt, x_in, ALU.add)
                if k in WRITES_X:
                    ins.then_inc(s["x_ready"], 1)
                    dve.wait_ge(s["x_ready"], before(k, WRITES_X) + n + 1)
                ln = {FIRST: x_in, LAST: zt, ROUND_A: zt, ROUND_B: zt, ROUND_C: zt}.get(k, b3(xnew[:, u, :]))
                if k in LN_RELU or k in ROUNDS:
                    c = before(k, LN_RELU + ROUNDS) + n
                    m, v, sd, r = mean[:, u, :], var[:, u, :], std[:, u, :], rstd[:, u, :]
                    link(nc.vector.tensor_reduce(m, ln, AX_X, ALU.add))
                    link(nc.vector.tensor_scalar(m, m, 1.0 / D, None, ALU.mult))
                    nc.vector.tensor_tensor(xct, ln, spread(m), ALU.subtract).then_inc(s["sq_ready"], 1)
                    dve.wait_ge(s["std_ready"], 2 * c + 1)
                    link(nc.vector.tensor_reduce(v, b3(sq[:, u, :]), AX_X, ALU.add))
                    nc.vector.tensor_scalar(v, v, 1.0 / D, 1e-5, ALU.mult, ALU.add).then_inc(s["sq_ready"], 1)
                    dve.wait_ge(s["std_ready"], 2 * c + 2)
                    link(nc.vector.reciprocal(r, sd))
                if k in LN_RELU:
                    if k != CONV_RES:
                        link(nc.vector.tensor_tensor(r, r, dinv[:, bass.ds(g * GB, GB)], ALU.mult))
                    out_free()
                    nc.vector.scalar_tensor_tensor(b3(tnew[:, u, :]), xct, 0.0, spread(r), ALU.max, ALU.mult).then_inc(s["t_ready"], 1)
                if k in ROUNDS:
                    link(nc.vector.tensor_tensor(xct, xct, spread(r), ALU.mult))
                    link(nc.vector.tensor_tensor(xct, xct, vec(B_GAMMA), ALU.mult))
                    link(nc.vector.tensor_tensor(xct, xct, vec(B_BETA), ALU.add))
                    out_free()
                    last = col(dinv, g) if k != LAST else x_in
                    nc.vector.tensor_tensor(b3(tnew[:, u, :]), xct, last, ALU.mult if k != LAST else ALU.add).then_inc(s["t_ready"], 1)
                while made[0] < LINKS[k]:
                    made[0] += 1
                    dve.sem_inc(s["chain"], 1)
                assert made[0] == LINKS[k], (k, made[0])
                dve.wait_ge(s["t_ready"], NG * k + n + 3)

            elinks = {CONV_RES: 8}

            def edge(k, a, t):
                kind = "src" if k == CONV_RES else "dst"
                EL = elinks.get(k, 3)
                for q in range(U):
                    n = U * t + q
                    made = [0]
                    base = a * NT * 3 + (NT * 5 if a > CONV_RES else 0) + n * EL

                    def link(ins):
                        made[0] += 1
                        ins.then_inc(s["echain"], 1)
                        dve.wait_ge(s["echain"], base + made[0])

                    c = bass.ds(n, 1)
                    dve.wait_ge(krow_in[q], SCATTERS * a + 16 * (t + 1))
                    dve.wait_ge(s["sum_done"], NT * a + n + 1)
                    dve.wait_ge(scattered[q], SCATTERS * a + 16 * t)
                    link(nc.vector.tensor_scalar(eq[:, q, :], krow[:, q, :], keyf[kind][:, c], None, ALU.is_equal))
                    link(nc.vector.tensor_tensor_reduce(junk[:], eq[:, q, :], lower[:], 1.0, 0.0, ALU.mult, ALU.add, cnt[:, q:q + 1]))
                    link(nc.vector.tensor_scalar(pos[:, q:q + 1], cnt[:, q:q + 1], 0.0, rowm[kind][:, c], ALU.is_equal, ALU.mult))
                    nc.vector.tensor_scalar(idx_s[:, q:q + 1], pos[:, q:q + 1], spare[:, 0:1], None, ALU.add)
                    if k == CONV_RES:
                        nc.vector.tensor_copy(idx_g[:, q, 1:2], row["dst"][:, c])
                    nc.vector.tensor_copy(idx_g[:, q, 0:1], row["src"][:, c]).then_inc(s["idx_ready"], 1)
                    if k == CONV_RES:
                        dve.wait_ge(s["q_ready"], n + 1)
                        link(nc.vector.tensor_tensor(qk[:, q, :], qs[:, q, :], pC[q % 2][:, D:2 * D], ALU.mult))
                        link(nc.vector.tensor_reduce(att[:, q, :], qk[:, q, :].rearrange("p (h d) -> p h d", h=HEADS), AX_X, ALU.add))
                        nc.vector.tensor_scalar(attc[:, q, :], att[:, q, :], -10.0, 10.0, ALU.max, ALU.min).then_inc(s["att_ready"], 1)
                        dve.wait_ge(s["exp_ready"], n + 1)
                        nc.vector.tensor_tensor(pay[:, q, 0:D].rearrange("p (h d) -> p h d", h=HEADS),
                                                pC[q % 2][:, 2 * D:3 * D].rearrange("p (h d) -> p h d", h=HEADS),
                                                pay[:, q, D:PAY].unsqueeze(2).to_broadcast([P, HEADS, DH]), ALU.mult).then_inc(s["pay_ready"], 1)
                        while made[0] < EL:
                            made[0] += 1
                            dve.sem_inc(s["echain"], 1)

            dve.sem_inc(s["idx_ready"], U)
            dve.sem_inc(s["t_ready"], 2)
            dve.wait_ge(s["mask"], 4)
            for k in range(10):
                with dve.Fori(0, NG // 2) as h:
                    for u in range(2):
                        step(k, h, u)
                if k != LAST:
                    with dve.Fori(0, NIT) as t:
                        edge(k, k, t)

        @block.tensor
        def _(pe):
            pe.sem_inc(s["trans_done"], 2)
            pe.sem_inc(s["y_ready"], 2)
            pe.sem_inc(s["g_ready"], 1)
            pe.sem_inc(s["sum_done"], U)
            pe.sem_inc(s["qkv_done"], U)
            pe.sem_inc(s["oh_used"], U)

            def count(t, start=False, stop=False):
                for q in range(U):
                    n = t * U + q
                    pe.wait_ge(s["oh_ready"], 2 * n + 2)
                    for hf in range(2):
                        ins = nc.tensor.matmul(pA[hf][:, 0:NBLK // 2], onehot_lo[:, q, :], onehot_hi[:, q, hf * NBLK // 2:(hf + 1) * NBLK // 2],
                                               start=start and q == 0, stop=stop and q == U - 1, skip_group_check=True)
                    ins.then_inc(s["oh_used"], 1)
                if stop:
                    pe.wait_ge(s["oh_used"], NT + U)
                    pe.sem_inc(s["deg_done"], 1)
            count(0, start=True)
            with pe.Fori(1, NIT - 1) as t:
                count(t)
            count(NIT - 1, stop=True)
            pe.wait_ge(s["mask"], 4)
            pe.wait_ge(s["const_in"], 16 * 17)

            def step(k, h, u):
                n = h * 2 + u
                if k not in CONVS:
                    return
                c = before(k, CONVS)
                w = wround[:] if k in ROUNDS else wsb[:, BIAS[k], :]
                pe.wait_ge(loaded[u], loads_before(k) + 16 * n_loads(k) * (h + 1))
                for j in range(HB):
                    ins = nc.tensor.transpose(pA[u][:, j * P:(j + 1) * P], own[:, u, j * P:(j + 1) * P], ident[:])
                ins.then_inc(s["trans_done"], 1)
                pe.wait_ge(s["aT_ready"], c + n + 1)
                pe.wait_ge(s["t_ready"], NG * k + n + 1)
                for j in range(HB):
                    ins = nc.tensor.matmul(pB[u][:, j * P:(j + 1) * P], aT[:, u, j * P:(j + 1) * P], w, start=True, stop=True)
                ins.then_inc(s["y_ready"], 1)
                if k == CONV_GATE:
                    pe.wait_ge(s["cat_ready"], n + 1)
                    for j in range(GB):
                        ins = nc.tensor.transpose(pC[j // HB][:, (j % HB) * P:(j % HB + 1) * P], cat[:, u, j, :, :].rearrange("p a d -> p (a d)"), ident[:])
                    ins.then_inc(s["catT_psum"], 1)
                    pe.wait_ge(s["catT_ready"], n * 2 + 2)
                    for j in range(GB):
                        ins = nc.tensor.matmul(pD[u][:, j * D:(j + 1) * D], catT[:, u, j, :], wgate[:], start=True, stop=True)
                    ins.then_inc(s["g_ready"], 1)

            def edge(k, a, t):
                for q in range(U):
                    m = U * t + q
                    n = NT * a + m
                    c = 1 if a > CONV_RES else 0
                    pe.wait_ge(gathered[q], 16 * NIT * (a + c) + (t + 1) * (32 if k == CONV_RES else 16))
                    pe.wait_ge(s["idx_ready"], n + 1 + U)
                    if k == CONV_RES:
                        nc.tensor.transpose(pB[q % 2][:, 0:P], msg[:, q, :], ident[:]).then_inc(s["hT_done"], 1)
                        pe.wait_ge(s["hT_ready"], m + 1)
                        nc.tensor.matmul(pC[q % 2][:, 0:3 * D], msgT[:, q, :], wqkv[:], start=True, stop=True).then_inc(s["qkv_done"], 1)
                        pe.wait_ge(s["pay_ready"], m + 1)
                    w = PAY if k == CONV_RES else D
                    pe.wait_ge(s["sum_used"], n + U - 1)
                    nc.tensor.matmul(pA[q % 2][:, 0:w], eq[:, q, :], pay[:, q, :] if k == CONV_RES else msg[:, q, 0:D],
                                     start=True, stop=True).then_inc(s["sum_done"], 1)

            for k in range(10):
                if k in CONVS:
                    with pe.Fori(0, NG // 2) as h:
                        for u in range(2):
                            step(k, h, u)
                if k != LAST:
                    with pe.Fori(0, NIT) as t:
                        edge(k, k, t)


def kernel(**inputs):
    import numpy as np
    import concourse.bacc as _bacc
    from concourse import mybir as _mybir
    from concourse.bass_utils import run_bass_kernel_spmd as _run

    a = {k: np.asarray(v) for k, v in inputs.items()}
    x = np.zeros((NROW, D), a["x"].dtype)
    x[:N_NODES] = a["x"]
    x = np.ascontiguousarray(x.reshape(NG, GB, P, D).transpose(0, 2, 1, 3)).reshape(NROW, D)
    edges = {}
    for k in ("src", "dst"):
        e = np.full((NT * P,), PAD_KEY, a[k].dtype)
        e[:N_EDGES] = a[k]
        edges[k + "_row"] = e.reshape(NT, P)
        edges[k] = np.ascontiguousarray(e.reshape(NT, P).T)
    wt = np.concatenate([a["L0_gnn_W1"].T, a["L0_gnn_W2"].T, a["L1_gnn_W1"], a["L1_gnn_W2"], a["L3_gnn_W"],
                         a["L0_gnn_Wg"].T, a["L2_gnn_Wq"], a["L2_gnn_Wk"], a["L2_gnn_Wv"]], axis=0)
    bias = np.stack([a["L0_gnn_b1"], a["L0_gnn_b2"], a["L1_gnn_b1"], a["L1_gnn_b2"], a["L3_gnn_b"], a["L0_gnn_bg"],
                     a["L3_gnn_gamma"], a["L3_gnn_beta"]])
    arrays = {"x": x, "src": edges["src"], "dst": edges["dst"], "dst_row": edges["dst_row"], "src_row": edges["src_row"],
              "wt": np.ascontiguousarray(wt), "bias": np.ascontiguousarray(bias)}
    nc = _bacc.Bacc("TRN2", target_bir_lowering=False, num_devices=1)
    args = [nc.dram_tensor(f"in_{n}", v.shape, _mybir.dt.from_np(v.dtype), kind="ExternalInput").ap() for n, v in arrays.items()]
    out = nc.dram_tensor("out_dram", (NROW, D), F32, kind="ExternalOutput").ap()
    gnn_kernel(nc, *args, out)
    r = _run(nc, [{f"in_{n}": v for n, v in arrays.items()}], core_ids=[0])
    got = np.asarray(r.results[0]["out_dram"]).reshape(NG, P, GB, D).transpose(0, 2, 1, 3)
    return np.ascontiguousarray(got).reshape(NROW, D)[:N_NODES]
```

```python
from contextlib import ExitStack

import concourse.bass as bass
from concourse import mybir

ALU = mybir.AluOpType
ACT = mybir.ActivationFunctionType
AX_X = mybir.AxisListType.X
F32 = mybir.dt.float32
BF16 = mybir.dt.bfloat16
I32 = mybir.dt.int32

P = 128
D = 64
HEADS = 4
DH = D // HEADS
GB = 8
N_NODES = 100000
N_EDGES = 50000
NG = -(-N_NODES // (P * GB))
NG += -NG % 4
NROW = NG * P * GB
NBLK = NG * GB
U = 4
NT = -(-N_EDGES // P)
NT += -NT % U
NIT = NT // U
PAD_KEY = 1 << 20
PAY = D + HEADS
W2 = GB * D
HB = GB // 2
PIECES = 3
MW = PIECES * D
RB = 8
AHEAD = 3
BACK = 3
TP = NT // 4
S4 = 4
FULL = (NIT - AHEAD) // S4

(FIRST, CONV_A, CONV_GATE, CONV_B, CONV_RES, ATT_RES, ROUND_A, ROUND_B, ROUND_C, LAST) = range(10)
CONVS = (CONV_A, CONV_GATE, CONV_B, CONV_RES, ROUND_A, ROUND_B, ROUND_C, LAST)
ROUNDS = (ROUND_A, ROUND_B, ROUND_C, LAST)
READS_X = (FIRST, CONV_GATE, CONV_RES, ATT_RES, LAST)
WRITES_X = (CONV_GATE, CONV_RES, ATT_RES)
LN_RELU = (FIRST, CONV_GATE, CONV_RES, ATT_RES)
LINKS = {FIRST: 6, CONV_A: 2, CONV_GATE: 16, CONV_B: 2, CONV_RES: 9, ATT_RES: 9, ROUND_A: 10, ROUND_B: 10, ROUND_C: 10, LAST: 10}


def gnn_kernel(nc, x, src, dst, dst_row, src_row, wt, bias, out):
    with ExitStack() as ctx:
        def sb(name, shape, dt=F32):
            return ctx.enter_context(nc.sbuf_tensor(name, shape, dt))

        def ps(name, shape, dt=F32):
            return ctx.enter_context(nc.psum_tensor(name, shape, dt))

        def sem(name):
            return ctx.enter_context(nc.semaphore(name))

        table = [nc.dram_tensor(f"table{k}", [NROW, D], F32).ap() for k in range(10)]
        total = [nc.dram_tensor(f"total{k}", [NROW + P, D], F32).ap() for k in range(10)]
        sel_d = nc.dram_tensor("sel_d", [NG, P, 2 * GB * P], BF16).ap()
        payload = nc.dram_tensor("payload", [NROW + P, PAY], F32).ap()
        xres = [nc.dram_tensor(f"xres{k}", [NROW, D], F32).ap() for k in range(3)]

        key = {"src": sb("src_key", [P, NT], I32), "dst": sb("dst_key", [P, NT], I32)}
        keyf = {k: sb(f"{k}_keyf", [P, NT]) for k in key}
        row = {k: sb(f"{k}_row", [P, NT], I32) for k in key}
        rowm = {k: sb(f"{k}_rowm", [P, NT]) for k in key}
        bits = sb("bits", [P, 2, NT], I32)
        lo = sb("lo", [P, NT])
        hi = sb("hi", [P, NT])
        spare = sb("spare", [P, 1])
        iota_b = sb("iota_b", [P, NBLK])
        ident = sb("ident", [P, P])
        lower = sb("lower", [P, P])
        onehot_lo = sb("onehot_lo", [P, U, P], BF16)
        root = sb("root", [P, NBLK])
        dinv = sb("dinv", [P, NBLK])
        wsb = sb("wsb", [P, 4, P])
        wround = sb("wround", [P, P])
        wgate = sb("wgate", [P, D])
        wqkv = sb("wqkv", [P, 3 * D])
        bsb = sb("bsb", [P, 8, D])
        zeros = sb("zeros", [P, GB * PAY])

        own = sb("own", [P, S4, W2])
        xt = sb("xt", [P, S4, W2])
        t0 = sb("t0", [P, S4, W2])
        pay_in = sb("pay_in", [P, S4, GB * PAY])
        onehot_hi = pay_in[:].rearrange("p a c -> p (a c)").bitcast(BF16)[:, 0:U * NBLK].rearrange("p (u b) -> p u b", u=U)
        aT = sb("aT", [P, 2, W2])
        z = sb("z", [P, S4, W2])
        sq = sb("sq", [P, 2, W2])
        xc = sb("xc", [P, S4, W2])
        gate = sb("gate", [P, 2, W2])
        xnew = sb("xnew", [P, S4, W2])
        tnew = sb("tnew", [P, S4, W2])
        mean = sb("mean", [P, S4, GB])
        var = sb("var", [P, S4, GB])
        std = sb("std", [P, S4, GB])
        rstd = sb("rstd", [P, S4, GB])
        rden = sb("rden", [P, S4, GB, HEADS])

        sel = sb("sel", [P, S4, 2 * GB, P], BF16)
        raw = sb("raw", [P, S4, U, D])
        rest = sb("rest", [P, 2, U, D])
        idx_f = sb("idx_f", [P, S4, U], I32)
        ring = sb("ring", [P, RB * U, MW], BF16)
        asum = sb("asum", [P, 2, W2])
        hh = sb("hh", [P, S4, W2])
        h0 = sb("h0", [P, S4, W2])
        hhT = sb("hhT", [P, GB, P])
        cat = hh[:].rearrange("p a c -> p (a c)").rearrange("p (u s k d) -> p u s k d", u=2, s=GB, k=2)
        catT = h0[:].rearrange("p a c -> p (a c)").rearrange("p (u s n) -> p u s n", u=2, s=GB)
        t0_f, tnew_f = (t[:].rearrange("p a c -> p (a c)") for t in (t0, tnew))
        first = tnew_f[:, 0:NBLK]
        first_i = tnew_f[:, NBLK:2 * NBLK].bitcast(I32)
        base_of = t0_f[:, 0:NBLK]
        tile0 = t0_f[:, NBLK:2 * NBLK]
        dloc = sb("dloc", [P, 2, NBLK])
        tiles_p = sb("tiles_p", [P, 4])
        place = sb("place", [1, NG, 2 * GB], I32)
        checks = sb("checks", [P, 4])
        flag = sb("flag", [1, 1], I32)
        ones = sb("ones", [P, P])
        wcent = sb("wcent", [P, P])
        bcent = sb("bcent", [P, D])
        wmean = sb("wmean", [P, 2])
        wgp = sb("wgp", [P, 2, P])

        idx_g = sb("idx_g", [P, U, 2], I32)
        idx_s = sb("idx_s", [P, U], I32)
        krow = sb("krow", [P, U, P], I32)
        eq = sb("eq", [P, U, P])
        junk = sb("junk", [P, P])
        cnt = sb("cnt", [P, U])
        pos = sb("pos", [P, U])
        msg = sb("msg", [P, U, 2 * D])
        msgT = sb("msgT", [P, U, P])
        qs = sb("qs", [P, U, D])
        qk = sb("qk", [P, U, D])
        att = sb("att", [P, U, HEADS])
        attc = sb("attc", [P, U, HEADS])
        pay = sb("pay", [P, U, PAY])
        summed = sb("summed", [P, U, PAY])

        pA = [ps(f"pA{u}", [P, 512]) for u in range(2)]
        pB = [ps(f"pB{u}", [P, 512]) for u in range(2)]
        pC = [ps(f"pC{u}", [P, 512]) for u in range(2)]
        pD = [ps(f"pD{u}", [P, 512]) for u in range(2)]
        rowlay = hh[0:TP, 0, :].bitcast(I32)
        rowlayf = h0[0:TP, 0, :]
        onehot_tile = [t[:].rearrange("p a c -> p (a c)")[:, o:o + NBLK] for t in (xt, own) for o in (0, 2 * W2)]
        size = z[:].rearrange("p a c -> p (a c)")[:, 0:NBLK]
        ends = z[:].rearrange("p a c -> p (a c)")[:, NBLK:2 * NBLK]
        hits = xc[:].rearrange("p a c -> p (a c)")[:, 0:2 * NBLK]
        hits2 = xnew[:].rearrange("p a c -> p (a c)")[:, 0:2 * NBLK]

        NAMES = ("row_in pchain c1 c2 oht_ready oht_used flag_ready fast_wt "
                 "f_idx f_hi f_rest f_mid f_split f_agg f_add f_trans f_evac f_mm f_z f_sqin f_sq f_var f_std f_pre f_x f_out "
                 "f_cat f_gtr f_gev f_gmm f_gin f_gate chz chx chr chn chf sel_made go const_in iota mask prep oh_ready oh_used deg_done root_done norm_done zero_ready zero_out "
                 "chain dchain sq_ready std_ready "
                 "trans_done aT_ready y_ready y_used cat_ready catT_psum catT_ready g_ready gate_ready "
                 "t_ready x_ready idx_ready "
                 "eq_ready sum_done sum_used echain "
                 "hT_done hT_ready qkv_done q_ready att_ready exp_ready pay_ready").split()
        s = {n: sem(n) for n in NAMES}
        loaded = [sem(f"loaded{u}") for u in range(2)]
        stored_t = [sem(f"stored_t{u}") for u in range(2)]
        stored_x = [sem(f"stored_x{u}") for u in range(2)]
        own_in = [sem(f"own_in{u}") for u in range(S4)]
        sel_in = [sem(f"sel_in{u}") for u in range(S4)]
        x_in = [sem(f"x_in{u}") for u in range(S4)]
        t0_in = [sem(f"t0_in{u}") for u in range(S4)]
        raw_in = [sem(f"raw_in{u}") for u in range(S4)]
        st_t = [sem(f"st_t{u}") for u in range(S4)]
        st_x = [sem(f"st_x{u}") for u in range(S4)]
        sel_out = [sem(f"sel_out{u}") for u in range(2)]
        krow_in = [sem(f"krow_in{q}") for q in range(U)]
        gathered = [sem(f"gathered{q}") for q in range(U)]
        scattered = [sem(f"scattered{q}") for q in range(U)]
        block = ctx.enter_context(nc.Block())

        def grp(tab, g, w=D):
            return tab[0:NROW, :].rearrange("(g p s) d -> g p (s d)", p=P, s=GB)[bass.ds(g, 1) if not isinstance(g, int) else slice(g, g + 1)].rearrange("g p c -> p (g c)")

        def col(t, g):
            return t[:, bass.ds(g * GB, GB)].unsqueeze(2).to_broadcast([P, GB, D])

        def b3(ap):
            return ap.rearrange("p (s d) -> p s d", s=GB)

        def spread(ap):
            return ap.unsqueeze(2).to_broadcast([P, GB, D])

        def vec(k):
            return bsb[:, k, :].unsqueeze(1).to_broadcast([P, GB, D])

        def before(k, kinds):
            return NG * sum(1 for j in range(k) if j in kinds)

        def n_loads(k):
            return (k in CONVS) + (k in READS_X) + (k == CONV_GATE) + (k == ATT_RES)

        def loads_before(k):
            return 16 * (NG // 2) * sum(n_loads(j) for j in range(k))

        def n_tstores(k):
            return 1 if k in (LAST, CONV_RES) else 2

        def tstores_before(k):
            return 16 * (NG // 2) * sum(n_tstores(j) for j in range(k))

        def xstores_before(k):
            return 16 * (NG // 2) * sum(1 for j in range(k) if j in WRITES_X)

        KINDS = {ev: CONVS for ev in "f_agg f_add f_trans f_evac f_mm f_hi f_rest f_mid f_split f_idx".split()}
        KINDS["f_z"] = ROUNDS
        KINDS["f_sqin"] = LN_RELU
        KINDS |= {ev: LN_RELU + ROUNDS for ev in "f_sq f_var f_std".split()}
        KINDS |= {ev: (CONV_GATE,) for ev in "f_cat f_gtr f_gev f_gmm f_gin f_gate".split()}
        KINDS |= {"f_pre": (ROUND_A, ROUND_B, ROUND_C), "f_x": WRITES_X, "f_out": tuple(range(10))}
        PER_BATCH = "f_hi f_rest f_mid f_split f_idx".split()

        def upto(ev, k, m):
            return (NIT if ev in PER_BATCH else NG) * sum(1 for j in range(k) if j in KINDS[ev]) + m + 1

        def after(eng, ev, k, m, lag=0):
            if isinstance(m, int) and m < lag:
                return
            eng.wait_ge(s[ev], upto(ev, k, m - lag))

        def landed(eng, sems, kinds, k, m, u, turn, each=1, lag=0):
            if isinstance(m, int) and m < lag:
                return
            eng.wait_ge(sems[u], 16 * (each * (turn - lag // S4 + 1) + NG // S4 * sum(dmas(j, kinds) for j in range(k))))

        def raw_before(k, q):
            return sum(1 for j in range(k) if j in CONVS) * len(range(q, NIT, S4))

        def dmas(j, kinds):
            return kinds.get(j, 0)

        X_LOADS = {k: 1 + (k == ATT_RES) for k in READS_X}
        T0_LOADS = {CONV_GATE: 1}
        OWN_LOADS = {k: 1 for k in CONVS}
        T_STORES = {k: 1 for k in range(10)}
        X_STORES = {k: 1 for k in WRITES_X}

        def x_part(k):
            return {CONV_GATE: 5, FIRST: 0, ATT_RES: 0}.get(k, 2)

        def steps(eng, k, body):
            lo = -(-(x_part(k) + 1 + S4) // S4)
            hi = FULL if k in CONVS else NG // S4
            for n in range(lo * S4):
                body(k, n, n % S4, n // S4)
            with eng.Fori(lo, hi) as it:
                for u in range(S4):
                    body(k, it * S4 + u, u, it)
            for n in range(hi * S4, NG + x_part(k) + 3):
                body(k, n, n % S4, n // S4)

        def at(n, u, it, off):
            m = n - off
            return (not isinstance(m, int)) or 0 <= m < NG, m, (u - off) % S4, it + (u - off) // S4

        def batch(n, u, it):
            b, q = n + AHEAD, u + AHEAD
            if isinstance(n, int):
                return b < NIT, b, b % S4, b % RB * U
            return True, b, q % S4, (it + q // S4) % (RB // S4) * (S4 * U) + q % S4 * U

        ZG = NG
        SCATTERS = 16 * NIT

        def links_before(k):
            return sum(NG * LINKS[j] for j in range(k))

        BIAS = {CONV_A: 0, CONV_GATE: 1, CONV_B: 2, CONV_RES: 3, ROUND_A: 4, ROUND_B: 4, ROUND_C: 4, LAST: 4}
        B_GATE, B_GAMMA, B_BETA = 5, 6, 7

        pG = pB[1]

        def y_bank(k, q):
            return pB[0] if k == CONV_GATE else pB[q % 2]

        @block.sync
        def _(sp):
            n = 0
            for t, a in ((key["src"], src), (key["dst"], dst)):
                sp.dma_start(t[:], a).then_inc(s["const_in"], 16)
            sp.wait_ge(s["zero_ready"], 1)
            for k in range(4):
                for h in range(2):
                    sp.dma_start(wsb[h * D:(h + 1) * D, k, h * D:(h + 1) * D], wt[k * D:(k + 1) * D, :]).then_inc(s["const_in"], 16)
            for h in range(2):
                sp.dma_start(wround[h * D:(h + 1) * D, h * D:(h + 1) * D], wt[4 * D:5 * D, :]).then_inc(s["const_in"], 16)
            sp.dma_start(wgate[:], wt[5 * D:7 * D, :]).then_inc(s["const_in"], 16)
            sp.dma_start(wqkv[0:D, 0:D], wt[7 * D:8 * D, :]).then_inc(s["const_in"], 16)
            sp.dma_start(wqkv[D:P, D:2 * D], wt[8 * D:9 * D, :]).then_inc(s["const_in"], 16)
            sp.dma_start(wqkv[D:P, 2 * D:3 * D], wt[9 * D:10 * D, :]).then_inc(s["const_in"], 16)
            sp.dma_start(bsb[:].rearrange("p k d -> p (k d)"), bias.rearrange("k d -> (k d)").partition_broadcast(P)).then_inc(s["const_in"], 16)
            for k in range(10):
                sp.dma_start(total[k][NROW:NROW + P, :], zeros[:, 0:D]).then_inc(s["zero_out"], 16)
            sp.dma_start(payload[NROW:NROW + P, :], zeros[:, 0:PAY]).then_inc(s["zero_out"], 16)
            with sp.Fori(0, NG) as g:
                sp.dma_start(grp(payload, g), zeros[:]).then_inc(s["zero_out"], 16)

            def load(k, g, u, base):
                if k in CONVS:
                    sp.wait_ge(s["trans_done"], before(k, CONVS) + base * 2 + u + 1)
                    sp.dma_start(own[:, u, :], grp(total[k - 1], g)).then_inc(loaded[u], 16)
                if k in READS_X or k == CONV_GATE or k == ATT_RES:
                    sp.wait_ge(s["t_ready"], NG * k + base * 2 + u + 1)
                if k in READS_X:
                    a = x if k in (FIRST, CONV_GATE) else xres[WRITES_X.index(k) - 1 if k != LAST else 2]
                    sp.dma_start(xt[:, u, :], grp(a, g)).then_inc(loaded[u], 16)
                if k == CONV_GATE:
                    sp.dma_start(t0[:, u, :], grp(table[FIRST], g)).then_inc(loaded[u], 16)
                if k == ATT_RES:
                    sp.dma_start(pay_in[:, u, :], grp(payload, g)).then_inc(loaded[u], 16)

            def store(k, g, u, base):
                if k in WRITES_X:
                    sp.wait_ge(s["x_ready"], before(k, WRITES_X) + base * 2 + u + 1)
                    sp.dma_start(grp(xres[WRITES_X.index(k)], g), xnew[:, u, :]).then_inc(stored_x[u], 16)
                sp.wait_ge(s["t_ready"], NG * k + base * 2 + u + 3)
                if k == LAST:
                    sp.dma_start(grp(out, g), tnew[:, u, :]).then_inc(stored_t[u], 16)
                else:
                    sp.dma_start(grp(table[k], g), tnew[:, u, :]).then_inc(stored_t[u], 16)
                    if n_tstores(k) == 2:
                        sp.dma_start(grp(total[k], g), tnew[:, u, :]).then_inc(stored_t[u], 16)

            def edge_rows(k, t, a):
                rows = src_row if k == CONV_RES else dst_row
                for q in range(U):
                    sp.wait_ge(s["idx_ready"], NT * a + t * U + q + 1)
                    sp.dma_start(krow[:, q, :], rows[bass.ds(t * U + q, 1), :].rearrange("a e -> (a e)").partition_broadcast(P)).then_inc(krow_in[q], 16)

            sp.dma_start(rowlay, dst_row.rearrange("(c p) e -> p c e", p=TP)).then_inc(s["row_in"], 16)
            for j in range(2):
                for h in range(2):
                    sp.dma_start(wgp[h * D:(h + 1) * D, j, h * D:(h + 1) * D], wt[(5 + j) * D:(6 + j) * D, :]).then_inc(s["row_in"], 16)
            with sp.Fori(0, NG // 2) as h:
                for u in range(2):
                    sp.wait_ge(s["sel_made"], h * 2 + u + 1)
                    sp.dma_start(sel_d[bass.ds(h * 2 + u, 1)].rearrange("a p c -> p (a c)"), sel[:, u].rearrange("p k n -> p (k n)")).then_inc(sel_out[u], 16)
            for u in range(2):
                sp.wait_ge(sel_out[u], 16 * (NG // 2))

            def fast(k, n, u, it):
                if k in CONVS:
                    live, m, q, turn = at(n, u, it, 0)
                    if live:
                        after(sp, "f_agg", k, m, S4)
                        sp.dma_start(sel[:, q].rearrange("p k n -> p (k n)"), sel_d[m:m + 1].rearrange("a p c -> p (a c)") if isinstance(m, int) else sel_d[bass.ds(m, 1)].rearrange("a p c -> p (a c)")).then_inc(sel_in[q], 16)
                        after(sp, "f_add", k, m, S4)
                        sp.dma_start(own[:, q, :], grp(table[k - 1], m)).then_inc(own_in[q], 16)
                if k == CONV_GATE:
                    live, m, q, turn = at(n, u, it, 0)
                    if live:
                        after(sp, "f_cat", k, m, S4)
                        sp.dma_start(t0[:, q, :], grp(table[FIRST], m)).then_inc(t0_in[q], 16)
                if k in READS_X:
                    live, m, q, turn = at(n, u, it, max(0, x_part(k) - 2))
                    if live:
                        after(sp, "f_out" if k == LAST else "f_x" if k in WRITES_X else "f_sqin", k, m, S4)
                        a = x if k in (FIRST, CONV_GATE) else xres[WRITES_X.index(k) - 1 if k != LAST else 2]
                        sp.dma_start(xt[:, q, :], grp(a, m)).then_inc(x_in[q], 16)
                        if k == ATT_RES:
                            sp.dma_start(pay_in[:, q, :], grp(payload, m)).then_inc(x_in[q], 16)
                live, m, q, turn = at(n, u, it, x_part(k) + 2)
                if live:
                    if k in WRITES_X:
                        after(sp, "f_x", k, m)
                        sp.dma_start(grp(xres[WRITES_X.index(k)], m), xnew[:, q, :]).then_inc(st_x[q], 16)
                    after(sp, "f_out", k, m)
                    sp.dma_start(grp(out if k == LAST else table[k], m), tnew[:, q, :]).then_inc(st_t[q], 16)

            def pass_stored(eng, sems, kinds, k):
                for q in range(S4):
                    eng.wait_ge(sems[q], 16 * (NG // S4) * sum(dmas(j, kinds) for j in range(k + 1)))

            sp.wait_ge(s["flag_ready"], 1)
            even = sp.value_load(flag[0:1, 0:1], min_val=0, max_val=1)
            with sp.If(even == 1):
                for k in range(10):
                    steps(sp, k, fast)
                    pass_stored(sp, st_t, T_STORES, k)
                    if k in WRITES_X:
                        pass_stored(sp, st_x, X_STORES, k)
                    if k == CONV_RES:
                        with sp.Fori(0, NIT) as t:
                            edge_rows(k, t, 0)
                        for q in range(U):
                            sp.wait_ge(scattered[q], SCATTERS)
            with sp.Else():
              for k in range(10):
                  load(k, 0, 0, 0)
                  load(k, 1, 1, 0)
                  with sp.Fori(1, NG // 2) as h:
                      for u in range(2):
                          load(k, h * 2 + u, u, h)
                          store(k, h * 2 + (u - 2), u, h - 1)
                  for u in range(2):
                      store(k, NG - 2 + u, u, NG // 2 - 1)
                  if k != LAST:
                      with sp.Fori(0, NIT) as t:
                          edge_rows(k, t, k)
                      if k == CONV_RES:
                          sp.wait_ge(s["zero_out"], 16 * (11 + NG))
                      for q in range(U):
                          sp.wait_ge(scattered[q], SCATTERS * (k + 1))
                      if k in WRITES_X:
                          for u in range(2):
                              sp.wait_ge(stored_x[u], xstores_before(k + 1))
              for u in range(2):
                  sp.wait_ge(stored_t[u], tstores_before(10))

        @block.gpsimd
        def _(pool):
            nc.gpsimd.iota(bits[:, 0, :].rearrange("p c -> p c")[:, 0:1], [[0, 1]], base=NROW, channel_multiplier=1).then_inc(s["iota"], 1)
            nc.gpsimd.iota(iota_b[:], [[1, NBLK]], base=0, channel_multiplier=0, allow_small_or_imprecise_dtypes=True).then_inc(s["iota"], 1)
            nc.gpsimd.memset(ident[:], 0.0).then_inc(s["mask"], 1)
            nc.gpsimd.memset(lower[:], 1.0).then_inc(s["mask"], 1)
            pool.wait_ge(s["mask"], 2)
            nc.gpsimd.affine_select(out=ident[:], in_=ident[:], compare_op=ALU.not_equal, fill=1.0, base=0,
                                    pattern=[[-1, P]], channel_multiplier=1).then_inc(s["mask"], 1)
            nc.gpsimd.affine_select(out=lower[:], in_=lower[:], compare_op=ALU.is_gt, fill=0.0, base=0,
                                    pattern=[[-1, P]], channel_multiplier=1).then_inc(s["mask"], 1)

            def gather(k, a, n, q, t):
                pool.wait_ge(s["idx_ready"], NT * a + U * t + q + 1 + U)
                pool.wait_ge(s["sum_done"], NT * a + U * t + q + 1)
                pool.sem_inc(s["go"], 1)
                if k == CONV_RES:
                    pool.indirect_dma_start(msg[:, q, 0:D], None, table[k], bass.IndirectOffsetOnAxis(ap=idx_g[:, q, 0:1], axis=0)).then_inc(gathered[q], 16)
                    pool.indirect_dma_start(msg[:, q, D:2 * D], None, table[k], bass.IndirectOffsetOnAxis(ap=idx_g[:, q, 1:2], axis=0)).then_inc(gathered[q], 16)
                else:
                    pool.indirect_dma_start(msg[:, q, 0:D], None, table[k], bass.IndirectOffsetOnAxis(ap=idx_g[:, q, 0:1], axis=0)).then_inc(gathered[q], 16)

            def scatter(k, a, q, t):
                pool.wait_ge(s["sum_used"], NT * a + U * t + q + 1 + U)
                if q:
                    pool.wait_ge(scattered[q - 1], SCATTERS * a + 16 * t + 16)
                else:
                    pool.wait_ge(scattered[U - 1], SCATTERS * a + 16 * t)
                w = PAY if k == CONV_RES else D
                pool.sem_inc(s["go"], 1)
                pool.indirect_dma_start(payload if k == CONV_RES else total[k], bass.IndirectOffsetOnAxis(ap=idx_s[:, q:q + 1], axis=0),
                                        summed[:, q, 0:w], None, compute_op=ALU.add).then_inc(scattered[q], 16)

            nc.gpsimd.iota(tiles_p[:], [[TP, 4]], base=0, channel_multiplier=1, allow_small_or_imprecise_dtypes=True).then_inc(s["iota"], 1)
            nc.gpsimd.iota(base_of[:], [[P, NBLK]], base=0, channel_multiplier=0, allow_small_or_imprecise_dtypes=True).then_inc(s["iota"], 1)
            nc.gpsimd.iota(tile0[:], [[U, NG], [0, GB]], base=0, channel_multiplier=0, allow_small_or_imprecise_dtypes=True).then_inc(s["iota"], 1)
            nc.gpsimd.memset(ones[:], 1.0).then_inc(s["iota"], 1)

            def edge_pass(k, a):
                for q in range(LEAD):
                    gather(k, a, q, q, 0)
                with pool.Fori(0, NIT - 1) as t:
                    for q in range(U):
                        gather(k, a, None, (q + LEAD) % U, t + (q + LEAD) // U)
                        scatter(k, a, q, t)
                for q in range(U):
                    if q + LEAD < U:
                        gather(k, a, None, q + LEAD, NIT - 1)
                    scatter(k, a, q, NIT - 1)

            def fast_gather(k, b, q):
                after(pool, "f_rest", k, b, S4)
                pool.sem_inc(s["go"], 1)
                nc.gpsimd.tensor_copy(idx_f[:, q, :], row["src"][:, bass.ds(b * U, U)]).then_inc(s["f_idx"], 1)
                after(pool, "f_idx", k, b)
                pool.sem_inc(s["go"], 1)
                for j in range(U):
                    pool.indirect_dma_start(raw[:, q, j, :], None, table[k - 1], bass.IndirectOffsetOnAxis(ap=idx_f[:, q, j:j + 1], axis=0)).then_inc(raw_in[q], 16)

            LEAD = 2
            pool.wait_ge(s["zero_out"], 16 * (11 + NG))
            pool.wait_ge(s["flag_ready"], 1)
            even = pool.value_load(flag[0:1, 0:1], min_val=0, max_val=1)
            with pool.If(even == 1):
                for k in range(10):
                    if k in CONVS:
                        for q in range(S4):
                            pool.wait_ge(st_t[q], 16 * (NG // S4) * k)
                        for b in range(S4):
                            fast_gather(k, b, b)
                        with pool.Fori(1, NIT // S4) as it:
                            for q in range(S4):
                                fast_gather(k, it * S4 + q, q)
                        for b in range(NIT - NIT % S4, NIT):
                            fast_gather(k, b, b % S4)
                    if k == CONV_RES:
                        for q in range(S4):
                            pool.wait_ge(st_t[q], 16 * (NG // S4) * (k + 1))
                        edge_pass(k, 0)
            with pool.Else():
              for k in range(9):
                for u in range(2):
                    pool.wait_ge(stored_t[u], tstores_before(k + 1))
                edge_pass(k, k)

        @block.scalar
        def _(act):
            act.wait_ge(s["deg_done"], 1)
            nc.scalar.activation(root[:, 0:NBLK // 2], pA[0][:, 0:NBLK // 2], ACT.Sqrt, bias=1.0).then_inc(s["root_done"], 1)
            nc.scalar.activation(root[:, NBLK // 2:NBLK], pA[1][:, 0:NBLK // 2], ACT.Sqrt, bias=1.0).then_inc(s["root_done"], 1)

            def step(k, h, u):
                n = h * 2 + u
                if k in CONVS:
                    c = before(k, CONVS)
                    act.wait_ge(s["trans_done"], c + n + 3)
                    act.wait_ge(s["y_ready"], c + n - 1 + 2)
                    nc.scalar.copy(aT[:, u, :], pA[u][:]).then_inc(s["aT_ready"], 1)
                if k == CONV_GATE:
                    act.wait_ge(s["catT_psum"], n + 1)
                    act.wait_ge(s["g_ready"], n + 1)
                    nc.scalar.copy(catT[:, u, 0:HB, :].rearrange("p a b -> p (a b)"), pC[0][:]).then_inc(s["catT_ready"], 1)
                    nc.scalar.copy(catT[:, u, HB:GB, :].rearrange("p a b -> p (a b)"), pC[1][:]).then_inc(s["catT_ready"], 1)
                    act.wait_ge(s["gate_ready"], n * 2 + 1)
                    nc.scalar.activation(gate[:, u, :], gate[:, u, :], ACT.Sigmoid).then_inc(s["gate_ready"], 1)
                if k in LN_RELU or k in ROUNDS:
                    c = before(k, LN_RELU + ROUNDS)
                    act.wait_ge(s["sq_ready"], 2 * (c + n) + 1)
                    nc.scalar.activation(sq[:, u, :], xc[:, u, :], ACT.Square).then_inc(s["std_ready"], 1)
                    act.wait_ge(s["sq_ready"], 2 * (c + n) + 2)
                    nc.scalar.activation(std[:, u, :], var[:, u, :], ACT.Sqrt).then_inc(s["std_ready"], 1)

            def edge(k, a, t):
                for q in range(U):
                    n = NT * a + U * t + q
                    if k == CONV_RES:
                        m = U * t + q
                        act.wait_ge(s["hT_done"], m + 1)
                        act.wait_ge(s["qkv_done"], m + 1)
                        nc.scalar.copy(msgT[:, q, :], pB[q % 2][:, 0:P]).then_inc(s["hT_ready"], 1)
                        act.wait_ge(s["qkv_done"], m + 1 + U)
                        nc.scalar.copy(qs[:, q, :], pC[q % 2][:, 0:D]).then_inc(s["q_ready"], 1)
                        act.wait_ge(s["att_ready"], m + 1)
                        nc.scalar.activation(pay[:, q, D:PAY], attc[:, q, :], ACT.Exp).then_inc(s["exp_ready"], 1)
                    act.wait_ge(s["sum_done"], n + 1 + U)
                    act.wait_ge(scattered[q], SCATTERS * a + 16 * t)
                    w = PAY if k == CONV_RES else D
                    nc.scalar.copy(summed[:, q, 0:w], pA[q % 2][:, 0:w]).then_inc(s["sum_used"], 1)

            def fast_hi(k, n, u, it):
                live, b, q, at0 = batch(n, u, it)
                if live and k in CONVS:
                    if isinstance(b, int):
                        act.wait_ge(raw_in[q], 16 * U * (b // S4 + 1 + raw_before(k, q)))
                    else:
                        act.wait_ge(raw_in[q], 16 * U * (it + (u + AHEAD) // S4 + 1 + raw_before(k, q)))
                    after(act, "f_agg", k, b, RB - BACK)
                    nc.scalar.copy(ring[:, bass.ds(at0, U), 0:D], raw[:, q]).then_inc(s["f_hi"], 1)

            def fast_mid(k, n, u, it):
                live, b, q, at0 = batch(n, u, it)
                if live and k in CONVS:
                    after(act, "f_rest", k, b)
                    nc.scalar.copy(ring[:, bass.ds(at0, U), D:2 * D], rest[:, q % 2]).then_inc(s["f_mid"], 1)

            def fast(k, n, u, it):
                fast_hi(k, n, u, it)
                r = x_part(k) + 1
                live, m, q, turn = at(n, u, it, r)
                if live and k in LN_RELU + ROUNDS:
                    after(act, "f_var", k, m)
                    nc.scalar.activation(std[:, q, :], var[:, q, :], ACT.Sqrt).then_inc(s["f_std"], 1)
                live, m, q, turn = at(n, u, it, 1)
                if live and k in CONVS:
                    after(act, "f_trans", k, m)
                    after(act, "f_mm", k, m, 2)
                    nc.scalar.copy(aT[:, q % 2, :], pA[q % 2][:]).then_inc(s["f_evac"], 1)
                fast_mid(k, n, u, it)
                if k == CONV_GATE:
                    live, m, q, turn = at(n, u, it, 3)
                    if live:
                        after(act, "f_gtr", k, m)
                        after(act, "f_gmm", k, m, 1)
                        nc.scalar.copy(hhT[:, 0:HB, :].rearrange("p a b -> p (a b)"), pD[0][:])
                        nc.scalar.copy(hhT[:, HB:GB, :].rearrange("p a b -> p (a b)"), pD[1][:]).then_inc(s["f_gev"], 1)
                    live, m, q, turn = at(n, u, it, 4)
                    if live:
                        after(act, "f_gin", k, m)
                        nc.scalar.activation(gate[:, q % 2, :], gate[:, q % 2, :], ACT.Sigmoid).then_inc(s["f_gate"], 1)
                live, m, q, turn = at(n, u, it, r)
                if live and k in KINDS["f_pre"]:
                    after(act, "f_pre", k, m)
                    landed(act, st_t, T_STORES, k, m, q, turn, lag=S4)
                    for j in range(GB):
                        ins = nc.scalar.mul(tnew[:, q, j * D:(j + 1) * D], xc[:, q, j * D:(j + 1) * D], dinv[:, bass.ds(m * GB + j, 1)])
                    ins.then_inc(s["f_out"], 1)
                live, m, q, turn = at(n, u, it, x_part(k))
                if live and k in LN_RELU + ROUNDS:
                    after(act, "f_z" if k in ROUNDS else "f_sqin", k, m)
                    after(act, "f_var", k, m, 2)
                    nc.scalar.activation(sq[:, q % 2, :], (z if k in ROUNDS else xc)[:, q, :], ACT.Square).then_inc(s["f_sq"], 1)

            act.sem_inc(s["sum_used"], U)
            act.wait_ge(s["flag_ready"], 1)
            even = act.value_load(flag[0:1, 0:1], min_val=0, max_val=1)
            with act.If(even == 1):
                for k in range(10):
                    if k in CONVS:
                        for b in range(AHEAD):
                            fast_hi(k, b - AHEAD, b - AHEAD, 0)
                            fast_mid(k, b - AHEAD, b - AHEAD, 0)
                    steps(act, k, fast)
                    if k == CONV_RES:
                        with act.Fori(0, NIT) as t:
                            edge(k, 0, t)
            with act.Else():
              for k in range(10):
                with act.Fori(0, NG // 2) as h:
                    for u in range(2):
                        step(k, h, u)
                if k != LAST:
                    with act.Fori(0, NIT) as t:
                        edge(k, k, t)

        @block.vector
        def _(dve):
            links = [0]

            def link(ins, name="dchain"):
                links[0] += 1
                ins.then_inc(s[name], 1)
                dve.wait_ge(s[name], links[0])

            nc.vector.memset(zeros[:], 0.0)
            nc.vector.memset(wqkv[:], 0.0)
            nc.vector.memset(wround[:], 0.0)
            nc.vector.memset(wgp[:], 0.0)
            nc.vector.memset(wsb[:], 0.0).then_inc(s["zero_ready"], 1)
            dve.wait_ge(s["iota"], 6)
            link(nc.vector.tensor_copy(spare[:], bits[:, 0, 0:1]))
            dve.wait_ge(s["const_in"], 16 * 17)
            for k in ("src", "dst"):
                link(nc.vector.tensor_copy(keyf[k][:], key[k][:]))
                link(nc.vector.tensor_scalar(row[k][:], key[k][:], 10, 10, ALU.logical_shift_right, ALU.logical_shift_left))
                link(nc.vector.tensor_scalar(bits[:, 0, :], key[k][:], P - 1, 3, ALU.bitwise_and, ALU.logical_shift_left))
                link(nc.vector.tensor_tensor(row[k][:], row[k][:], bits[:, 0, :], ALU.bitwise_or))
                link(nc.vector.tensor_scalar(bits[:, 0, :], key[k][:], 7, GB - 1, ALU.logical_shift_right, ALU.bitwise_and))
                link(nc.vector.tensor_tensor(row[k][:], row[k][:], bits[:, 0, :], ALU.bitwise_or))
                link(nc.vector.tensor_scalar(row[k][:], row[k][:], NROW - 1, None, ALU.min))
                link(nc.vector.tensor_scalar(rowm[k][:], row[k][:], spare[:, 0:1], None, ALU.subtract))
            link(nc.vector.tensor_scalar(bits[:, 0, :], key["dst"][:], P - 1, None, ALU.bitwise_and))
            link(nc.vector.tensor_scalar(bits[:, 1, :], key["dst"][:], 7, None, ALU.logical_shift_right))
            link(nc.vector.tensor_copy(lo[:], bits[:, 0, :]))
            link(nc.vector.tensor_copy(hi[:], bits[:, 1, :]))

            def onehots(t):
                for q in range(U):
                    n = t * U + q
                    dve.wait_ge(s["oh_used"], n + 1)
                    nc.vector.tensor_scalar(onehot_lo[:, q, :], iota_b[:, 0:P], lo[:, bass.ds(n, 1)], None, ALU.is_equal).then_inc(s["oh_ready"], 1)
                    nc.vector.tensor_scalar(onehot_hi[:, q, :], iota_b[:], hi[:, bass.ds(n, 1)], None, ALU.is_equal).then_inc(s["oh_ready"], 1)
            with dve.Fori(0, NIT) as t:
                onehots(t)
            dve.wait_ge(s["root_done"], 2)
            for h in range(2):
                cols = slice(h * NBLK // 2, (h + 1) * NBLK // 2)
                ins = nc.vector.tensor_copy(size[:, cols], pA[h][:, 0:NBLK // 2])
            ins.then_inc(s["c1"], 1)
            dve.wait_ge(s["c2"], 1)
            nc.vector.memset(hits[:], 1.0)
            for h in range(2):
                cols = slice(h * NBLK // 2, (h + 1) * NBLK // 2)
                ins = nc.vector.tensor_copy(size[:, cols], pB[h][:, 0:NBLK // 2])
            link(ins)
            link(nc.vector.tensor_tensor_scan(ends, hits[:, 0:NBLK], size, 0.0, ALU.mult, ALU.add))
            link(nc.vector.tensor_tensor(ends, ends, size, ALU.subtract))
            link(nc.vector.tensor_copy(first_i[:], ends))
            link(nc.vector.tensor_scalar(first_i[:], first_i[:], 7, None, ALU.logical_shift_right))
            link(nc.vector.tensor_copy(first[:], first_i[:]))
            dve.wait_ge(s["row_in"], 16 * 5)
            link(nc.vector.tensor_copy(rowlayf, rowlay))
            for k in range(2):
                if k:
                    dve.wait_ge(s["oht_used"], 1)
                    link(nc.vector.tensor_scalar(tiles_p[:], tiles_p[:], -1.0, None, ALU.add))
                for c in range(4):
                    nc.vector.tensor_scalar(onehot_tile[c], first[:], tiles_p[:, c:c + 1], None, ALU.is_equal).then_inc(s["oht_ready"], 1)
            dve.wait_ge(s["oht_used"], 2)
            for k in range(2):
                for h in range(2):
                    cols = slice(h * NBLK // 2, (h + 1) * NBLK // 2)
                    ins = nc.vector.tensor_tensor(dloc[:, k, cols], (pC, pD)[k][h][:, 0:NBLK // 2], base_of[:, cols], ALU.subtract)
            link(ins)
            flat = dloc[:].rearrange("p k b -> p (k b)")
            link(nc.vector.tensor_scalar(hits, flat, 0.0, None, ALU.is_ge))
            link(nc.vector.scalar_tensor_tensor(hits2, flat, float(P), hits, ALU.is_lt, ALU.mult))
            link(nc.vector.tensor_reduce(checks[:, 0:1], hits2, AX_X, ALU.add))
            link(nc.vector.tensor_tensor(size, first[:], tile0[:], ALU.subtract))
            link(nc.vector.tensor_scalar(hits[:, 0:NBLK], size, float(U * (AHEAD - 1) + U - 2), None, ALU.is_gt))
            link(nc.vector.tensor_scalar(hits[:, NBLK:2 * NBLK], size, float(-U * BACK), None, ALU.is_lt))
            nc.vector.tensor_reduce(checks[:, 1:2], hits, AX_X, ALU.add).then_inc(s["c1"], 1)
            dve.wait_ge(s["c2"], 2)
            link(nc.vector.tensor_copy(checks[:, 0:2], pA[0][:, 0:2]))
            link(nc.vector.tensor_scalar(checks[:, 2:3], checks[:, 0:1], float(N_EDGES), None, ALU.is_equal))
            link(nc.vector.tensor_scalar(checks[:, 3:4], checks[:, 1:2], 0.0, checks[:, 2:3], ALU.is_equal, ALU.mult))
            spots = place[:].rearrange("o g c -> o (g c)").rearrange("o (b k) -> o b k", k=2)
            for k in range(2):
                if k:
                    link(nc.vector.tensor_scalar(first_i[0:1, :], first_i[0:1, :], 1, None, ALU.add))
                link(nc.vector.tensor_scalar(base_of[0:1, :].bitcast(I32), first_i[0:1, :], RB * U - 1, None, ALU.bitwise_and))
                link(nc.vector.tensor_scalar(spots[:, :, k], base_of[0:1, :].bitcast(I32), MW, None, ALU.mult))
            nc.vector.tensor_copy(flag[:], checks[0:1, 3:4]).then_inc(s["flag_ready"], 1)
            with dve.Fori(0, NG // 2) as h:
                for u in range(2):
                    dve.wait_ge(sel_out[u], h * 16)
                    nc.vector.tensor_tensor(sel[:, u].rearrange("p (b k) n -> p k b n", k=2),
                                            dloc[:, :, bass.ds((h * 2 + u) * GB, GB)].unsqueeze(3).to_broadcast([P, 2, GB, P]),
                                            iota_b[:, 0:P].unsqueeze(1).unsqueeze(1).to_broadcast([P, 2, GB, P]), ALU.is_equal).then_inc(s["sel_made"], 1)
            for h in range(2):
                rows = slice(h * D, (h + 1) * D)
                link(nc.vector.tensor_reduce(wmean[rows, 0:1], wround[rows, rows], AX_X, ALU.add))
                link(nc.vector.tensor_scalar(wmean[rows, 1:2], wmean[rows, 0:1], 1.0 / D, None, ALU.mult))
            link(nc.vector.tensor_copy(wcent[:], wround[:]))
            for h in range(2):
                rows = slice(h * D, (h + 1) * D)
                link(nc.vector.tensor_scalar(wcent[rows, rows], wround[rows, rows], wmean[rows, 1:2], None, ALU.subtract))
            link(nc.vector.tensor_reduce(wmean[:, 0:1], bsb[:, BIAS[ROUND_A], :], AX_X, ALU.add))
            link(nc.vector.tensor_scalar(wmean[:, 1:2], wmean[:, 0:1], 1.0 / D, None, ALU.mult))
            nc.vector.tensor_scalar(bcent[:], bsb[:, BIAS[ROUND_A], :], wmean[:, 1:2], None, ALU.subtract).then_inc(s["fast_wt"], 1)
            dve.wait_ge(s["fast_wt"], 1)
            dve.wait_ge(s["root_done"], 2)
            nc.vector.reciprocal(dinv[:], root[:]).then_inc(s["norm_done"], 1)
            dve.wait_ge(s["norm_done"], 1)

            def step(k, h, u):
                base = links_before(k) + (h * 2 + u) * LINKS[k]
                n = h * 2 + u
                g = n
                made = [0]

                def link(ins):
                    made[0] += 1
                    ins.then_inc(s["chain"], 1)
                    dve.wait_ge(s["chain"], base + made[0])

                dve.wait_ge(loaded[u], loads_before(k) + 16 * n_loads(k) * (h + 1))
                zt, xct = b3(z[:, u, :]), b3(xc[:, u, :])
                x_in = b3(xt[:, u, :])
                if k in CONVS:
                    dve.wait_ge(s["y_ready"], before(k, CONVS) + n + 1 + 2)
                    ins = nc.vector.tensor_tensor(zt, b3(pB[u][:]), col(dinv, g), ALU.mult)
                    link(ins)
                    ins = nc.vector.tensor_tensor(zt, zt, vec(BIAS[k]), ALU.add)
                    link(ins)
                ln_in = None
                def out_free():
                    dve.wait_ge(stored_t[u], tstores_before(k) + 16 * n_tstores(k) * h)

                def x_free():
                    dve.wait_ge(stored_x[u], xstores_before(k) + 16 * h)

                if k in (CONV_A, CONV_B):
                    out_free()
                    nc.vector.scalar_tensor_tensor(b3(tnew[:, u, :]), zt, 0.0, col(dinv, g), ALU.max, ALU.mult).then_inc(s["t_ready"], 1)
                if k == CONV_GATE:
                    h0 = cat[:, u, :, 1, :]
                    hh = cat[:, u, :, 0, :]
                    link(nc.vector.tensor_tensor(h0, b3(t0[:, u, :]), col(root, g), ALU.mult))
                    nc.vector.scalar_tensor_tensor(hh, zt, 0.0, h0, ALU.max, ALU.add).then_inc(s["cat_ready"], 1)
                    dve.wait_ge(s["g_ready"], n + 1 + 1)
                    nc.vector.tensor_tensor(b3(gate[:, u, :]), b3(pD[u][:]), vec(B_GATE), ALU.add).then_inc(s["gate_ready"], 1)
                    dve.wait_ge(s["gate_ready"], n * 2 + 2)
                    link(nc.vector.tensor_tensor(zt, hh, b3(gate[:, u, :]), ALU.mult))
                    x_free()
                    ins = nc.vector.tensor_tensor(b3(xnew[:, u, :]), zt, x_in, ALU.add)
                if k == CONV_RES:
                    x_free()
                    ins = nc.vector.scalar_tensor_tensor(b3(xnew[:, u, :]), zt, 0.0, x_in, ALU.max, ALU.add)
                if k == ATT_RES:
                    pin = pay_in[:, u, :].rearrange("p (s c) -> p s c", s=GB)
                    link(nc.vector.tensor_scalar(rden[:, u, :, :], pin[:, :, D:PAY], 1e-8, None, ALU.add))
                    link(nc.vector.reciprocal(rden[:, u, :, :], rden[:, u, :, :]))
                    for hd in range(HEADS):
                        ins = nc.vector.tensor_tensor(zt[:, :, hd * DH:(hd + 1) * DH], pin[:, :, hd * DH:(hd + 1) * DH],
                                                      rden[:, u, :, hd:hd + 1].to_broadcast([P, GB, DH]), ALU.mult)
                    link(ins)
                    x_free()
                    ins = nc.vector.tensor_tensor(b3(xnew[:, u, :]), zt, x_in, ALU.add)
                if k in WRITES_X:
                    ins.then_inc(s["x_ready"], 1)
                    dve.wait_ge(s["x_ready"], before(k, WRITES_X) + n + 1)
                ln = {FIRST: x_in, LAST: zt, ROUND_A: zt, ROUND_B: zt, ROUND_C: zt}.get(k, b3(xnew[:, u, :]))
                if k in LN_RELU or k in ROUNDS:
                    c = before(k, LN_RELU + ROUNDS) + n
                    m, v, sd, r = mean[:, u, :], var[:, u, :], std[:, u, :], rstd[:, u, :]
                    link(nc.vector.tensor_reduce(m, ln, AX_X, ALU.add))
                    link(nc.vector.tensor_scalar(m, m, 1.0 / D, None, ALU.mult))
                    nc.vector.tensor_tensor(xct, ln, spread(m), ALU.subtract).then_inc(s["sq_ready"], 1)
                    dve.wait_ge(s["std_ready"], 2 * c + 1)
                    link(nc.vector.tensor_reduce(v, b3(sq[:, u, :]), AX_X, ALU.add))
                    nc.vector.tensor_scalar(v, v, 1.0 / D, 1e-5, ALU.mult, ALU.add).then_inc(s["sq_ready"], 1)
                    dve.wait_ge(s["std_ready"], 2 * c + 2)
                    link(nc.vector.reciprocal(r, sd))
                if k in LN_RELU:
                    if k != CONV_RES:
                        link(nc.vector.tensor_tensor(r, r, dinv[:, bass.ds(g * GB, GB)], ALU.mult))
                    out_free()
                    nc.vector.scalar_tensor_tensor(b3(tnew[:, u, :]), xct, 0.0, spread(r), ALU.max, ALU.mult).then_inc(s["t_ready"], 1)
                if k in ROUNDS:
                    link(nc.vector.tensor_tensor(xct, xct, spread(r), ALU.mult))
                    link(nc.vector.tensor_tensor(xct, xct, vec(B_GAMMA), ALU.mult))
                    link(nc.vector.tensor_tensor(xct, xct, vec(B_BETA), ALU.add))
                    out_free()
                    last = col(dinv, g) if k != LAST else x_in
                    nc.vector.tensor_tensor(b3(tnew[:, u, :]), xct, last, ALU.mult if k != LAST else ALU.add).then_inc(s["t_ready"], 1)
                while made[0] < LINKS[k]:
                    made[0] += 1
                    dve.sem_inc(s["chain"], 1)
                assert made[0] == LINKS[k], (k, made[0])
                dve.wait_ge(s["t_ready"], NG * k + n + 3)

            elinks = {CONV_RES: 8}

            def edge(k, a, t):
                kind = "src" if k == CONV_RES else "dst"
                EL = elinks.get(k, 3)
                for q in range(U):
                    n = U * t + q
                    made = [0]
                    base = a * NT * 3 + (NT * 5 if a > CONV_RES else 0) + n * EL

                    def link(ins):
                        made[0] += 1
                        ins.then_inc(s["echain"], 1)
                        dve.wait_ge(s["echain"], base + made[0])

                    c = bass.ds(n, 1)
                    dve.wait_ge(krow_in[q], SCATTERS * a + 16 * (t + 1))
                    dve.wait_ge(s["sum_done"], NT * a + n + 1)
                    dve.wait_ge(scattered[q], SCATTERS * a + 16 * t)
                    link(nc.vector.tensor_scalar(eq[:, q, :], krow[:, q, :], keyf[kind][:, c], None, ALU.is_equal))
                    link(nc.vector.tensor_tensor_reduce(junk[:], eq[:, q, :], lower[:], 1.0, 0.0, ALU.mult, ALU.add, cnt[:, q:q + 1]))
                    link(nc.vector.tensor_scalar(pos[:, q:q + 1], cnt[:, q:q + 1], 0.0, rowm[kind][:, c], ALU.is_equal, ALU.mult))
                    nc.vector.tensor_scalar(idx_s[:, q:q + 1], pos[:, q:q + 1], spare[:, 0:1], None, ALU.add)
                    if k == CONV_RES:
                        nc.vector.tensor_copy(idx_g[:, q, 1:2], row["dst"][:, c])
                    nc.vector.tensor_copy(idx_g[:, q, 0:1], row["src"][:, c]).then_inc(s["idx_ready"], 1)
                    if k == CONV_RES:
                        dve.wait_ge(s["q_ready"], n + 1)
                        link(nc.vector.tensor_tensor(qk[:, q, :], qs[:, q, :], pC[q % 2][:, D:2 * D], ALU.mult))
                        link(nc.vector.tensor_reduce(att[:, q, :], qk[:, q, :].rearrange("p (h d) -> p h d", h=HEADS), AX_X, ALU.add))
                        nc.vector.tensor_scalar(attc[:, q, :], att[:, q, :], -10.0, 10.0, ALU.max, ALU.min).then_inc(s["att_ready"], 1)
                        dve.wait_ge(s["exp_ready"], n + 1)
                        nc.vector.tensor_tensor(pay[:, q, 0:D].rearrange("p (h d) -> p h d", h=HEADS),
                                                pC[q % 2][:, 2 * D:3 * D].rearrange("p (h d) -> p h d", h=HEADS),
                                                pay[:, q, D:PAY].unsqueeze(2).to_broadcast([P, HEADS, DH]), ALU.mult).then_inc(s["pay_ready"], 1)
                        while made[0] < EL:
                            made[0] += 1
                            dve.sem_inc(s["echain"], 1)

            dve.sem_inc(s["idx_ready"], U)
            dve.sem_inc(s["t_ready"], 2)
            dve.wait_ge(s["mask"], 4)
            def fast_rest(k, n, u, it):
                live, b, q, at0 = batch(n, u, it)
                if live and k in CONVS:
                    after(dve, "f_hi", k, b)
                    after(dve, "f_split", k, b, 2)
                    nc.vector.tensor_tensor(rest[:, q % 2], raw[:, q], ring[:, bass.ds(at0, U), 0:D], ALU.subtract).then_inc(s["f_rest"], 1)

            def fast_lo(k, n, u, it):
                live, b, q, at0 = batch(n, u, it)
                if live and k in CONVS:
                    after(dve, "f_mid", k, b)
                    nc.vector.tensor_tensor(ring[:, bass.ds(at0, U), 2 * D:3 * D], rest[:, q % 2], ring[:, bass.ds(at0, U), D:2 * D], ALU.subtract).then_inc(s["f_split"], 1)

            def linker(name, k, m, per):
                made = [0]
                start = CHAINS[name](k) + m * per

                def link(ins):
                    made[0] += 1
                    assert made[0] <= per
                    ins.then_inc(s[name], 1)
                    dve.wait_ge(s[name], start + made[0])
                return link

            Z_LINKS = {CONV_A: 2, CONV_B: 2, CONV_GATE: 3, CONV_RES: 2, ATT_RES: 3, ROUND_A: 1, ROUND_B: 1, ROUND_C: 1, LAST: 1}
            X_LINKS = {k: 3 if k == CONV_GATE else 2 for k in LN_RELU}
            N_LINKS = {k: 2 for k in LN_RELU} | {CONV_RES: 1} | {k: 3 for k in ROUNDS} | {LAST: 4}
            CHAINS = {"chz": lambda k: NG * sum(Z_LINKS.get(j, 0) for j in range(k)),
                      "chx": lambda k: NG * sum(X_LINKS.get(j, 0) for j in range(k)),
                      "chr": lambda k: NG * sum(1 for j in range(k) if j in LN_RELU + ROUNDS),
                      "chn": lambda k: NG * sum(N_LINKS.get(j, 0) for j in range(k))}

            def fast(k, n, u, it):
                fast_rest(k, n, u, it)
                live, m, q, turn = at(n, u, it, x_part(k) + 1)
                if live and k in LN_RELU + ROUNDS:
                    link = linker("chr", k, m, 1)
                    after(dve, "f_sq", k, m)
                    after(dve, "f_std", k, m, S4)
                    link(nc.vector.tensor_reduce(var[:, q, :], b3(sq[:, q % 2, :]), AX_X, ALU.add))
                    nc.vector.tensor_scalar(var[:, q, :], var[:, q, :], 1.0 / D, 1e-5, ALU.mult, ALU.add).then_inc(s["f_var"], 1)
                live, m, q, turn = at(n, u, it, 0)
                if live and k in CONVS:
                    after(dve, "f_agg", k, m)
                    after(dve, "f_trans", k, m, 2)
                    landed(dve, own_in, OWN_LOADS, k, m, q, turn)
                    nc.vector.tensor_tensor(asum[:, q % 2, :], pC[q % 2][:], own[:, q, :], ALU.add).then_inc(s["f_add"], 1)
                live, m, q, turn = at(n, u, it, x_part(k) + 1)
                if live and k in LN_RELU + ROUNDS:
                    link = linker("chn", k, m, N_LINKS[k])
                    r = rstd[:, q, :]
                    after(dve, "f_std", k, m)
                    link(nc.vector.reciprocal(r, std[:, q, :]))
                    if k in LN_RELU:
                        if k != CONV_RES:
                            link(nc.vector.tensor_tensor(r, r, dinv[:, bass.ds(m * GB, GB)], ALU.mult))
                        landed(dve, st_t, T_STORES, k, m, q, turn, lag=S4)
                        nc.vector.scalar_tensor_tensor(b3(tnew[:, q, :]), b3(xc[:, q, :]), 0.0, spread(r), ALU.max, ALU.mult).then_inc(s["f_out"], 1)
                    else:
                        if k != LAST:
                            after(dve, "f_out", k, m, S4)
                        link(nc.vector.tensor_tensor(b3(xc[:, q, :]), b3(z[:, q, :]), spread(r), ALU.mult))
                        link(nc.vector.tensor_tensor(b3(xc[:, q, :]), b3(xc[:, q, :]), vec(B_GAMMA), ALU.mult))
                        ins = nc.vector.tensor_tensor(b3(xc[:, q, :]), b3(xc[:, q, :]), vec(B_BETA), ALU.add)
                        if k == LAST:
                            link(ins)
                            landed(dve, x_in, X_LOADS, k, m, q, turn)
                            landed(dve, st_t, T_STORES, k, m, q, turn, lag=S4)
                            nc.vector.tensor_tensor(tnew[:, q, :], xc[:, q, :], xt[:, q, :], ALU.add).then_inc(s["f_out"], 1)
                        else:
                            ins.then_inc(s["f_pre"], 1)
                fast_lo(k, n, u, it)
                live, m, q, turn = at(n, u, it, 2)
                if live and k in CONVS:
                    link = linker("chz", k, m, Z_LINKS[k])
                    zt = b3(z[:, q, :])
                    after(dve, "f_mm", k, m)
                    if k in ROUNDS:
                        after(dve, "f_sq", k, m, S4)
                    link(nc.vector.tensor_tensor(zt, b3(y_bank(k, q)[:]), col(dinv, m), ALU.mult))
                    if k in ROUNDS:
                        nc.vector.tensor_tensor(zt, zt, bcent[:].unsqueeze(1).to_broadcast([P, GB, D]), ALU.add).then_inc(s["f_z"], 1)
                    else:
                        link(nc.vector.tensor_tensor(zt, zt, vec(BIAS[k]), ALU.add))
                    if k in (CONV_A, CONV_B):
                        landed(dve, st_t, T_STORES, k, m, q, turn, lag=S4)
                        nc.vector.scalar_tensor_tensor(b3(tnew[:, q, :]), zt, 0.0, col(dinv, m), ALU.max, ALU.mult).then_inc(s["f_out"], 1)
                    if k == CONV_GATE:
                        landed(dve, t0_in, T0_LOADS, k, m, q, turn)
                        after(dve, "f_gtr", k, m, S4)
                        link(nc.vector.tensor_tensor(b3(h0[:, q, :]), b3(t0[:, q, :]), col(root, m), ALU.mult))
                        nc.vector.scalar_tensor_tensor(hh[:, q, :], z[:, q, :], 0.0, h0[:, q, :], ALU.max, ALU.add).then_inc(s["f_cat"], 1)
                if k == CONV_GATE:
                    live, m, q, turn = at(n, u, it, 4)
                    if live:
                        after(dve, "f_gmm", k, m)
                        nc.vector.tensor_tensor(b3(gate[:, q % 2, :]), b3(pG[:]), vec(B_GATE), ALU.add).then_inc(s["f_gin"], 1)
                live, m, q, turn = at(n, u, it, x_part(k))
                if live and k in LN_RELU:
                    link = linker("chx", k, m, X_LINKS[k])
                    landed(dve, x_in, X_LOADS, k, m, q, turn, each=X_LOADS[k])
                    if k in WRITES_X:
                        landed(dve, st_x, X_STORES, k, m, q, turn, lag=S4)
                    if k == CONV_GATE:
                        after(dve, "f_gate", k, m)
                        link(nc.vector.tensor_tensor(hh[:, q, :], hh[:, q, :], gate[:, q % 2, :], ALU.mult))
                        nc.vector.tensor_tensor(xnew[:, q, :], hh[:, q, :], xt[:, q, :], ALU.add).then_inc(s["f_x"], 1)
                    if k == CONV_RES:
                        nc.vector.scalar_tensor_tensor(xnew[:, q, :], z[:, q, :], 0.0, xt[:, q, :], ALU.max, ALU.add).then_inc(s["f_x"], 1)
                    if k == ATT_RES:
                        lz = linker("chz", k, m, Z_LINKS[k])
                        pin = pay_in[:, q, :].rearrange("p (s c) -> p s c", s=GB)
                        lz(nc.vector.tensor_scalar(rden[:, q, :, :], pin[:, :, D:PAY], 1e-8, None, ALU.add))
                        lz(nc.vector.reciprocal(rden[:, q, :, :], rden[:, q, :, :]))
                        for hd in range(HEADS):
                            ins = nc.vector.tensor_tensor(b3(z[:, q, :])[:, :, hd * DH:(hd + 1) * DH], pin[:, :, hd * DH:(hd + 1) * DH],
                                                          rden[:, q, :, hd:hd + 1].to_broadcast([P, GB, DH]), ALU.mult)
                        lz(ins)
                        nc.vector.tensor_tensor(xnew[:, q, :], z[:, q, :], xt[:, q, :], ALU.add).then_inc(s["f_x"], 1)
                    if k in WRITES_X:
                        after(dve, "f_x", k, m)
                    xn = b3((xt if k == FIRST else xnew)[:, q, :])
                    link(nc.vector.tensor_reduce(mean[:, q, :], xn, AX_X, ALU.add))
                    link(nc.vector.tensor_scalar(mean[:, q, :], mean[:, q, :], 1.0 / D, None, ALU.mult))
                    after(dve, "f_out", k, m, S4)
                    nc.vector.tensor_tensor(b3(xc[:, q, :]), xn, spread(mean[:, q, :]), ALU.subtract).then_inc(s["f_sqin"], 1)

            dve.wait_ge(s["flag_ready"], 1)
            even = dve.value_load(flag[0:1, 0:1], min_val=0, max_val=1)
            with dve.If(even == 1):
                for k in range(10):
                    if k in CONVS:
                        for b in range(AHEAD):
                            fast_rest(k, b - AHEAD, b - AHEAD, 0)
                            fast_lo(k, b - AHEAD, b - AHEAD, 0)
                    steps(dve, k, fast)
                    if k == CONV_RES:
                        with dve.Fori(0, NIT) as t:
                            edge(k, 0, t)
            with dve.Else():
              for k in range(10):
                with dve.Fori(0, NG // 2) as h:
                    for u in range(2):
                        step(k, h, u)
                if k != LAST:
                    with dve.Fori(0, NIT) as t:
                        edge(k, k, t)

        @block.tensor
        def _(pe):
            pe.sem_inc(s["trans_done"], 2)
            pe.sem_inc(s["y_ready"], 2)
            pe.sem_inc(s["g_ready"], 1)
            pe.sem_inc(s["sum_done"], U)
            pe.sem_inc(s["qkv_done"], U)
            pe.sem_inc(s["oh_used"], U)

            def count(t, start=False, stop=False):
                for q in range(U):
                    n = t * U + q
                    pe.wait_ge(s["oh_ready"], 2 * n + 2)
                    for hf in range(2):
                        ins = nc.tensor.matmul(pA[hf][:, 0:NBLK // 2], onehot_lo[:, q, :], onehot_hi[:, q, hf * NBLK // 2:(hf + 1) * NBLK // 2],
                                               start=start and q == 0, stop=stop and q == U - 1, skip_group_check=True)
                    ins.then_inc(s["oh_used"], 1)
                if stop:
                    pe.wait_ge(s["oh_used"], NT + U)
                    pe.sem_inc(s["deg_done"], 1)
            count(0, start=True)
            with pe.Fori(1, NIT - 1) as t:
                count(t)
            count(NIT - 1, stop=True)
            pe.wait_ge(s["mask"], 4)
            pe.wait_ge(s["const_in"], 16 * 17)

            def step(k, h, u):
                n = h * 2 + u
                if k not in CONVS:
                    return
                c = before(k, CONVS)
                w = wround[:] if k in ROUNDS else wsb[:, BIAS[k], :]
                pe.wait_ge(loaded[u], loads_before(k) + 16 * n_loads(k) * (h + 1))
                for j in range(HB):
                    ins = nc.tensor.transpose(pA[u][:, j * P:(j + 1) * P], own[:, u, j * P:(j + 1) * P], ident[:])
                ins.then_inc(s["trans_done"], 1)
                pe.wait_ge(s["aT_ready"], c + n + 1)
                pe.wait_ge(s["t_ready"], NG * k + n + 1)
                for j in range(HB):
                    ins = nc.tensor.matmul(pB[u][:, j * P:(j + 1) * P], aT[:, u, j * P:(j + 1) * P], w, start=True, stop=True)
                ins.then_inc(s["y_ready"], 1)
                if k == CONV_GATE:
                    pe.wait_ge(s["cat_ready"], n + 1)
                    for j in range(GB):
                        ins = nc.tensor.transpose(pC[j // HB][:, (j % HB) * P:(j % HB + 1) * P], cat[:, u, j, :, :].rearrange("p a d -> p (a d)"), ident[:])
                    ins.then_inc(s["catT_psum"], 1)
                    pe.wait_ge(s["catT_ready"], n * 2 + 2)
                    for j in range(GB):
                        ins = nc.tensor.matmul(pD[u][:, j * D:(j + 1) * D], catT[:, u, j, :], wgate[:], start=True, stop=True)
                    ins.then_inc(s["g_ready"], 1)

            def edge(k, a, t):
                for q in range(U):
                    m = U * t + q
                    n = NT * a + m
                    c = 1 if a > CONV_RES else 0
                    pe.wait_ge(gathered[q], 16 * NIT * (a + c) + (t + 1) * (32 if k == CONV_RES else 16))
                    pe.wait_ge(s["idx_ready"], n + 1 + U)
                    if k == CONV_RES:
                        nc.tensor.transpose(pB[q % 2][:, 0:P], msg[:, q, :], ident[:]).then_inc(s["hT_done"], 1)
                        pe.wait_ge(s["hT_ready"], m + 1)
                        nc.tensor.matmul(pC[q % 2][:, 0:3 * D], msgT[:, q, :], wqkv[:], start=True, stop=True).then_inc(s["qkv_done"], 1)
                        pe.wait_ge(s["pay_ready"], m + 1)
                    w = PAY if k == CONV_RES else D
                    pe.wait_ge(s["sum_used"], n + U - 1)
                    nc.tensor.matmul(pA[q % 2][:, 0:w], eq[:, q, :], pay[:, q, :] if k == CONV_RES else msg[:, q, 0:D],
                                     start=True, stop=True).then_inc(s["sum_done"], 1)

            pe.wait_ge(s["c1"], 1)
            for h in range(2):
                ins = nc.tensor.matmul(pB[h][:, 0:NBLK // 2], ones[:], size[:, h * NBLK // 2:(h + 1) * NBLK // 2], start=True, stop=True)
            ins.then_inc(s["c2"], 1)
            for k in range(2):
                for c in range(4):
                    pe.wait_ge(s["oht_ready"], 4 * k + c + 1)
                    for h in range(2):
                        ins = nc.tensor.matmul((pC, pD)[k][h][:, 0:NBLK // 2], rowlayf[:, c * P:(c + 1) * P],
                                               onehot_tile[c][0:TP, h * NBLK // 2:(h + 1) * NBLK // 2], start=c == 0, stop=c == 3)
                ins.then_inc(s["oht_used"], 1)
            pe.wait_ge(s["c1"], 2)
            pe.wait_ge(s["root_done"], 2)
            nc.tensor.matmul(pA[0][:, 0:2], ones[:], checks[:, 0:2], start=True, stop=True).then_inc(s["c2"], 1)

            spots = [pe.alloc_register(f"spot{j}") for j in range(2 * GB)]
            Y_USED = {CONV_A: "f_out", CONV_B: "f_out", CONV_GATE: "f_cat", CONV_RES: "f_x"} | {k: "f_z" for k in ROUNDS}
            columns = ring[:].rearrange("p t c -> p (t c)")

            def fast(k, n, u, it):
                live, m, q, turn = at(n, u, it, 0)
                if live and k in CONVS:
                    pe.load(spots, place[0:1, bass.ds(m, 1), :])
                    spot = [pe.snap(r, min_val=0, max_val=(RB * U - 1) * MW) for r in spots]
                    landed(pe, sel_in, OWN_LOADS, k, m, q, turn)
                    last = min(m + AHEAD - 1, NIT - 1) if isinstance(m, int) else m + (AHEAD - 1)
                    after(pe, "f_split", k, last)
                    after(pe, "f_add", k, m, 2)
                    for j in range(GB):
                        for e in range(2):
                            for part in range(PIECES):
                                ins = nc.tensor.matmul(pC[q % 2][:, j * D:(j + 1) * D], sel[:, q, 2 * j + e, :],
                                                       columns[:, bass.ds(spot[2 * j + e] + part * D, D)],
                                                       start=e == 0 and part == 0, stop=e == 1 and part == PIECES - 1)
                    ins.then_inc(s["f_agg"], 1)
                live, m, q, turn = at(n, u, it, 1)
                if live and k in CONVS:
                    after(pe, "f_add", k, m)
                    after(pe, "f_evac", k, m, 2)
                    for j in range(HB):
                        ins = nc.tensor.transpose(pA[q % 2][:, j * P:(j + 1) * P], asum[:, q % 2, j * P:(j + 1) * P], ident[:])
                    ins.then_inc(s["f_trans"], 1)
                live, m, q, turn = at(n, u, it, 2)
                if live and k in CONVS:
                    after(pe, "f_evac", k, m)
                    after(pe, Y_USED[k], k, m, 1 if k == CONV_GATE else 2)
                    y = y_bank(k, q)
                    w = wcent[:] if k in ROUNDS else wsb[:, BIAS[k], :]
                    for j in range(HB):
                        ins = nc.tensor.matmul(y[:, j * P:(j + 1) * P], aT[:, q % 2, j * P:(j + 1) * P], w, start=True, stop=True)
                    ins.then_inc(s["f_mm"], 1)
                if k == CONV_GATE:
                    live, m, q, turn = at(n, u, it, 3)
                    if live:
                        after(pe, "f_cat", k, m)
                        after(pe, "f_gev", k, m, 1)
                        for j in range(HB):
                            nc.tensor.transpose(pD[0][:, j * P:(j + 1) * P], hh[:, q, j * P:(j + 1) * P], ident[:])
                        for j in range(HB):
                            ins = nc.tensor.transpose(pD[1][:, j * P:(j + 1) * P], h0[:, q, j * P:(j + 1) * P], ident[:])
                        ins.then_inc(s["f_gtr"], 1)
                    live, m, q, turn = at(n, u, it, 4)
                    if live:
                        after(pe, "f_gev", k, m)
                        after(pe, "f_gin", k, m, 1)
                        for j in range(HB):
                            for part in range(2):
                                ins = nc.tensor.matmul(pG[:, j * P:(j + 1) * P], hhT[:, part * HB + j, :], wgp[:, part, :],
                                                       start=part == 0, stop=part == 1)
                        ins.then_inc(s["f_gmm"], 1)

            pe.wait_ge(s["flag_ready"], 1)
            even = pe.value_load(flag[0:1, 0:1], min_val=0, max_val=1)
            pe.wait_ge(s["fast_wt"], 1)
            pe.wait_ge(s["row_in"], 16 * 5)
            with pe.If(even == 1):
                for k in range(10):
                    if k in CONVS:
                        steps(pe, k, fast)
                    if k == CONV_RES:
                        with pe.Fori(0, NIT) as t:
                            edge(k, 0, t)
            with pe.Else():
              for k in range(10):
                if k in CONVS:
                    with pe.Fori(0, NG // 2) as h:
                        for u in range(2):
                            step(k, h, u)
                if k != LAST:
                    with pe.Fori(0, NIT) as t:
                        edge(k, k, t)


def kernel(**inputs):
    import numpy as np
    import concourse.bacc as _bacc
    from concourse import mybir as _mybir
    from concourse.bass_utils import run_bass_kernel_spmd as _run

    a = {k: np.asarray(v) for k, v in inputs.items()}
    x = np.zeros((NROW, D), a["x"].dtype)
    x[:N_NODES] = a["x"]
    x = np.ascontiguousarray(x.reshape(NG, GB, P, D).transpose(0, 2, 1, 3)).reshape(NROW, D)
    edges = {}
    for k in ("src", "dst"):
        e = np.full((NT * P,), PAD_KEY, a[k].dtype)
        e[:N_EDGES] = a[k]
        edges[k + "_row"] = e.reshape(NT, P)
        edges[k] = np.ascontiguousarray(e.reshape(NT, P).T)
    wt = np.concatenate([a["L0_gnn_W1"].T, a["L0_gnn_W2"].T, a["L1_gnn_W1"], a["L1_gnn_W2"], a["L3_gnn_W"],
                         a["L0_gnn_Wg"].T, a["L2_gnn_Wq"], a["L2_gnn_Wk"], a["L2_gnn_Wv"]], axis=0)
    bias = np.stack([a["L0_gnn_b1"], a["L0_gnn_b2"], a["L1_gnn_b1"], a["L1_gnn_b2"], a["L3_gnn_b"], a["L0_gnn_bg"],
                     a["L3_gnn_gamma"], a["L3_gnn_beta"]])
    arrays = {"x": x, "src": edges["src"], "dst": edges["dst"], "dst_row": edges["dst_row"], "src_row": edges["src_row"],
              "wt": np.ascontiguousarray(wt), "bias": np.ascontiguousarray(bias)}
    nc = _bacc.Bacc("TRN2", target_bir_lowering=False, num_devices=1)
    args = [nc.dram_tensor(f"in_{n}", v.shape, _mybir.dt.from_np(v.dtype), kind="ExternalInput").ap() for n, v in arrays.items()]
    out = nc.dram_tensor("out_dram", (NROW, D), F32, kind="ExternalOutput").ap()
    gnn_kernel(nc, *args, out)
    r = _run(nc, [{f"in_{n}": v for n, v in arrays.items()}], core_ids=[0])
    got = np.asarray(r.results[0]["out_dram"]).reshape(NG, P, GB, D).transpose(0, 2, 1, 3)
    return np.ascontiguousarray(got).reshape(NROW, D)[:N_NODES]
```

```python
from contextlib import ExitStack

import concourse.bass as bass
from concourse import mybir

ALU = mybir.AluOpType
ACT = mybir.ActivationFunctionType
AX_X = mybir.AxisListType.X
F32 = mybir.dt.float32
BF16 = mybir.dt.bfloat16
I32 = mybir.dt.int32

P = 128
D = 64
HEADS = 4
DH = D // HEADS
GB = 8
N_NODES = 100000
N_EDGES = 50000
NG = -(-N_NODES // (P * GB))
NG += -NG % 4
NROW = NG * P * GB
NBLK = NG * GB
U = 4
NT = -(-N_EDGES // P)
NT += -NT % U
NIT = NT // U
PAD_KEY = 1 << 20
PAY = D + HEADS
PT = 2
W2 = GB * D
HB = GB // 2
RB = 8
AHEAD = 3
BACK = 3
TP = NT // 4
S4 = 4
FULL = (NIT - AHEAD) // S4

(FIRST, CONV_A, CONV_GATE, CONV_B, CONV_RES, ATT_RES, ROUND_A, ROUND_B, ROUND_C, LAST) = range(10)
CONVS = (CONV_A, CONV_GATE, CONV_B, CONV_RES, ROUND_A, ROUND_B, ROUND_C, LAST)
ROUNDS = (ROUND_A, ROUND_B, ROUND_C, LAST)
READS_X = (FIRST, CONV_GATE, CONV_RES, ATT_RES, LAST)
WRITES_X = (CONV_GATE, CONV_RES, ATT_RES)
LN_RELU = (FIRST, CONV_GATE, CONV_RES, ATT_RES)
LINKS = {FIRST: 6, CONV_A: 2, CONV_GATE: 16, CONV_B: 2, CONV_RES: 9, ATT_RES: 9, ROUND_A: 10, ROUND_B: 10, ROUND_C: 10, LAST: 10}


def gnn_kernel(nc, x, src, dst, dst_row, src_row, wt, bias, out):
    with ExitStack() as ctx:
        def sb(name, shape, dt=F32):
            return ctx.enter_context(nc.sbuf_tensor(name, shape, dt))

        def ps(name, shape, dt=F32):
            return ctx.enter_context(nc.psum_tensor(name, shape, dt))

        def sem(name):
            return ctx.enter_context(nc.semaphore(name))

        table = [nc.dram_tensor(f"table{k}", [NROW, D], F32).ap() for k in range(10)]
        total = [nc.dram_tensor(f"total{k}", [NROW + P, D], F32).ap() for k in range(10)]
        sel_d = nc.dram_tensor("sel_d", [NG, P, 2 * GB * P], BF16).ap()
        payloads = [nc.dram_tensor(f"payload{q}", [NROW + P, PAY], F32).ap() for q in range(PT)]
        payload = payloads[0]
        xres = [nc.dram_tensor(f"xres{k}", [NROW, D], F32).ap() for k in range(3)]

        key = {"src": sb("src_key", [P, NT], I32), "dst": sb("dst_key", [P, NT], I32)}
        keyf = {k: sb(f"{k}_keyf", [P, NT]) for k in key}
        row = {k: sb(f"{k}_row", [P, NT], I32) for k in key}
        rowm = {k: sb(f"{k}_rowm", [P, NT]) for k in key}
        bits = sb("bits", [P, 2, NT], I32)
        lo = sb("lo", [P, NT])
        hi = sb("hi", [P, NT])
        spare = sb("spare", [P, 1])
        iota_b = sb("iota_b", [P, NBLK])
        ident = sb("ident", [P, P])
        lower = sb("lower", [P, P])
        onehot_lo = sb("onehot_lo", [P, U, P], BF16)
        root = sb("root", [P, NBLK])
        dinv = sb("dinv", [P, NBLK])
        wsb = sb("wsb", [P, 4, P])
        wround = sb("wround", [P, P])
        wgate = sb("wgate", [P, D])
        wqkv = sb("wqkv", [P, 3 * D])
        bsb = sb("bsb", [P, 8, D])
        zeros = sb("zeros", [P, GB * PAY])

        own = sb("own", [P, S4, W2])
        xt = sb("xt", [P, S4, W2])
        t0 = sb("t0", [P, S4, W2])
        pay_in = sb("pay_in", [P, S4, GB * PAY])
        onehot_hi = pay_in[:].rearrange("p a c -> p (a c)").bitcast(BF16)[:, 0:U * NBLK].rearrange("p (u b) -> p u b", u=U)
        aT = sb("aT", [P, 2, W2])
        z = sb("z", [P, S4, W2])
        sq = sb("sq", [P, 2, W2])
        xc = sb("xc", [P, S4, W2])
        gate = sb("gate", [P, 2, W2])
        xnew = sb("xnew", [P, S4, W2])
        tnew = sb("tnew", [P, S4, W2])
        mean = sb("mean", [P, S4, GB])
        var = sb("var", [P, S4, GB])
        std = sb("std", [P, S4, GB])
        rstd = sb("rstd", [P, S4, GB])
        rden = sb("rden", [P, S4, GB, HEADS])

        sel = sb("sel", [P, S4, 2 * GB, P], BF16)
        pay_more = sel[:].rearrange("p a k n -> p (a k n)").bitcast(F32)[:, 0:(PT - 1) * 2 * GB * PAY].rearrange("p (j u c) -> p j u c", j=PT - 1, u=2)
        idx_f = sb("idx_f", [P, S4, U], I32)
        ring = sb("ring", [P, RB * U + 1, D])
        sel32 = sb("sel32", [P, 2, 2 * GB, P])
        asum = sb("asum", [P, 2, W2])
        hh = sb("hh", [P, S4, W2])
        h0 = sb("h0", [P, S4, W2])
        hhT = sb("hhT", [P, GB, P])
        cat = hh[:].rearrange("p a c -> p (a c)").rearrange("p (u s k d) -> p u s k d", u=2, s=GB, k=2)
        catT = h0[:].rearrange("p a c -> p (a c)").rearrange("p (u s n) -> p u s n", u=2, s=GB)
        t0_f, tnew_f = (t[:].rearrange("p a c -> p (a c)") for t in (t0, tnew))
        first = tnew_f[:, 0:NBLK]
        first_i = tnew_f[:, NBLK:2 * NBLK].bitcast(I32)
        base_of = t0_f[:, 0:NBLK]
        tile0 = t0_f[:, NBLK:2 * NBLK]
        dloc = sb("dloc", [P, 2, NBLK])
        tiles_p = sb("tiles_p", [P, 4])
        place = sb("place", [1, NG, 2 * GB], I32)
        checks = sb("checks", [P, 4])
        flag = sb("flag", [1, 1], I32)
        ones = sb("ones", [P, P])
        wcent = sb("wcent", [P, P])
        bcent = sb("bcent", [P, D])
        wmean = sb("wmean", [P, 2])
        wgp = sb("wgp", [P, 2, P])

        idx_g = sb("idx_g", [P, U, 2], I32)
        idx_s = sb("idx_s", [P, U], I32)
        krow = sb("krow", [P, U, P], I32)
        eq = sb("eq", [P, U, P])
        junk = sb("junk", [P, P])
        cnt = sb("cnt", [P, U])
        pos = sb("pos", [P, U])
        msg = sb("msg", [P, U, 2 * D])
        msgT = sb("msgT", [P, U, P])
        qs = sb("qs", [P, U, D])
        qk = sb("qk", [P, U, D])
        att = sb("att", [P, U, HEADS])
        attc = sb("attc", [P, U, HEADS])
        pay = sb("pay", [P, U, PAY])
        summed = sb("summed", [P, U, PAY])

        pA = [ps(f"pA{u}", [P, 512]) for u in range(2)]
        pB = [ps(f"pB{u}", [P, 512]) for u in range(2)]
        pC = [ps(f"pC{u}", [P, 512]) for u in range(2)]
        pD = [ps(f"pD{u}", [P, 512]) for u in range(2)]
        rowlay = hh[0:TP, 0, :].bitcast(I32)
        rowlayf = h0[0:TP, 0, :]
        onehot_tile = [t[:].rearrange("p a c -> p (a c)")[:, o:o + NBLK] for t in (xt, own) for o in (0, 2 * W2)]
        size = z[:].rearrange("p a c -> p (a c)")[:, 0:NBLK]
        ends = z[:].rearrange("p a c -> p (a c)")[:, NBLK:2 * NBLK]
        hits = xc[:].rearrange("p a c -> p (a c)")[:, 0:2 * NBLK]
        hits2 = xnew[:].rearrange("p a c -> p (a c)")[:, 0:2 * NBLK]

        NAMES = ("row_in c1 c2 oht_ready oht_used flag_ready fast_wt f_idx f_sel f_agg f_add f_trans f_evac f_mm "
                 "f_z f_sqin f_sq f_var f_std f_pre f_x f_out f_cat f_gtr f_gev f_gmm f_gin f_gate chz chx chr "
                 "chn sel_made go const_in iota mask oh_ready oh_used deg_done root_done norm_done zero_ready "
                 "zero_out zero_pay f_pay f_h0 chain dchain sq_ready std_ready trans_done aT_ready y_ready "
                 "cat_ready catT_psum catT_ready g_ready gate_ready t_ready x_ready idx_ready sum_done sum_used "
                 "echain achain hT_done hT_ready qkv_done q_ready att_ready exp_ready pay_ready").split()
        s = {n: sem(n) for n in NAMES}
        loaded = [sem(f"loaded{u}") for u in range(2)]
        stored_t = [sem(f"stored_t{u}") for u in range(2)]
        stored_x = [sem(f"stored_x{u}") for u in range(2)]
        own_in = [sem(f"own_in{u}") for u in range(S4)]
        sel_in = [sem(f"sel_in{u}") for u in range(S4)]
        x_in = [sem(f"x_in{u}") for u in range(S4)]
        t0_in = [sem(f"t0_in{u}") for u in range(S4)]
        raw_in = [sem(f"raw_in{u}") for u in range(S4)]
        st_t = [sem(f"st_t{u}") for u in range(S4)]
        st_x = [sem(f"st_x{u}") for u in range(S4)]
        sel_out = [sem(f"sel_out{u}") for u in range(2)]
        krow_in = [sem(f"krow_in{q}") for q in range(U)]
        gathered = [sem(f"gathered{q}") for q in range(U)]
        scattered = [sem(f"scattered{q}") for q in range(U)]
        block = ctx.enter_context(nc.Block())

        def grp(tab, g, w=D):
            return tab[0:NROW, :].rearrange("(g p s) d -> g p (s d)", p=P, s=GB)[bass.ds(g, 1) if not isinstance(g, int) else slice(g, g + 1)].rearrange("g p c -> p (g c)")

        def col(t, g):
            return t[:, bass.ds(g * GB, GB)].unsqueeze(2).to_broadcast([P, GB, D])

        def b3(ap):
            return ap.rearrange("p (s d) -> p s d", s=GB)

        def spread(ap):
            return ap.unsqueeze(2).to_broadcast([P, GB, D])

        def vec(k):
            return bsb[:, k, :].unsqueeze(1).to_broadcast([P, GB, D])

        def before(k, kinds):
            return NG * sum(1 for j in range(k) if j in kinds)

        def n_loads(k):
            return (k in CONVS) + (k in READS_X) + (k == CONV_GATE) + (k == ATT_RES)

        def loads_before(k):
            return 16 * (NG // 2) * sum(n_loads(j) for j in range(k))

        def n_tstores(k):
            return 1 if k in (LAST, CONV_RES) else 2

        def tstores_before(k):
            return 16 * (NG // 2) * sum(n_tstores(j) for j in range(k))

        def xstores_before(k):
            return 16 * (NG // 2) * sum(1 for j in range(k) if j in WRITES_X)

        KINDS = {ev: CONVS for ev in "f_agg f_add f_trans f_evac f_mm f_sel f_idx".split()}
        KINDS["f_z"] = ROUNDS
        KINDS["f_sqin"] = LN_RELU
        KINDS |= {ev: LN_RELU + ROUNDS for ev in "f_sq f_var f_std".split()}
        KINDS |= {ev: (CONV_GATE,) for ev in "f_cat f_gtr f_gev f_gmm f_gin f_gate".split()}
        KINDS["f_pay"] = (ATT_RES,)
        KINDS["f_h0"] = (CONV_GATE,)
        KINDS |= {"f_pre": (ROUND_A, ROUND_B, ROUND_C), "f_x": WRITES_X, "f_out": tuple(range(10))}
        PER_BATCH = ("f_idx",)

        def upto(ev, k, m):
            return (NIT if ev in PER_BATCH else NG) * sum(1 for j in range(k) if j in KINDS[ev]) + m + 1

        def after(eng, ev, k, m, lag=0):
            if isinstance(m, int) and m < lag:
                return
            eng.wait_ge(s[ev], upto(ev, k, m - lag))

        def landed(eng, sems, kinds, k, m, u, turn, each=1, lag=0):
            if isinstance(m, int) and m < lag:
                return
            eng.wait_ge(sems[u], 16 * (each * (turn - lag // S4 + 1) + NG // S4 * sum(dmas(j, kinds) for j in range(k))))

        def raw_before(k, q):
            return sum(1 for j in range(k) if j in CONVS) * len(range(q, NIT, S4))

        def dmas(j, kinds):
            return kinds.get(j, 0)

        X_LOADS = {k: 1 + PT * (k == ATT_RES) for k in READS_X}
        T0_LOADS = {CONV_GATE: 1}
        OWN_LOADS = {k: 1 for k in CONVS}
        T_STORES = {k: 1 for k in range(10)}
        X_STORES = {k: 1 for k in WRITES_X}

        def x_part(k):
            return {CONV_GATE: 5, FIRST: 0, ATT_RES: 0}.get(k, 2)

        def steps(eng, k, body):
            lo = -(-(x_part(k) + 1 + S4) // S4)
            hi = FULL if k in CONVS else NG // S4 - 1
            for n in range(lo * S4):
                body(k, n, n % S4, n // S4)
            with eng.Fori(lo, hi) as it:
                for u in range(S4):
                    body(k, it * S4 + u, u, it)
            for n in range(hi * S4, NG + x_part(k) + 4):
                body(k, n, n % S4, n // S4)

        def at(n, u, it, off):
            m = n - off
            return (not isinstance(m, int)) or 0 <= m < NG, m, (u - off) % S4, it + (u - off) // S4

        def over(eng, n, peel, body):
            if peel:
                body(0)
            with eng.Fori(int(peel), n) as i:
                body(i)

        def earlier(eng, sem_, value):
            if not (isinstance(value, int) and value == 0):
                eng.wait_ge(sem_, value)

        ZERO_PAY = PT * (NG + 1)
        SCATTERS = 16 * NIT

        def links_before(k):
            return sum(NG * LINKS[j] for j in range(k))

        LEAD = 3

        def edge_steps(eng, body):
            def static(n):
                return lambda off: (0 <= n + off < NT, (n + off) // U, (n + off) % U)

            def dynamic(t, q):
                return lambda off: (True, t + (q + off) // U, (q + off) % U)
            for n in range(-IDX_LEAD, U):
                body(static(n))
            with eng.Fori(1, NIT - 1) as t:
                for q in range(U):
                    body(dynamic(t, q))
            for n in range(NT - U, NT + 2):
                body(static(n))

        IDX_LEAD = LEAD

        def slot_scattered(eng, q, t, a=0):
            if not (isinstance(t, int) and t == 0 and a == 0):
                eng.wait_ge(scattered[q], SCATTERS * a + 16 * t)

        BIAS = {CONV_A: 0, CONV_GATE: 1, CONV_B: 2, CONV_RES: 3, ROUND_A: 4, ROUND_B: 4, ROUND_C: 4, LAST: 4}
        B_GATE, B_GAMMA, B_BETA = 5, 6, 7

        pG = pB[1]

        def y_bank(k, q):
            return pB[0] if k == CONV_GATE else pB[q % 2]

        @block.sync
        def _(sp):
            n = 0
            for t, a in ((key["src"], src), (key["dst"], dst)):
                sp.dma_start(t[:], a).then_inc(s["const_in"], 16)
            sp.wait_ge(s["zero_ready"], 1)
            for k in range(4):
                for h in range(2):
                    sp.dma_start(wsb[h * D:(h + 1) * D, k, h * D:(h + 1) * D], wt[k * D:(k + 1) * D, :]).then_inc(s["const_in"], 16)
            for h in range(2):
                sp.dma_start(wround[h * D:(h + 1) * D, h * D:(h + 1) * D], wt[4 * D:5 * D, :]).then_inc(s["const_in"], 16)
            sp.dma_start(wgate[:], wt[5 * D:7 * D, :]).then_inc(s["const_in"], 16)
            sp.dma_start(wqkv[0:D, 0:D], wt[7 * D:8 * D, :]).then_inc(s["const_in"], 16)
            sp.dma_start(wqkv[D:P, D:2 * D], wt[8 * D:9 * D, :]).then_inc(s["const_in"], 16)
            sp.dma_start(wqkv[D:P, 2 * D:3 * D], wt[9 * D:10 * D, :]).then_inc(s["const_in"], 16)
            sp.dma_start(bsb[:].rearrange("p k d -> p (k d)"), bias.rearrange("k d -> (k d)").partition_broadcast(P)).then_inc(s["const_in"], 16)
            for k in range(10):
                sp.dma_start(total[k][NROW:NROW + P, :], zeros[:, 0:D]).then_inc(s["zero_out"], 16)

            def load(k, g, u, base):
                if k in CONVS:
                    sp.wait_ge(s["trans_done"], before(k, CONVS) + base * 2 + u + 1)
                    sp.dma_start(own[:, u, :], grp(total[k - 1], g)).then_inc(loaded[u], 16)
                if k in READS_X or k == CONV_GATE or k == ATT_RES:
                    sp.wait_ge(s["t_ready"], NG * k + base * 2 + u + 1)
                if k in READS_X:
                    a = x if k in (FIRST, CONV_GATE) else xres[WRITES_X.index(k) - 1 if k != LAST else 2]
                    sp.dma_start(xt[:, u, :], grp(a, g)).then_inc(loaded[u], 16)
                if k == CONV_GATE:
                    sp.dma_start(t0[:, u, :], grp(table[FIRST], g)).then_inc(loaded[u], 16)
                if k == ATT_RES:
                    sp.dma_start(pay_in[:, u, :], grp(payload, g)).then_inc(loaded[u], 16)

            def store(k, g, u, base):
                if k in WRITES_X:
                    sp.wait_ge(s["x_ready"], before(k, WRITES_X) + base * 2 + u + 1)
                    sp.dma_start(grp(xres[WRITES_X.index(k)], g), xnew[:, u, :]).then_inc(stored_x[u], 16)
                sp.wait_ge(s["t_ready"], NG * k + base * 2 + u + 3)
                if k == LAST:
                    sp.dma_start(grp(out, g), tnew[:, u, :]).then_inc(stored_t[u], 16)
                else:
                    sp.dma_start(grp(table[k], g), tnew[:, u, :]).then_inc(stored_t[u], 16)
                    if n_tstores(k) == 2:
                        sp.dma_start(grp(total[k], g), tnew[:, u, :]).then_inc(stored_t[u], 16)

            def edge_rows(k, t, a):
                rows = src_row if k == CONV_RES else dst_row
                for q in range(U):
                    sp.wait_ge(s["idx_ready"], NT * a + t * U + q + 1)
                    sp.dma_start(krow[:, q, :], rows[bass.ds(t * U + q, 1), :].rearrange("a e -> (a e)").partition_broadcast(P)).then_inc(krow_in[q], 16)

            sp.dma_start(rowlay, dst_row.rearrange("(c p) e -> p c e", p=TP)).then_inc(s["row_in"], 16)
            for j in range(2):
                for h in range(2):
                    sp.dma_start(wgp[h * D:(h + 1) * D, j, h * D:(h + 1) * D], wt[(5 + j) * D:(6 + j) * D, :]).then_inc(s["row_in"], 16)
            with sp.Fori(0, NG // 2) as h:
                for u in range(2):
                    sp.wait_ge(s["sel_made"], h * 2 + u + 1)
                    sp.dma_start(sel_d[bass.ds(h * 2 + u, 1)].rearrange("a p c -> p (a c)"), sel[:, u].rearrange("p k n -> p (k n)")).then_inc(sel_out[u], 16)
            for u in range(2):
                sp.wait_ge(sel_out[u], 16 * (NG // 2))

            def fast_loads(k, n, u, it):
                if k in CONVS:
                    live, m, q, turn = at(n, u, it, -2)
                    if live:
                        after(sp, "f_sel", k, m, S4)
                        sp.dma_start(sel[:, q].rearrange("p k n -> p (k n)"), sel_d[m:m + 1].rearrange("a p c -> p (a c)") if isinstance(m, int) else sel_d[bass.ds(m, 1)].rearrange("a p c -> p (a c)")).then_inc(sel_in[q], 16)
                        after(sp, "f_add", k, m, S4)
                        sp.dma_start(own[:, q, :], grp(table[k - 1], m)).then_inc(own_in[q], 16)
                if k == CONV_GATE:
                    live, m, q, turn = at(n, u, it, -1)
                    if live:
                        after(sp, "f_cat", k, m, S4)
                        sp.dma_start(t0[:, q, :], grp(table[FIRST], m)).then_inc(t0_in[q], 16)
                if k in READS_X:
                    live, m, q, turn = at(n, u, it, x_part(k) - 2 - (k in CONVS))
                    if live:
                        after(sp, "f_out" if k == LAST else "f_x" if k in WRITES_X else "f_sqin", k, m, S4)
                        a = x if k in (FIRST, CONV_GATE) else xres[WRITES_X.index(k) - 1 if k != LAST else 2]
                        sp.dma_start(xt[:, q, :], grp(a, m)).then_inc(x_in[q], 16)
                        if k == ATT_RES:
                            sp.dma_start(pay_in[:, q, :], grp(payload, m)).then_inc(x_in[q], 16)
                            after(sp, "f_pay", k, m, 2)
                            for j in range(1, PT):
                                sp.dma_start(pay_more[:, j - 1, q % 2, :], grp(payloads[j], m)).then_inc(x_in[q], 16)

            def fast(k, n, u, it):
                fast_loads(k, n, u, it)
                live, m, q, turn = at(n, u, it, x_part(k) + 3)
                if live:
                    if k in WRITES_X:
                        after(sp, "f_x", k, m)
                        sp.dma_start(grp(xres[WRITES_X.index(k)], m), xnew[:, q, :]).then_inc(st_x[q], 16)
                    after(sp, "f_out", k, m)
                    sp.dma_start(grp(out if k == LAST else table[k], m), tnew[:, q, :]).then_inc(st_t[q], 16)

            def pass_stored(eng, sems, kinds, k):
                for q in range(S4):
                    eng.wait_ge(sems[q], 16 * (NG // S4) * sum(dmas(j, kinds) for j in range(k + 1)))

            sp.wait_ge(s["flag_ready"], 1)
            even = sp.value_load(flag[0:1, 0:1], min_val=0, max_val=1)
            with sp.If(even == 1):
                for k in range(10):
                    for n in (-2, -1):
                        fast_loads(k, n, n, 0)
                    steps(sp, k, fast)
                    pass_stored(sp, st_t, T_STORES, k)
                    if k in WRITES_X:
                        pass_stored(sp, st_x, X_STORES, k)
                    if k == CONV_RES:
                        with sp.Fori(0, NIT) as t:
                            edge_rows(k, t, 0)
                        for q in range(U):
                            sp.wait_ge(scattered[q], SCATTERS)
            with sp.Else():
              for k in range(10):
                  load(k, 0, 0, 0)
                  load(k, 1, 1, 0)
                  with sp.Fori(1, NG // 2) as h:
                      for u in range(2):
                          load(k, h * 2 + u, u, h)
                          store(k, h * 2 + (u - 2), u, h - 1)
                  for u in range(2):
                      store(k, NG - 2 + u, u, NG // 2 - 1)
                  if k != LAST:
                      with sp.Fori(0, NIT) as t:
                          edge_rows(k, t, k)
                      if k == CONV_RES:
                          sp.wait_ge(s["zero_pay"], 16 * ZERO_PAY)
                      for q in range(U):
                          sp.wait_ge(scattered[q], SCATTERS * (k + 1))
                      if k in WRITES_X:
                          for u in range(2):
                              sp.wait_ge(stored_x[u], xstores_before(k + 1))
              for u in range(2):
                  sp.wait_ge(stored_t[u], tstores_before(10))

        @block.gpsimd
        def _(pool):
            nc.gpsimd.iota(bits[:, 0, 0:1], [[0, 1]], base=NROW, channel_multiplier=1).then_inc(s["iota"], 1)
            nc.gpsimd.iota(iota_b[:], [[1, NBLK]], base=0, channel_multiplier=0, allow_small_or_imprecise_dtypes=True).then_inc(s["iota"], 1)
            nc.gpsimd.memset(ident[:], 0.0).then_inc(s["mask"], 1)
            nc.gpsimd.memset(lower[:], 1.0).then_inc(s["mask"], 1)
            pool.wait_ge(s["mask"], 2)
            nc.gpsimd.affine_select(out=ident[:], in_=ident[:], compare_op=ALU.not_equal, fill=1.0, base=0,
                                    pattern=[[-1, P]], channel_multiplier=1).then_inc(s["mask"], 1)
            nc.gpsimd.affine_select(out=lower[:], in_=lower[:], compare_op=ALU.is_gt, fill=0.0, base=0,
                                    pattern=[[-1, P]], channel_multiplier=1).then_inc(s["mask"], 1)

            def gather(k, a, n, q, t):
                pool.wait_ge(s["idx_ready"], NT * a + U * t + q + 1 + U)
                pool.wait_ge(s["sum_done"], NT * a + U * t + q + 1)
                pool.sem_inc(s["go"], 1)
                if k == CONV_RES:
                    pool.indirect_dma_start(msg[:, q, 0:D], None, table[k], bass.IndirectOffsetOnAxis(ap=idx_g[:, q, 0:1], axis=0)).then_inc(gathered[q], 16)
                    pool.indirect_dma_start(msg[:, q, D:2 * D], None, table[k], bass.IndirectOffsetOnAxis(ap=idx_g[:, q, 1:2], axis=0)).then_inc(gathered[q], 16)
                else:
                    pool.indirect_dma_start(msg[:, q, 0:D], None, table[k], bass.IndirectOffsetOnAxis(ap=idx_g[:, q, 0:1], axis=0)).then_inc(gathered[q], 16)

            def scatter(k, a, q, t, apart=False):
                pool.wait_ge(s["sum_used"], NT * a + U * t + q + 1 + U)
                if apart:
                    if q >= PT:
                        pool.wait_ge(scattered[q - PT], 16 * (t + 1))
                    else:
                        slot_scattered(pool, q - PT + U, t)
                elif q:
                    pool.wait_ge(scattered[q - 1], SCATTERS * a + 16 * t + 16)
                else:
                    earlier(pool, scattered[U - 1], SCATTERS * a + 16 * t)
                w = PAY if k == CONV_RES else D
                pool.sem_inc(s["go"], 1)
                pool.indirect_dma_start(payloads[q % PT if apart else 0] if k == CONV_RES else total[k], bass.IndirectOffsetOnAxis(ap=idx_s[:, q:q + 1], axis=0),
                                        summed[:, q, 0:w], None, compute_op=ALU.add).then_inc(scattered[q], 16)

            nc.gpsimd.iota(tiles_p[:], [[TP, 4]], base=0, channel_multiplier=1, allow_small_or_imprecise_dtypes=True).then_inc(s["iota"], 1)
            nc.gpsimd.iota(base_of[:], [[P, NBLK]], base=0, channel_multiplier=0, allow_small_or_imprecise_dtypes=True).then_inc(s["iota"], 1)
            nc.gpsimd.iota(tile0[:], [[U, NG], [0, GB]], base=0, channel_multiplier=0, allow_small_or_imprecise_dtypes=True).then_inc(s["iota"], 1)
            nc.gpsimd.memset(ones[:], 1.0).then_inc(s["iota"], 1)

            def edge_pass(k, a):
                for q in range(LEAD):
                    gather(k, a, q, q, 0)

                def body(t):
                    for q in range(U):
                        gather(k, a, None, (q + LEAD) % U, t + (q + LEAD) // U)
                        scatter(k, a, q, t)
                over(pool, NIT - 1, a == 0, body)
                for q in range(U):
                    if q + LEAD < U:
                        gather(k, a, None, q + LEAD, NIT - 1)
                    scatter(k, a, q, NIT - 1)

            def fast_gather(k, b, slot):
                q = slot % S4
                after(pool, "f_agg", k, b, RB - BACK)
                if isinstance(b, int) and S4 <= b < RB - BACK:
                    pool.wait_ge(raw_in[q], 16 * U * (b // S4 + raw_before(k, q)))
                pool.sem_inc(s["go"], 1)
                nc.gpsimd.tensor_copy(idx_f[:, q, :], row["src"][:, bass.ds(b * U, U)]).then_inc(s["f_idx"], 1)
                after(pool, "f_idx", k, b)
                pool.sem_inc(s["go"], 1)
                for j in range(U):
                    pool.indirect_dma_start(ring[:, slot * U + j, :], None, table[k - 1], bass.IndirectOffsetOnAxis(ap=idx_f[:, q, j:j + 1], axis=0)).then_inc(raw_in[q], 16)

            def gate_input(k, m, q, turn):
                landed(pool, t0_in, T0_LOADS, k, m, q, turn)
                after(pool, "f_gtr", k, m, S4)
                pool.sem_inc(s["go"], 1)
                nc.gpsimd.tensor_tensor(b3(h0[:, q, :]), b3(t0[:, q, :]), col(root, m), ALU.mult).then_inc(s["f_h0"], 1)

            def add_payloads(k, m, q, turn):
                landed(pool, x_in, X_LOADS, k, m, q, turn, each=X_LOADS[k])
                pool.sem_inc(s["go"], 1)
                ins = nc.gpsimd.tensor_tensor(pay_in[:, q, :], pay_in[:, q, :], pay_more[:, 0, q % 2, :], ALU.add)
                ins.then_inc(s["f_pay"], 1)

            def fast_edge(tile):
                live, t, q = tile(LEAD)
                if live:
                    gather(CONV_RES, 0, None, q, t)
                live, t, q = tile(-1)
                if live:
                    scatter(CONV_RES, 0, q, t, apart=True)

            pool.wait_ge(s["zero_out"], 16 * 10)
            pool.wait_ge(s["flag_ready"], 1)
            even = pool.value_load(flag[0:1, 0:1], min_val=0, max_val=1)
            with pool.If(even == 1):
                for k in range(10):
                    if k in CONVS:
                        for q in range(S4):
                            pool.wait_ge(st_t[q], 16 * (NG // S4) * k)
                        for b in range(RB):
                            fast_gather(k, b, b)
                            if k == CONV_GATE and b >= AHEAD:
                                gate_input(k, b - AHEAD, (b - AHEAD) % S4, (b - AHEAD) // S4)
                        with pool.Fori(1, NIT // RB) as it:
                            for slot in range(RB):
                                fast_gather(k, it * RB + slot, slot)
                                if k == CONV_GATE:
                                    gate_input(k, it * RB + (slot - AHEAD), (slot - AHEAD) % S4, it * 2 + (slot - AHEAD) // S4)
                        for b in range(NIT - NIT % RB, NIT):
                            fast_gather(k, b, b % RB)
                            if k == CONV_GATE:
                                gate_input(k, b - AHEAD, (b - AHEAD) % S4, (b - AHEAD) // S4)
                        if k == CONV_GATE:
                            for m in range(NIT - AHEAD, NG):
                                gate_input(k, m, m % S4, m // S4)
                    if k == CONV_RES:
                        for q in range(S4):
                            pool.wait_ge(st_t[q], 16 * (NG // S4) * (k + 1))
                        pool.wait_ge(s["zero_pay"], 16 * ZERO_PAY)
                        edge_steps(pool, fast_edge)
                    if k == ATT_RES:
                        with pool.Fori(0, NG // S4) as it:
                            for q in range(S4):
                                add_payloads(k, it * S4 + q, q, it)
            with pool.Else():
              for k in range(9):
                for u in range(2):
                    pool.wait_ge(stored_t[u], tstores_before(k + 1))
                if k == CONV_RES:
                    pool.wait_ge(s["zero_pay"], 16 * ZERO_PAY)
                edge_pass(k, k)

        @block.scalar
        def _(act):
            act.wait_ge(s["zero_ready"], 1)
            for tab in payloads:
                act.dma_start(tab[NROW:NROW + P, :], zeros[:, 0:PAY]).then_inc(s["zero_pay"], 16)
            with act.Fori(0, NG) as g:
                for tab in payloads:
                    act.dma_start(grp(tab, g), zeros[:]).then_inc(s["zero_pay"], 16)
            act.wait_ge(s["deg_done"], 1)
            nc.scalar.activation(root[:, 0:NBLK // 2], pA[0][:, 0:NBLK // 2], ACT.Sqrt, bias=1.0).then_inc(s["root_done"], 1)
            nc.scalar.activation(root[:, NBLK // 2:NBLK], pA[1][:, 0:NBLK // 2], ACT.Sqrt, bias=1.0).then_inc(s["root_done"], 1)

            def step(k, h, u):
                n = h * 2 + u
                if k in CONVS:
                    c = before(k, CONVS)
                    act.wait_ge(s["trans_done"], c + n + 3)
                    act.wait_ge(s["y_ready"], c + n - 1 + 2)
                    nc.scalar.copy(aT[:, u, :], pA[u][:]).then_inc(s["aT_ready"], 1)
                if k == CONV_GATE:
                    act.wait_ge(s["catT_psum"], n + 1)
                    act.wait_ge(s["g_ready"], n + 1)
                    nc.scalar.copy(catT[:, u, 0:HB, :].rearrange("p a b -> p (a b)"), pC[0][:]).then_inc(s["catT_ready"], 1)
                    nc.scalar.copy(catT[:, u, HB:GB, :].rearrange("p a b -> p (a b)"), pC[1][:]).then_inc(s["catT_ready"], 1)
                    act.wait_ge(s["gate_ready"], n * 2 + 1)
                    nc.scalar.activation(gate[:, u, :], gate[:, u, :], ACT.Sigmoid).then_inc(s["gate_ready"], 1)
                if k in LN_RELU or k in ROUNDS:
                    c = before(k, LN_RELU + ROUNDS)
                    act.wait_ge(s["sq_ready"], 2 * (c + n) + 1)
                    nc.scalar.activation(sq[:, u, :], xc[:, u, :], ACT.Square).then_inc(s["std_ready"], 1)
                    act.wait_ge(s["sq_ready"], 2 * (c + n) + 2)
                    nc.scalar.activation(std[:, u, :], var[:, u, :], ACT.Sqrt).then_inc(s["std_ready"], 1)

            def edge_q(t, q):
                m = U * t + q
                act.wait_ge(s["hT_done"], m + 1)
                act.wait_ge(s["qkv_done"], m + 1)
                nc.scalar.copy(msgT[:, q, :], pB[q % 2][:, 0:P]).then_inc(s["hT_ready"], 1)
                act.wait_ge(s["qkv_done"], m + 1 + U)
                nc.scalar.copy(qs[:, q, :], pC[q % 2][:, 0:D]).then_inc(s["q_ready"], 1)

            def edge_exp(t, q):
                act.wait_ge(s["att_ready"], U * t + q + 1)
                nc.scalar.activation(pay[:, q, D:PAY], attc[:, q, :], ACT.Exp).then_inc(s["exp_ready"], 1)

            def edge_sums(k, a, t, q):
                act.wait_ge(s["sum_done"], NT * a + U * t + q + 1 + U)
                slot_scattered(act, q, t, a)
                w = PAY if k == CONV_RES else D
                nc.scalar.copy(summed[:, q, 0:w], pA[q % 2][:, 0:w]).then_inc(s["sum_used"], 1)

            def edge(k, a, t):
                for q in range(U):
                    if k == CONV_RES:
                        edge_q(t, q)
                        edge_exp(t, q)
                    edge_sums(k, a, t, q)

            def fast_edge(tile):
                live, t, q = tile(1)
                if live:
                    edge_q(t, q)
                live, t, q = tile(0)
                if live:
                    edge_exp(t, q)
                live, t, q = tile(-1)
                if live:
                    edge_sums(CONV_RES, 0, t, q)

            def fast_select(k, n, u, it):
                live, m, q, turn = at(n, u, it, -1)
                if live and k in CONVS:
                    landed(act, sel_in, OWN_LOADS, k, m, q, turn)
                    after(act, "f_agg", k, m, 2)
                    nc.scalar.copy(sel32[:, q % 2].rearrange("p k n -> p (k n)"), sel[:, q].rearrange("p k n -> p (k n)")).then_inc(s["f_sel"], 1)

            def fast(k, n, u, it):
                fast_select(k, n, u, it)
                r = x_part(k) + 1
                live, m, q, turn = at(n, u, it, r)
                if live and k in LN_RELU + ROUNDS:
                    after(act, "f_var", k, m)
                    nc.scalar.activation(std[:, q, :], var[:, q, :], ACT.Sqrt).then_inc(s["f_std"], 1)
                live, m, q, turn = at(n, u, it, r + 1)
                if live and k in KINDS["f_pre"]:
                    after(act, "f_pre", k, m)
                    landed(act, st_t, T_STORES, k, m, q, turn, lag=S4)
                    for j in range(GB):
                        ins = nc.scalar.mul(tnew[:, q, j * D:(j + 1) * D], xc[:, q, j * D:(j + 1) * D], dinv[:, bass.ds(m * GB + j, 1)])
                    ins.then_inc(s["f_out"], 1)
                live, m, q, turn = at(n, u, it, 1)
                if live and k in CONVS:
                    after(act, "f_trans", k, m)
                    after(act, "f_mm", k, m, 2)
                    nc.scalar.copy(aT[:, q % 2, :], pA[q % 2][:]).then_inc(s["f_evac"], 1)
                if k == CONV_GATE:
                    live, m, q, turn = at(n, u, it, 3)
                    if live:
                        after(act, "f_gtr", k, m)
                        after(act, "f_gmm", k, m, 1)
                        nc.scalar.copy(hhT[:, 0:HB, :].rearrange("p a b -> p (a b)"), pD[0][:])
                        nc.scalar.copy(hhT[:, HB:GB, :].rearrange("p a b -> p (a b)"), pD[1][:]).then_inc(s["f_gev"], 1)
                    live, m, q, turn = at(n, u, it, 4)
                    if live:
                        after(act, "f_gin", k, m)
                        nc.scalar.activation(gate[:, q % 2, :], gate[:, q % 2, :], ACT.Sigmoid).then_inc(s["f_gate"], 1)
                live, m, q, turn = at(n, u, it, x_part(k))
                if live and k in LN_RELU + ROUNDS:
                    after(act, "f_z" if k in ROUNDS else "f_sqin", k, m)
                    after(act, "f_var", k, m, 2)
                    nc.scalar.activation(sq[:, q % 2, :], (z if k in ROUNDS else xc)[:, q, :], ACT.Square).then_inc(s["f_sq"], 1)

            act.sem_inc(s["sum_used"], U)
            act.wait_ge(s["flag_ready"], 1)
            even = act.value_load(flag[0:1, 0:1], min_val=0, max_val=1)
            with act.If(even == 1):
                for k in range(10):
                    if k in CONVS:
                        fast_select(k, -1, -1, 0)
                    steps(act, k, fast)
                    if k == CONV_RES:
                        edge_steps(act, fast_edge)
            with act.Else():
              for k in range(10):
                with act.Fori(0, NG // 2) as h:
                    for u in range(2):
                        step(k, h, u)
                if k != LAST:
                    over(act, NIT, k == FIRST, lambda t: edge(k, k, t))

        @block.vector
        def _(dve):
            links = [0]

            def link(ins, name="dchain"):
                links[0] += 1
                ins.then_inc(s[name], 1)
                dve.wait_ge(s[name], links[0])

            nc.vector.memset(zeros[:], 0.0)
            nc.vector.memset(wqkv[:], 0.0)
            nc.vector.memset(wround[:], 0.0)
            nc.vector.memset(wgp[:], 0.0)
            nc.vector.memset(ring[:], 0.0)
            nc.vector.memset(wsb[:], 0.0).then_inc(s["zero_ready"], 1)
            dve.wait_ge(s["iota"], 6)
            link(nc.vector.tensor_copy(spare[:], bits[:, 0, 0:1]))
            dve.wait_ge(s["const_in"], 16 * 17)
            for k in ("src", "dst"):
                link(nc.vector.tensor_copy(keyf[k][:], key[k][:]))
                link(nc.vector.tensor_scalar(row[k][:], key[k][:], 10, 10, ALU.logical_shift_right, ALU.logical_shift_left))
                link(nc.vector.tensor_scalar(bits[:, 0, :], key[k][:], P - 1, 3, ALU.bitwise_and, ALU.logical_shift_left))
                link(nc.vector.tensor_tensor(row[k][:], row[k][:], bits[:, 0, :], ALU.bitwise_or))
                link(nc.vector.tensor_scalar(bits[:, 0, :], key[k][:], 7, GB - 1, ALU.logical_shift_right, ALU.bitwise_and))
                link(nc.vector.tensor_tensor(row[k][:], row[k][:], bits[:, 0, :], ALU.bitwise_or))
                link(nc.vector.tensor_scalar(row[k][:], row[k][:], NROW - 1, None, ALU.min))
                link(nc.vector.tensor_scalar(rowm[k][:], row[k][:], spare[:, 0:1], None, ALU.subtract))
            link(nc.vector.tensor_scalar(bits[:, 0, :], key["dst"][:], P - 1, None, ALU.bitwise_and))
            link(nc.vector.tensor_scalar(bits[:, 1, :], key["dst"][:], 7, None, ALU.logical_shift_right))
            link(nc.vector.tensor_copy(lo[:], bits[:, 0, :]))
            link(nc.vector.tensor_copy(hi[:], bits[:, 1, :]))

            def onehots(t):
                for q in range(U):
                    n = t * U + q
                    dve.wait_ge(s["oh_used"], n + 1)
                    nc.vector.tensor_scalar(onehot_lo[:, q, :], iota_b[:, 0:P], lo[:, bass.ds(n, 1)], None, ALU.is_equal).then_inc(s["oh_ready"], 1)
                    nc.vector.tensor_scalar(onehot_hi[:, q, :], iota_b[:], hi[:, bass.ds(n, 1)], None, ALU.is_equal).then_inc(s["oh_ready"], 1)
            with dve.Fori(0, NIT) as t:
                onehots(t)
            dve.wait_ge(s["root_done"], 2)
            for h in range(2):
                cols = slice(h * NBLK // 2, (h + 1) * NBLK // 2)
                ins = nc.vector.tensor_copy(size[:, cols], pA[h][:, 0:NBLK // 2])
            ins.then_inc(s["c1"], 1)
            dve.wait_ge(s["c2"], 1)
            nc.vector.memset(hits[:], 1.0)
            for h in range(2):
                cols = slice(h * NBLK // 2, (h + 1) * NBLK // 2)
                ins = nc.vector.tensor_copy(size[:, cols], pB[h][:, 0:NBLK // 2])
            link(ins)
            link(nc.vector.tensor_tensor_scan(ends, hits[:, 0:NBLK], size, 0.0, ALU.mult, ALU.add))
            link(nc.vector.tensor_tensor(ends, ends, size, ALU.subtract))
            link(nc.vector.tensor_copy(first_i[:], ends))
            link(nc.vector.tensor_scalar(first_i[:], first_i[:], 7, None, ALU.logical_shift_right))
            link(nc.vector.tensor_copy(first[:], first_i[:]))
            dve.wait_ge(s["row_in"], 16 * 5)
            link(nc.vector.tensor_copy(rowlayf, rowlay))
            for k in range(2):
                if k:
                    dve.wait_ge(s["oht_used"], 1)
                    link(nc.vector.tensor_scalar(tiles_p[:], tiles_p[:], -1.0, None, ALU.add))
                for c in range(4):
                    nc.vector.tensor_scalar(onehot_tile[c], first[:], tiles_p[:, c:c + 1], None, ALU.is_equal).then_inc(s["oht_ready"], 1)
            dve.wait_ge(s["oht_used"], 2)
            for k in range(2):
                for h in range(2):
                    cols = slice(h * NBLK // 2, (h + 1) * NBLK // 2)
                    ins = nc.vector.tensor_tensor(dloc[:, k, cols], (pC, pD)[k][h][:, 0:NBLK // 2], base_of[:, cols], ALU.subtract)
            link(ins)
            flat = dloc[:].rearrange("p k b -> p (k b)")
            link(nc.vector.tensor_scalar(hits, flat, 0.0, None, ALU.is_ge))
            link(nc.vector.scalar_tensor_tensor(hits2, flat, float(P), hits, ALU.is_lt, ALU.mult))
            link(nc.vector.tensor_reduce(checks[:, 0:1], hits2, AX_X, ALU.add))
            link(nc.vector.tensor_tensor(size, first[:], tile0[:], ALU.subtract))
            link(nc.vector.tensor_scalar(hits[:, 0:NBLK], size, float(U * (AHEAD - 1) + U - 2), None, ALU.is_gt))
            link(nc.vector.tensor_scalar(hits[:, NBLK:2 * NBLK], size, float(-U * BACK), None, ALU.is_lt))
            nc.vector.tensor_reduce(checks[:, 1:2], hits, AX_X, ALU.add).then_inc(s["c1"], 1)
            dve.wait_ge(s["c2"], 2)
            link(nc.vector.tensor_copy(checks[:, 0:2], pA[0][:, 0:2]))
            link(nc.vector.tensor_scalar(checks[:, 2:3], checks[:, 0:1], float(N_EDGES), None, ALU.is_equal))
            link(nc.vector.tensor_scalar(checks[:, 3:4], checks[:, 1:2], 0.0, checks[:, 2:3], ALU.is_equal, ALU.mult))
            spots = place[:].rearrange("o g c -> o (g c)").rearrange("o (b k) -> o b k", k=2)
            for k in range(2):
                if k:
                    link(nc.vector.tensor_scalar(first_i[0:1, :], first_i[0:1, :], 1, None, ALU.add))
                link(nc.vector.tensor_scalar(base_of[0:1, :].bitcast(I32), first_i[0:1, :], RB * U - 1, None, ALU.bitwise_and))
                link(nc.vector.tensor_scalar(spots[:, :, k], base_of[0:1, :].bitcast(I32), D, None, ALU.mult))
            nc.vector.tensor_copy(flag[:], checks[0:1, 3:4]).then_inc(s["flag_ready"], 1)
            def select(h, u):
                nc.vector.tensor_tensor(sel[:, u].rearrange("p (b k) n -> p k b n", k=2),
                                        dloc[:, :, bass.ds((h * 2 + u) * GB, GB)].unsqueeze(3).to_broadcast([P, 2, GB, P]),
                                        iota_b[:, 0:P].unsqueeze(1).unsqueeze(1).to_broadcast([P, 2, GB, P]), ALU.is_equal).then_inc(s["sel_made"], 1)
            for u in range(2):
                select(0, u)
            with dve.Fori(1, NG // 2) as h:
                for u in range(2):
                    dve.wait_ge(sel_out[u], h * 16)
                    select(h, u)
            for h in range(2):
                rows = slice(h * D, (h + 1) * D)
                link(nc.vector.tensor_reduce(wmean[rows, 0:1], wround[rows, rows], AX_X, ALU.add))
                link(nc.vector.tensor_scalar(wmean[rows, 1:2], wmean[rows, 0:1], 1.0 / D, None, ALU.mult))
            link(nc.vector.tensor_copy(wcent[:], wround[:]))
            for h in range(2):
                rows = slice(h * D, (h + 1) * D)
                link(nc.vector.tensor_scalar(wcent[rows, rows], wround[rows, rows], wmean[rows, 1:2], None, ALU.subtract))
            link(nc.vector.tensor_reduce(wmean[:, 0:1], bsb[:, BIAS[ROUND_A], :], AX_X, ALU.add))
            link(nc.vector.tensor_scalar(wmean[:, 1:2], wmean[:, 0:1], 1.0 / D, None, ALU.mult))
            nc.vector.tensor_scalar(bcent[:], bsb[:, BIAS[ROUND_A], :], wmean[:, 1:2], None, ALU.subtract).then_inc(s["fast_wt"], 1)
            dve.wait_ge(s["fast_wt"], 1)
            dve.wait_ge(s["root_done"], 2)
            nc.vector.reciprocal(dinv[:], root[:]).then_inc(s["norm_done"], 1)
            dve.wait_ge(s["norm_done"], 1)

            def step(k, h, u):
                base = links_before(k) + (h * 2 + u) * LINKS[k]
                n = h * 2 + u
                g = n
                made = [0]

                def link(ins):
                    made[0] += 1
                    ins.then_inc(s["chain"], 1)
                    dve.wait_ge(s["chain"], base + made[0])

                dve.wait_ge(loaded[u], loads_before(k) + 16 * n_loads(k) * (h + 1))
                zt, xct = b3(z[:, u, :]), b3(xc[:, u, :])
                x_in = b3(xt[:, u, :])
                if k in CONVS:
                    dve.wait_ge(s["y_ready"], before(k, CONVS) + n + 1 + 2)
                    ins = nc.vector.tensor_tensor(zt, b3(pB[u][:]), col(dinv, g), ALU.mult)
                    link(ins)
                    ins = nc.vector.tensor_tensor(zt, zt, vec(BIAS[k]), ALU.add)
                    link(ins)
                ln_in = None
                def out_free():
                    earlier(dve, stored_t[u], tstores_before(k) + 16 * n_tstores(k) * h)

                def x_free():
                    earlier(dve, stored_x[u], xstores_before(k) + 16 * h)

                if k in (CONV_A, CONV_B):
                    out_free()
                    nc.vector.scalar_tensor_tensor(b3(tnew[:, u, :]), zt, 0.0, col(dinv, g), ALU.max, ALU.mult).then_inc(s["t_ready"], 1)
                if k == CONV_GATE:
                    h0 = cat[:, u, :, 1, :]
                    hh = cat[:, u, :, 0, :]
                    link(nc.vector.tensor_tensor(h0, b3(t0[:, u, :]), col(root, g), ALU.mult))
                    nc.vector.scalar_tensor_tensor(hh, zt, 0.0, h0, ALU.max, ALU.add).then_inc(s["cat_ready"], 1)
                    dve.wait_ge(s["g_ready"], n + 1 + 1)
                    nc.vector.tensor_tensor(b3(gate[:, u, :]), b3(pD[u][:]), vec(B_GATE), ALU.add).then_inc(s["gate_ready"], 1)
                    dve.wait_ge(s["gate_ready"], n * 2 + 2)
                    link(nc.vector.tensor_tensor(zt, hh, b3(gate[:, u, :]), ALU.mult))
                    x_free()
                    ins = nc.vector.tensor_tensor(b3(xnew[:, u, :]), zt, x_in, ALU.add)
                if k == CONV_RES:
                    x_free()
                    ins = nc.vector.scalar_tensor_tensor(b3(xnew[:, u, :]), zt, 0.0, x_in, ALU.max, ALU.add)
                if k == ATT_RES:
                    pin = pay_in[:, u, :].rearrange("p (s c) -> p s c", s=GB)
                    link(nc.vector.tensor_scalar(rden[:, u, :, :], pin[:, :, D:PAY], 1e-8, None, ALU.add))
                    link(nc.vector.reciprocal(rden[:, u, :, :], rden[:, u, :, :]))
                    for hd in range(HEADS):
                        ins = nc.vector.tensor_tensor(zt[:, :, hd * DH:(hd + 1) * DH], pin[:, :, hd * DH:(hd + 1) * DH],
                                                      rden[:, u, :, hd:hd + 1].to_broadcast([P, GB, DH]), ALU.mult)
                    link(ins)
                    x_free()
                    ins = nc.vector.tensor_tensor(b3(xnew[:, u, :]), zt, x_in, ALU.add)
                if k in WRITES_X:
                    ins.then_inc(s["x_ready"], 1)
                    dve.wait_ge(s["x_ready"], before(k, WRITES_X) + n + 1)
                ln = {FIRST: x_in, LAST: zt, ROUND_A: zt, ROUND_B: zt, ROUND_C: zt}.get(k, b3(xnew[:, u, :]))
                if k in LN_RELU or k in ROUNDS:
                    c = before(k, LN_RELU + ROUNDS) + n
                    m, v, sd, r = mean[:, u, :], var[:, u, :], std[:, u, :], rstd[:, u, :]
                    link(nc.vector.tensor_reduce(m, ln, AX_X, ALU.add))
                    link(nc.vector.tensor_scalar(m, m, 1.0 / D, None, ALU.mult))
                    nc.vector.tensor_tensor(xct, ln, spread(m), ALU.subtract).then_inc(s["sq_ready"], 1)
                    dve.wait_ge(s["std_ready"], 2 * c + 1)
                    link(nc.vector.tensor_reduce(v, b3(sq[:, u, :]), AX_X, ALU.add))
                    nc.vector.tensor_scalar(v, v, 1.0 / D, 1e-5, ALU.mult, ALU.add).then_inc(s["sq_ready"], 1)
                    dve.wait_ge(s["std_ready"], 2 * c + 2)
                    link(nc.vector.reciprocal(r, sd))
                if k in LN_RELU:
                    if k != CONV_RES:
                        link(nc.vector.tensor_tensor(r, r, dinv[:, bass.ds(g * GB, GB)], ALU.mult))
                    out_free()
                    nc.vector.scalar_tensor_tensor(b3(tnew[:, u, :]), xct, 0.0, spread(r), ALU.max, ALU.mult).then_inc(s["t_ready"], 1)
                if k in ROUNDS:
                    link(nc.vector.tensor_tensor(xct, xct, spread(r), ALU.mult))
                    link(nc.vector.tensor_tensor(xct, xct, vec(B_GAMMA), ALU.mult))
                    link(nc.vector.tensor_tensor(xct, xct, vec(B_BETA), ALU.add))
                    out_free()
                    last = col(dinv, g) if k != LAST else x_in
                    nc.vector.tensor_tensor(b3(tnew[:, u, :]), xct, last, ALU.mult if k != LAST else ALU.add).then_inc(s["t_ready"], 1)
                while made[0] < LINKS[k]:
                    made[0] += 1
                    dve.sem_inc(s["chain"], 1)
                assert made[0] == LINKS[k], (k, made[0])
                dve.wait_ge(s["t_ready"], NG * k + n + 3)

            def edge_index(k, a, t, q, late=False):
                kind = "src" if k == CONV_RES else "dst"
                n = U * t + q
                c = bass.ds(n, 1)
                base = (a * NT + n) * 3
                dve.wait_ge(krow_in[q], SCATTERS * a + 16 * (t + 1))
                dve.wait_ge(s["sum_done"], NT * a + n + 1)
                nc.vector.tensor_scalar(eq[:, q, :], krow[:, q, :], keyf[kind][:, c], None, ALU.is_equal).then_inc(s["echain"], 1)
                dve.wait_ge(s["echain"], base + 1)
                nc.vector.tensor_tensor_reduce(junk[:], eq[:, q, :], lower[:], 1.0, 0.0, ALU.mult, ALU.add, cnt[:, q:q + 1]).then_inc(s["echain"], 1)
                dve.wait_ge(s["echain"], base + 2)
                nc.vector.tensor_scalar(pos[:, q:q + 1], cnt[:, q:q + 1], 0.0, rowm[kind][:, c], ALU.is_equal, ALU.mult).then_inc(s["echain"], 1)
                dve.wait_ge(s["echain"], base + 3)
                if not late:
                    target(a, t, q)
                if k == CONV_RES:
                    nc.vector.tensor_copy(idx_g[:, q, 1:2], row["dst"][:, c])
                nc.vector.tensor_copy(idx_g[:, q, 0:1], row["src"][:, c]).then_inc(s["idx_ready"], 1)

            def target(a, t, q):
                slot_scattered(dve, q, t, a)
                nc.vector.tensor_scalar(idx_s[:, q:q + 1], pos[:, q:q + 1], spare[:, 0:1], None, ALU.add)

            def edge_weights(t, q):
                n = U * t + q
                dve.wait_ge(s["q_ready"], n + 1)
                nc.vector.tensor_tensor(qk[:, q, :], qs[:, q, :], pC[q % 2][:, D:2 * D], ALU.mult).then_inc(s["achain"], 1)
                dve.wait_ge(s["achain"], 2 * n + 1)
                nc.vector.tensor_reduce(att[:, q, :], qk[:, q, :].rearrange("p (h d) -> p h d", h=HEADS), AX_X, ALU.add).then_inc(s["achain"], 1)
                dve.wait_ge(s["achain"], 2 * n + 2)
                nc.vector.tensor_scalar(attc[:, q, :], att[:, q, :], -10.0, 10.0, ALU.max, ALU.min).then_inc(s["att_ready"], 1)
                dve.wait_ge(s["exp_ready"], n + 1)
                nc.vector.tensor_tensor(pay[:, q, 0:D].rearrange("p (h d) -> p h d", h=HEADS),
                                        pC[q % 2][:, 2 * D:3 * D].rearrange("p (h d) -> p h d", h=HEADS),
                                        pay[:, q, D:PAY].unsqueeze(2).to_broadcast([P, HEADS, DH]), ALU.mult).then_inc(s["pay_ready"], 1)

            def edge(k, a, t):
                for q in range(U):
                    edge_index(k, a, t, q)
                    if k == CONV_RES:
                        edge_weights(t, q)

            def fast_edge(tile):
                live, t, q = tile(IDX_LEAD)
                if live:
                    edge_index(CONV_RES, 0, t, q, late=True)
                live, t, q = tile(0)
                if live:
                    target(0, t, q)
                    edge_weights(t, q)

            dve.sem_inc(s["idx_ready"], U)
            dve.sem_inc(s["t_ready"], 2)
            dve.wait_ge(s["mask"], 4)
            def linker(name, k, m, per):
                made = [0]
                start = CHAINS[name](k) + m * per

                def link(ins):
                    made[0] += 1
                    assert made[0] <= per
                    ins.then_inc(s[name], 1)
                    dve.wait_ge(s[name], start + made[0])
                return link

            Z_LINKS = {CONV_A: 2, CONV_B: 2, CONV_GATE: 2, CONV_RES: 2, ATT_RES: 3, ROUND_A: 1, ROUND_B: 1, ROUND_C: 1, LAST: 1}
            X_LINKS = {k: 3 if k == CONV_GATE else 2 for k in LN_RELU}
            N_LINKS = {k: 2 for k in LN_RELU} | {CONV_RES: 1} | {k: 3 for k in ROUNDS} | {LAST: 4}
            CHAINS = {"chz": lambda k: NG * sum(Z_LINKS.get(j, 0) for j in range(k)),
                      "chx": lambda k: NG * sum(X_LINKS.get(j, 0) for j in range(k)),
                      "chr": lambda k: NG * sum(1 for j in range(k) if j in LN_RELU + ROUNDS),
                      "chn": lambda k: NG * sum(N_LINKS.get(j, 0) for j in range(k))}

            def fast(k, n, u, it):
                live, m, q, turn = at(n, u, it, x_part(k) + 1)
                if live and k in LN_RELU + ROUNDS:
                    link = linker("chr", k, m, 1)
                    after(dve, "f_sq", k, m)
                    after(dve, "f_std", k, m, S4)
                    link(nc.vector.tensor_reduce(var[:, q, :], b3(sq[:, q % 2, :]), AX_X, ALU.add))
                    nc.vector.tensor_scalar(var[:, q, :], var[:, q, :], 1.0 / D, 1e-5, ALU.mult, ALU.add).then_inc(s["f_var"], 1)
                live, m, q, turn = at(n, u, it, 0)
                if live and k in CONVS:
                    after(dve, "f_agg", k, m)
                    after(dve, "f_trans", k, m, 2)
                    landed(dve, own_in, OWN_LOADS, k, m, q, turn)
                    nc.vector.tensor_tensor(asum[:, q % 2, :], pC[q % 2][:], own[:, q, :], ALU.add).then_inc(s["f_add"], 1)
                live, m, q, turn = at(n, u, it, 2)
                if live and k in CONVS:
                    link = linker("chz", k, m, Z_LINKS[k])
                    zt = b3(z[:, q, :])
                    after(dve, "f_mm", k, m)
                    if k in ROUNDS:
                        after(dve, "f_sq", k, m, S4)
                    link(nc.vector.tensor_tensor(zt, b3(y_bank(k, q)[:]), col(dinv, m), ALU.mult))
                    if k in ROUNDS:
                        nc.vector.tensor_tensor(zt, zt, bcent[:].unsqueeze(1).to_broadcast([P, GB, D]), ALU.add).then_inc(s["f_z"], 1)
                    else:
                        link(nc.vector.tensor_tensor(zt, zt, vec(BIAS[k]), ALU.add))
                    if k in (CONV_A, CONV_B):
                        landed(dve, st_t, T_STORES, k, m, q, turn, lag=S4)
                        nc.vector.scalar_tensor_tensor(b3(tnew[:, q, :]), zt, 0.0, col(dinv, m), ALU.max, ALU.mult).then_inc(s["f_out"], 1)
                    if k == CONV_GATE:
                        after(dve, "f_gtr", k, m, S4)
                        after(dve, "f_h0", k, m)
                        nc.vector.scalar_tensor_tensor(hh[:, q, :], z[:, q, :], 0.0, h0[:, q, :], ALU.max, ALU.add).then_inc(s["f_cat"], 1)
                if k == CONV_GATE:
                    live, m, q, turn = at(n, u, it, 4)
                    if live:
                        after(dve, "f_gmm", k, m)
                        nc.vector.tensor_tensor(b3(gate[:, q % 2, :]), b3(pG[:]), vec(B_GATE), ALU.add).then_inc(s["f_gin"], 1)
                live, m, q, turn = at(n, u, it, x_part(k))
                if live and k in LN_RELU:
                    link = linker("chx", k, m, X_LINKS[k])
                    landed(dve, x_in, X_LOADS, k, m, q, turn, each=X_LOADS[k])
                    if k in WRITES_X:
                        landed(dve, st_x, X_STORES, k, m, q, turn, lag=S4)
                    if k == CONV_GATE:
                        after(dve, "f_gate", k, m)
                        link(nc.vector.tensor_tensor(hh[:, q, :], hh[:, q, :], gate[:, q % 2, :], ALU.mult))
                        nc.vector.tensor_tensor(xnew[:, q, :], hh[:, q, :], xt[:, q, :], ALU.add).then_inc(s["f_x"], 1)
                    if k == CONV_RES:
                        nc.vector.scalar_tensor_tensor(xnew[:, q, :], z[:, q, :], 0.0, xt[:, q, :], ALU.max, ALU.add).then_inc(s["f_x"], 1)
                    if k == ATT_RES:
                        lz = linker("chz", k, m, Z_LINKS[k])
                        after(dve, "f_pay", k, m)
                        pin = pay_in[:, q, :].rearrange("p (s c) -> p s c", s=GB)
                        lz(nc.vector.tensor_scalar(rden[:, q, :, :], pin[:, :, D:PAY], 1e-8, None, ALU.add))
                        lz(nc.vector.reciprocal(rden[:, q, :, :], rden[:, q, :, :]))
                        for hd in range(HEADS):
                            ins = nc.vector.tensor_tensor(b3(z[:, q, :])[:, :, hd * DH:(hd + 1) * DH], pin[:, :, hd * DH:(hd + 1) * DH],
                                                          rden[:, q, :, hd:hd + 1].to_broadcast([P, GB, DH]), ALU.mult)
                        lz(ins)
                        nc.vector.tensor_tensor(xnew[:, q, :], z[:, q, :], xt[:, q, :], ALU.add).then_inc(s["f_x"], 1)
                    if k in WRITES_X:
                        after(dve, "f_x", k, m)
                    xn = b3((xt if k == FIRST else xnew)[:, q, :])
                    link(nc.vector.tensor_reduce(mean[:, q, :], xn, AX_X, ALU.add))
                    link(nc.vector.tensor_scalar(mean[:, q, :], mean[:, q, :], 1.0 / D, None, ALU.mult))
                    after(dve, "f_out", k, m, S4)
                    nc.vector.tensor_tensor(b3(xc[:, q, :]), xn, spread(mean[:, q, :]), ALU.subtract).then_inc(s["f_sqin"], 1)
                live, m, q, turn = at(n, u, it, x_part(k) + 1)
                if live and k in LN_RELU + ROUNDS:
                    link = linker("chn", k, m, N_LINKS[k])
                    r = rstd[:, q, :]
                    after(dve, "f_std", k, m)
                    link(nc.vector.reciprocal(r, std[:, q, :]))
                    if k in LN_RELU:
                        if k != CONV_RES:
                            link(nc.vector.tensor_tensor(r, r, dinv[:, bass.ds(m * GB, GB)], ALU.mult))
                        landed(dve, st_t, T_STORES, k, m, q, turn, lag=S4)
                        nc.vector.scalar_tensor_tensor(b3(tnew[:, q, :]), b3(xc[:, q, :]), 0.0, spread(r), ALU.max, ALU.mult).then_inc(s["f_out"], 1)
                    else:
                        if k != LAST:
                            after(dve, "f_out", k, m, S4)
                        link(nc.vector.tensor_tensor(b3(xc[:, q, :]), b3(z[:, q, :]), spread(r), ALU.mult))
                        link(nc.vector.tensor_tensor(b3(xc[:, q, :]), b3(xc[:, q, :]), vec(B_GAMMA), ALU.mult))
                        ins = nc.vector.tensor_tensor(b3(xc[:, q, :]), b3(xc[:, q, :]), vec(B_BETA), ALU.add)
                        if k == LAST:
                            link(ins)
                            landed(dve, x_in, X_LOADS, k, m, q, turn)
                            landed(dve, st_t, T_STORES, k, m, q, turn, lag=S4)
                            nc.vector.tensor_tensor(tnew[:, q, :], xc[:, q, :], xt[:, q, :], ALU.add).then_inc(s["f_out"], 1)
                        else:
                            ins.then_inc(s["f_pre"], 1)

            dve.wait_ge(s["flag_ready"], 1)
            even = dve.value_load(flag[0:1, 0:1], min_val=0, max_val=1)
            with dve.If(even == 1):
                for k in range(10):
                    steps(dve, k, fast)
                    if k == CONV_RES:
                        edge_steps(dve, fast_edge)
            with dve.Else():
              for k in range(10):
                def both(h):
                    for u in range(2):
                        step(k, h, u)
                over(dve, NG // 2, k in (FIRST, CONV_GATE), both)
                if k != LAST:
                    over(dve, NIT, k == FIRST, lambda t: edge(k, k, t))

        @block.tensor
        def _(pe):
            pe.sem_inc(s["trans_done"], 2)
            pe.sem_inc(s["y_ready"], 2)
            pe.sem_inc(s["g_ready"], 1)
            pe.sem_inc(s["sum_done"], U)
            pe.sem_inc(s["qkv_done"], U)
            pe.sem_inc(s["oh_used"], U)

            def count(t, start=False, stop=False):
                for q in range(U):
                    n = t * U + q
                    pe.wait_ge(s["oh_ready"], 2 * n + 2)
                    for hf in range(2):
                        ins = nc.tensor.matmul(pA[hf][:, 0:NBLK // 2], onehot_lo[:, q, :], onehot_hi[:, q, hf * NBLK // 2:(hf + 1) * NBLK // 2],
                                               start=start and q == 0, stop=stop and q == U - 1, skip_group_check=True)
                    ins.then_inc(s["oh_used"], 1)
                if stop:
                    pe.wait_ge(s["oh_used"], NT + U)
                    pe.sem_inc(s["deg_done"], 1)
            count(0, start=True)
            with pe.Fori(1, NIT - 1) as t:
                count(t)
            count(NIT - 1, stop=True)
            pe.wait_ge(s["mask"], 4)
            pe.wait_ge(s["const_in"], 16 * 17)

            def step(k, h, u):
                n = h * 2 + u
                if k not in CONVS:
                    return
                c = before(k, CONVS)
                w = wround[:] if k in ROUNDS else wsb[:, BIAS[k], :]
                pe.wait_ge(loaded[u], loads_before(k) + 16 * n_loads(k) * (h + 1))
                for j in range(HB):
                    ins = nc.tensor.transpose(pA[u][:, j * P:(j + 1) * P], own[:, u, j * P:(j + 1) * P], ident[:])
                ins.then_inc(s["trans_done"], 1)
                pe.wait_ge(s["aT_ready"], c + n + 1)
                pe.wait_ge(s["t_ready"], NG * k + n + 1)
                for j in range(HB):
                    ins = nc.tensor.matmul(pB[u][:, j * P:(j + 1) * P], aT[:, u, j * P:(j + 1) * P], w, start=True, stop=True)
                ins.then_inc(s["y_ready"], 1)
                if k == CONV_GATE:
                    pe.wait_ge(s["cat_ready"], n + 1)
                    for j in range(GB):
                        ins = nc.tensor.transpose(pC[j // HB][:, (j % HB) * P:(j % HB + 1) * P], cat[:, u, j, :, :].rearrange("p a d -> p (a d)"), ident[:])
                    ins.then_inc(s["catT_psum"], 1)
                    pe.wait_ge(s["catT_ready"], n * 2 + 2)
                    for j in range(GB):
                        ins = nc.tensor.matmul(pD[u][:, j * D:(j + 1) * D], catT[:, u, j, :], wgate[:], start=True, stop=True)
                    ins.then_inc(s["g_ready"], 1)

            def edge_products(a, t, q):
                m = U * t + q
                nc.tensor.transpose(pB[q % 2][:, 0:P], msg[:, q, :], ident[:]).then_inc(s["hT_done"], 1)
                pe.wait_ge(s["hT_ready"], m + 1)
                nc.tensor.matmul(pC[q % 2][:, 0:3 * D], msgT[:, q, :], wqkv[:], start=True, stop=True).then_inc(s["qkv_done"], 1)

            def edge_sum(k, a, t, q):
                m = U * t + q
                if k == CONV_RES:
                    pe.wait_ge(s["pay_ready"], m + 1)
                w = PAY if k == CONV_RES else D
                pe.wait_ge(s["sum_used"], NT * a + m + U - 1)
                nc.tensor.matmul(pA[q % 2][:, 0:w], eq[:, q, :], pay[:, q, :] if k == CONV_RES else msg[:, q, 0:D],
                                 start=True, stop=True).then_inc(s["sum_done"], 1)

            def edge(k, a, t):
                for q in range(U):
                    n = NT * a + U * t + q
                    c = 1 if a > CONV_RES else 0
                    pe.wait_ge(gathered[q], 16 * NIT * (a + c) + (t + 1) * (32 if k == CONV_RES else 16))
                    pe.wait_ge(s["idx_ready"], n + 1 + U)
                    if k == CONV_RES:
                        edge_products(a, t, q)
                    edge_sum(k, a, t, q)

            def fast_edge(tile):
                live, t, q = tile(1)
                if live:
                    pe.wait_ge(gathered[q], 32 * (t + 1))
                    edge_products(0, t, q)
                live, t, q = tile(0)
                if live:
                    edge_sum(CONV_RES, 0, t, q)

            pe.wait_ge(s["c1"], 1)
            for h in range(2):
                ins = nc.tensor.matmul(pB[h][:, 0:NBLK // 2], ones[:], size[:, h * NBLK // 2:(h + 1) * NBLK // 2], start=True, stop=True)
            ins.then_inc(s["c2"], 1)
            for k in range(2):
                for c in range(4):
                    pe.wait_ge(s["oht_ready"], 4 * k + c + 1)
                    for h in range(2):
                        ins = nc.tensor.matmul((pC, pD)[k][h][:, 0:NBLK // 2], rowlayf[:, c * P:(c + 1) * P],
                                               onehot_tile[c][0:TP, h * NBLK // 2:(h + 1) * NBLK // 2], start=c == 0, stop=c == 3)
                ins.then_inc(s["oht_used"], 1)
            pe.wait_ge(s["c1"], 2)
            pe.wait_ge(s["root_done"], 2)
            nc.tensor.matmul(pA[0][:, 0:2], ones[:], checks[:, 0:2], start=True, stop=True).then_inc(s["c2"], 1)

            spots = [pe.alloc_register(f"spot{j}") for j in range(2 * GB)]
            Y_USED = {CONV_A: "f_out", CONV_B: "f_out", CONV_GATE: "f_cat", CONV_RES: "f_x"} | {k: "f_z" for k in ROUNDS}
            columns = ring[:].rearrange("p t c -> p (t c)")

            def fast(k, n, u, it):
                live, m, q, turn = at(n, u, it, 0)
                if live and k in CONVS:
                    pe.load(spots, place[0:1, bass.ds(m, 1), :])
                    spot = [pe.snap(r, min_val=0, max_val=(RB * U - 1) * D) for r in spots]
                    if not isinstance(m, int):
                        pe.wait_ge(raw_in[(u + AHEAD) % S4], 16 * U * (it + (u + AHEAD) // S4 + 1 + raw_before(k, (u + AHEAD) % S4)))
                    else:
                        for b in range(0 if m == 0 else m + AHEAD, min(m + AHEAD + 1, NIT)):
                            pe.wait_ge(raw_in[b % S4], 16 * U * (b // S4 + 1 + raw_before(k, b % S4)))
                    after(pe, "f_sel", k, m)
                    after(pe, "f_add", k, m, 2)
                    for j in range(GB):
                        width = P if j < GB - 1 else D
                        for e in range(2):
                            ins = nc.tensor.matmul(pC[q % 2][:, j * D:j * D + width], sel32[:, q % 2, 2 * j + e, :],
                                                   columns[:, bass.ds(spot[2 * j + e], width)],
                                                   start=e == 0, stop=e == 1, skip_group_check=True)
                    ins.then_inc(s["f_agg"], 1)
                live, m, q, turn = at(n, u, it, 1)
                if live and k in CONVS:
                    after(pe, "f_add", k, m)
                    after(pe, "f_evac", k, m, 2)
                    for j in range(HB):
                        ins = nc.tensor.transpose(pA[q % 2][:, j * P:(j + 1) * P], asum[:, q % 2, j * P:(j + 1) * P], ident[:])
                    ins.then_inc(s["f_trans"], 1)
                live, m, q, turn = at(n, u, it, 2)
                if live and k in CONVS:
                    after(pe, "f_evac", k, m)
                    after(pe, Y_USED[k], k, m, 1 if k == CONV_GATE else 2)
                    y = y_bank(k, q)
                    w = wcent[:] if k in ROUNDS else wsb[:, BIAS[k], :]
                    for j in range(HB):
                        ins = nc.tensor.matmul(y[:, j * P:(j + 1) * P], aT[:, q % 2, j * P:(j + 1) * P], w, start=True, stop=True)
                    ins.then_inc(s["f_mm"], 1)
                if k == CONV_GATE:
                    live, m, q, turn = at(n, u, it, 3)
                    if live:
                        after(pe, "f_cat", k, m)
                        after(pe, "f_gev", k, m, 1)
                        for j in range(HB):
                            nc.tensor.transpose(pD[0][:, j * P:(j + 1) * P], hh[:, q, j * P:(j + 1) * P], ident[:])
                        for j in range(HB):
                            ins = nc.tensor.transpose(pD[1][:, j * P:(j + 1) * P], h0[:, q, j * P:(j + 1) * P], ident[:])
                        ins.then_inc(s["f_gtr"], 1)
                    live, m, q, turn = at(n, u, it, 4)
                    if live:
                        after(pe, "f_gev", k, m)
                        after(pe, "f_gin", k, m, 1)
                        for j in range(HB):
                            for part in range(2):
                                ins = nc.tensor.matmul(pG[:, j * P:(j + 1) * P], hhT[:, part * HB + j, :], wgp[:, part, :],
                                                       start=part == 0, stop=part == 1)
                        ins.then_inc(s["f_gmm"], 1)

            pe.wait_ge(s["flag_ready"], 1)
            even = pe.value_load(flag[0:1, 0:1], min_val=0, max_val=1)
            pe.wait_ge(s["fast_wt"], 1)
            pe.wait_ge(s["row_in"], 16 * 5)
            with pe.If(even == 1):
                for k in range(10):
                    if k in CONVS:
                        steps(pe, k, fast)
                    if k == CONV_RES:
                        edge_steps(pe, fast_edge)
            with pe.Else():
              for k in range(10):
                if k in CONVS:
                    with pe.Fori(0, NG // 2) as h:
                        for u in range(2):
                            step(k, h, u)
                if k != LAST:
                    with pe.Fori(0, NIT) as t:
                        edge(k, k, t)


def kernel(**inputs):
    import numpy as np
    import concourse.bacc as _bacc
    from concourse import mybir as _mybir
    from concourse.bass_utils import run_bass_kernel_spmd as _run

    a = {k: np.asarray(v) for k, v in inputs.items()}
    x = np.zeros((NROW, D), a["x"].dtype)
    x[:N_NODES] = a["x"]
    x = np.ascontiguousarray(x.reshape(NG, GB, P, D).transpose(0, 2, 1, 3)).reshape(NROW, D)
    edges = {}
    for k in ("src", "dst"):
        e = np.full((NT * P,), PAD_KEY, a[k].dtype)
        e[:N_EDGES] = a[k]
        edges[k + "_row"] = e.reshape(NT, P)
        edges[k] = np.ascontiguousarray(e.reshape(NT, P).T)
    wt = np.concatenate([a["L0_gnn_W1"].T, a["L0_gnn_W2"].T, a["L1_gnn_W1"], a["L1_gnn_W2"], a["L3_gnn_W"],
                         a["L0_gnn_Wg"].T, a["L2_gnn_Wq"], a["L2_gnn_Wk"], a["L2_gnn_Wv"]], axis=0)
    bias = np.stack([a["L0_gnn_b1"], a["L0_gnn_b2"], a["L1_gnn_b1"], a["L1_gnn_b2"], a["L3_gnn_b"], a["L0_gnn_bg"],
                     a["L3_gnn_gamma"], a["L3_gnn_beta"]])
    arrays = {"x": x, "src": edges["src"], "dst": edges["dst"], "dst_row": edges["dst_row"], "src_row": edges["src_row"],
              "wt": np.ascontiguousarray(wt), "bias": np.ascontiguousarray(bias)}
    nc = _bacc.Bacc("TRN2", target_bir_lowering=False, num_devices=1)
    args = [nc.dram_tensor(f"in_{n}", v.shape, _mybir.dt.from_np(v.dtype), kind="ExternalInput").ap() for n, v in arrays.items()]
    out = nc.dram_tensor("out_dram", (NROW, D), F32, kind="ExternalOutput").ap()
    gnn_kernel(nc, *args, out)
    r = _run(nc, [{f"in_{n}": v for n, v in arrays.items()}], core_ids=[0])
    got = np.asarray(r.results[0]["out_dram"]).reshape(NG, P, GB, D).transpose(0, 2, 1, 3)
    return np.ascontiguousarray(got).reshape(NROW, D)[:N_NODES]
```
